# Optimizing a Trainium2 kernel written in Bass

```python
import numpy as np
import jax
import jax.numpy as jnp

def _softmax(x, axis=-1):
    return jax.nn.softmax(x, axis=axis)

def _gelu(x):
    return jax.nn.gelu(x, approximate=True)

def _silu(x):
    return jax.nn.silu(x)

def _sigmoid(x):
    return jax.nn.sigmoid(x)

def _layernorm(x, axis=-1, eps=1e-05):
    m = jnp.mean(x, axis=axis, keepdims=True)
    v = jnp.var(x, axis=axis, keepdims=True)
    return (x - m) / jnp.sqrt(v + eps)

def _scatter_add(tgt, idx, src, axis=0):
    return tgt.at[idx].add(src)

def _segment_sum(src, seg, n):
    return jax.ops.segment_sum(src, seg, n)
kernel_name = 'mk_sandwich_d2_jaxref_r8_cc9c5e'

def setup_inputs(seed: int=0):
    np.random.seed(seed)
    _w = jnp.asarray

    def _L0_attn_setup():
        import jax, jax.numpy as jnp
        import numpy as np
        B, S, D, H = (2, 256, 128, 16)
        HD = D // H
        FF = 512
        NUM_ITERS = 8
        DT = 0.1
        LN_EPS = 1e-05

        def _ln(x, g, b):
            m = jnp.mean(x, axis=-1, keepdims=True)
            v = jnp.var(x, axis=-1, keepdims=True)
            return (x - m) * jax.lax.rsqrt(v + LN_EPS) * g + b

        def _forward(x, qkv_w, qkv_b, out_w, out_b, g_attn, b_attn, g1, b1, g2, b2, w_ctx, w_x, b_inl, ff_w1, ff_b1, ff_w2, ff_b2):
            b, s, d = x.shape
            xn = _ln(x, g_attn, b_attn)
            qkv = (xn @ qkv_w + qkv_b).reshape(b, s, 3, H, HD)
            qkv = jnp.transpose(qkv, (2, 0, 3, 1, 4))
            q, k, v = (qkv[0], qkv[1], qkv[2])
            scores = jnp.einsum('bhqd,bhkd->bhqk', q, k) / np.sqrt(HD).astype(np.float32)
            causal = jnp.triu(jnp.ones((s, s), dtype=bool), 1)
            scores = jnp.where(causal[None, None], -jnp.inf, scores)
            attn_w = jax.nn.softmax(scores, axis=-1)
            attn = jnp.einsum('bhqk,bhkd->bhqd', attn_w, v)
            attn = jnp.transpose(attn, (0, 2, 1, 3)).reshape(b, s, d)
            attn = attn @ out_w + out_b
            x = x + attn
            ctx = attn.reshape(b * s, d)
            xs = _ln(x, g1, b1).reshape(b * s, d)
            vs = jnp.zeros_like(xs)

            def step(carry, _):
                xs, vs = carry
                u = jnp.tanh(ctx @ w_ctx + xs @ w_x + b_inl)
                vn = vs + DT * (u - xs - vs)
                xn_ = xs + DT * vn
                return ((xn_, vn), None)
            (xs, vs), _ = jax.lax.scan(step, (xs, vs), None, length=NUM_ITERS)
            x = x + xs.reshape(b, s, d)
            h = _ln(x, g2, b2)
            h = jax.nn.gelu(h @ ff_w1 + ff_b1, approximate=False)
            x = x + (h @ ff_w2 + ff_b2)
            return x
        key = jax.random.key(seed)
        ks = jax.random.split(key, 16)

        def xav(k, shape):
            lim = np.sqrt(6.0 / (shape[0] + shape[1]))
            return jax.random.uniform(k, shape, minval=-lim, maxval=lim, dtype=jnp.float32)
        return {'x': jax.random.normal(ks[0], (B, S, D), dtype=jnp.float32), 'qkv_w': xav(ks[1], (D, 3 * D)), 'qkv_b': jnp.zeros((3 * D,), jnp.float32), 'out_w': xav(ks[2], (D, D)), 'out_b': jnp.zeros((D,), jnp.float32), 'g_attn': jnp.ones((D,), jnp.float32), 'b_attn': jnp.zeros((D,), jnp.float32), 'g1': jnp.ones((D,), jnp.float32), 'b1': jnp.zeros((D,), jnp.float32), 'g2': jnp.ones((D,), jnp.float32), 'b2': jnp.zeros((D,), jnp.float32), 'w_ctx': xav(ks[3], (D, D)), 'w_x': xav(ks[4], (D, D)), 'b_inl': jnp.zeros((D,), jnp.float32), 'ff_w1': xav(ks[5], (D, FF)), 'ff_b1': jnp.zeros((FF,), jnp.float32), 'ff_w2': xav(ks[6], (FF, D)), 'ff_b2': jnp.zeros((D,), jnp.float32)}
    _L0_attn_in = _L0_attn_setup()

    def _L0_ffn_setup():
        import jax, jax.numpy as jnp
        import numpy as np
        B, T, D, H, E = (4, 256, 128, 512, 8)
        key = jax.random.key(seed)
        ks = jax.random.split(key, 7)
        x = jax.random.normal(ks[0], (B, T, D), dtype=jnp.float32)
        Wg = jax.random.normal(ks[1], (D, E), dtype=jnp.float32) / np.sqrt(D)
        bg = jax.random.normal(ks[2], (E,), dtype=jnp.float32) * 0.01
        W1 = jax.random.normal(ks[3], (E, D, H), dtype=jnp.float32) / np.sqrt(D)
        b1 = jax.random.normal(ks[4], (E, H), dtype=jnp.float32) * 0.01
        W2 = jax.random.normal(ks[5], (E, H, D), dtype=jnp.float32) / np.sqrt(H)
        b2 = jax.random.normal(ks[6], (E, D), dtype=jnp.float32) * 0.01
        return {'x': x, 'Wg': Wg, 'bg': bg, 'W1': W1, 'b1': b1, 'W2': W2, 'b2': b2}
    _L0_ffn_in = _L0_ffn_setup()

    def _L1_attn_setup():
        import jax, jax.numpy as jnp
        import numpy as np
        D_MODEL = 128
        D_INNER = 256
        D_STATE = 16
        D_CONV = 4
        DT_RANK = 64
        EPS = 1e-05

        def _causal_depthwise_conv(x, conv_w, conv_b):
            B, L, C = x.shape
            xt = jnp.transpose(x, (0, 2, 1))
            xt = jnp.pad(xt, ((0, 0), (0, 0), (D_CONV - 1, 0)))
            k = conv_w[:, None, :]
            y = jax.lax.conv_general_dilated(xt, k, window_strides=(1,), padding='VALID', dimension_numbers=('NCH', 'OIH', 'NCH'), feature_group_count=C)
            y = y + conv_b[None, :, None]
            return jnp.transpose(y, (0, 2, 1))

        def _selective_scan(u, delta, A, Bm, Cm, D_param):
            dA = jnp.exp(delta[..., None] * A[None, None])
            dBu = delta[..., None] * Bm[:, :, None, :] * u[..., None]
            h0 = jnp.zeros((u.shape[0], u.shape[2], A.shape[1]), u.dtype)

            def step(h, inp):
                dA_t, dBu_t, c_t = inp
                h = dA_t * h + dBu_t
                y = jnp.einsum('bdn,bn->bd', h, c_t)
                return (h, y)
            xs = (jnp.moveaxis(dA, 1, 0), jnp.moveaxis(dBu, 1, 0), jnp.moveaxis(Cm, 1, 0))
            _, ys = jax.lax.scan(step, h0, xs)
            y = jnp.moveaxis(ys, 0, 1)
            return y + u * D_param[None, None]
        key = jax.random.key(seed)
        ks = jax.random.split(key, 10)
        B, L = (2, 128)
        w = lambda k, shape, s: jax.random.normal(k, shape, jnp.float32) * s
        A = jnp.tile(jnp.arange(1, D_STATE + 1, dtype=jnp.float32), (D_INNER, 1))
        return {'hidden_states': jax.random.normal(ks[0], (B, L, D_MODEL), jnp.float32), 'norm_w': jnp.ones((D_MODEL,), jnp.float32), 'norm_b': jnp.zeros((D_MODEL,), jnp.float32), 'in_proj_w': w(ks[1], (D_MODEL, 2 * D_INNER), 0.02), 'conv_w': w(ks[2], (D_INNER, D_CONV), 0.2), 'conv_b': jnp.zeros((D_INNER,), jnp.float32), 'x_proj_w': w(ks[3], (D_INNER, DT_RANK + 2 * D_STATE), 0.02), 'dt_proj_w': w(ks[4], (DT_RANK, D_INNER), 0.1), 'dt_proj_b': w(ks[5], (D_INNER,), 0.1), 'A_log': jnp.log(A), 'D_param': jnp.ones((D_INNER,), jnp.float32), 'out_proj_w': w(ks[6], (D_INNER, D_MODEL), 0.02)}
    _L1_attn_in = _L1_attn_setup()

    def _L1_ffn_setup():
        import jax, jax.numpy as jnp
        import numpy as np
        B, N, C, H, REG = (1, 2309, 128, 16, 5)
        D = C // H
        key = jax.random.key(seed)
        k0, k1, k2, k3 = jax.random.split(key, 4)
        x = jax.random.normal(k0, (B, N, C), dtype=jnp.float32)
        g_info = jax.random.normal(k1, (12, 2, C), dtype=jnp.float32)
        W_qkv = jax.random.normal(k2, (C, 3 * C), dtype=jnp.float32) * 0.02
        W_proj = jax.random.normal(k3, (C, C), dtype=jnp.float32) * 0.02
        b_proj = jnp.zeros((C,), dtype=jnp.float32)
        return {'x': x, 'g_info': g_info, 'W_qkv': W_qkv, 'W_proj': W_proj, 'b_proj': b_proj}
    _L1_ffn_in = _L1_ffn_setup()
    _d = {'L0_attn_x': _L0_attn_in['x'], 'L0_attn_qkv_w': _L0_attn_in['qkv_w'], 'L0_attn_qkv_b': _L0_attn_in['qkv_b'], 'L0_attn_out_w': _L0_attn_in['out_w'], 'L0_attn_out_b': _L0_attn_in['out_b'], 'L0_attn_g_attn': _L0_attn_in['g_attn'], 'L0_attn_b_attn': _L0_attn_in['b_attn'], 'L0_attn_g1': _L0_attn_in['g1'], 'L0_attn_b1': _L0_attn_in['b1'], 'L0_attn_g2': _L0_attn_in['g2'], 'L0_attn_b2': _L0_attn_in['b2'], 'L0_attn_w_ctx': _L0_attn_in['w_ctx'], 'L0_attn_w_x': _L0_attn_in['w_x'], 'L0_attn_b_inl': _L0_attn_in['b_inl'], 'L0_attn_ff_w1': _L0_attn_in['ff_w1'], 'L0_attn_ff_b1': _L0_attn_in['ff_b1'], 'L0_attn_ff_w2': _L0_attn_in['ff_w2'], 'L0_attn_ff_b2': _L0_attn_in['ff_b2'], 'L0_ffn_Wg': _L0_ffn_in['Wg'], 'L0_ffn_bg': _L0_ffn_in['bg'], 'L0_ffn_W1': _L0_ffn_in['W1'], 'L0_ffn_b1': _L0_ffn_in['b1'], 'L0_ffn_W2': _L0_ffn_in['W2'], 'L0_ffn_b2': _L0_ffn_in['b2'], 'L1_attn_norm_w': _L1_attn_in['norm_w'], 'L1_attn_norm_b': _L1_attn_in['norm_b'], 'L1_attn_in_proj_w': _L1_attn_in['in_proj_w'], 'L1_attn_conv_w': _L1_attn_in['conv_w'], 'L1_attn_conv_b': _L1_attn_in['conv_b'], 'L1_attn_x_proj_w': _L1_attn_in['x_proj_w'], 'L1_attn_dt_proj_w': _L1_attn_in['dt_proj_w'], 'L1_attn_dt_proj_b': _L1_attn_in['dt_proj_b'], 'L1_attn_A_log': _L1_attn_in['A_log'], 'L1_attn_D_param': _L1_attn_in['D_param'], 'L1_attn_out_proj_w': _L1_attn_in['out_proj_w'], 'L1_ffn_g_info': _L1_ffn_in['g_info'], 'L1_ffn_W_qkv': _L1_ffn_in['W_qkv'], 'L1_ffn_W_proj': _L1_ffn_in['W_proj'], 'L1_ffn_b_proj': _L1_ffn_in['b_proj']}
    _x0 = _d['L0_attn_x']
    _d['L0_attn_x'] = jax.random.normal(jax.random.fold_in(jax.random.key(seed), 1), (4, 1024, 128), dtype=_x0.dtype)
    del _x0
    return _d

def reference(L0_attn_x, L0_attn_qkv_w, L0_attn_qkv_b, L0_attn_out_w, L0_attn_out_b, L0_attn_g_attn, L0_attn_b_attn, L0_attn_g1, L0_attn_b1, L0_attn_g2, L0_attn_b2, L0_attn_w_ctx, L0_attn_w_x, L0_attn_b_inl, L0_attn_ff_w1, L0_attn_ff_b1, L0_attn_ff_w2, L0_attn_ff_b2, L0_ffn_Wg, L0_ffn_bg, L0_ffn_W1, L0_ffn_b1, L0_ffn_W2, L0_ffn_b2, L1_attn_norm_w, L1_attn_norm_b, L1_attn_in_proj_w, L1_attn_conv_w, L1_attn_conv_b, L1_attn_x_proj_w, L1_attn_dt_proj_w, L1_attn_dt_proj_b, L1_attn_A_log, L1_attn_D_param, L1_attn_out_proj_w, L1_ffn_g_info, L1_ffn_W_qkv, L1_ffn_W_proj, L1_ffn_b_proj):

    def _L0_attn_ref(x, qkv_w, qkv_b, out_w, out_b, g_attn, b_attn, g1, b1, g2, b2, w_ctx, w_x, b_inl, ff_w1, ff_b1, ff_w2, ff_b2):
        import jax, jax.numpy as jnp
        import numpy as np
        B, S, D, H = (2, 256, 128, 16)
        HD = D // H
        FF = 512
        NUM_ITERS = 8
        DT = 0.1
        LN_EPS = 1e-05

        def _ln(x, g, b):
            m = jnp.mean(x, axis=-1, keepdims=True)
            v = jnp.var(x, axis=-1, keepdims=True)
            return (x - m) * jax.lax.rsqrt(v + LN_EPS) * g + b

        def _forward(x, qkv_w, qkv_b, out_w, out_b, g_attn, b_attn, g1, b1, g2, b2, w_ctx, w_x, b_inl, ff_w1, ff_b1, ff_w2, ff_b2):
            b, s, d = x.shape
            xn = _ln(x, g_attn, b_attn)
            qkv = (xn @ qkv_w + qkv_b).reshape(b, s, 3, H, HD)
            qkv = jnp.transpose(qkv, (2, 0, 3, 1, 4))
            q, k, v = (qkv[0], qkv[1], qkv[2])
            scores = jnp.einsum('bhqd,bhkd->bhqk', q, k) / np.sqrt(HD).astype(np.float32)
            causal = jnp.triu(jnp.ones((s, s), dtype=bool), 1)
            scores = jnp.where(causal[None, None], -jnp.inf, scores)
            attn_w = jax.nn.softmax(scores, axis=-1)
            attn = jnp.einsum('bhqk,bhkd->bhqd', attn_w, v)
            attn = jnp.transpose(attn, (0, 2, 1, 3)).reshape(b, s, d)
            attn = attn @ out_w + out_b
            x = x + attn
            ctx = attn.reshape(b * s, d)
            xs = _ln(x, g1, b1).reshape(b * s, d)
            vs = jnp.zeros_like(xs)

            def step(carry, _):
                xs, vs = carry
                u = jnp.tanh(ctx @ w_ctx + xs @ w_x + b_inl)
                vn = vs + DT * (u - xs - vs)
                xn_ = xs + DT * vn
                return ((xn_, vn), None)
            (xs, vs), _ = jax.lax.scan(step, (xs, vs), None, length=NUM_ITERS)
            x = x + xs.reshape(b, s, d)
            h = _ln(x, g2, b2)
            h = jax.nn.gelu(h @ ff_w1 + ff_b1, approximate=False)
            x = x + (h @ ff_w2 + ff_b2)
            return x
        return _forward(x, qkv_w, qkv_b, out_w, out_b, g_attn, b_attn, g1, b1, g2, b2, w_ctx, w_x, b_inl, ff_w1, ff_b1, ff_w2, ff_b2)

    def _L0_ffn_ref(x, Wg, bg, W1, b1, W2, b2):
        import jax, jax.numpy as jnp
        import numpy as np
        B, T, D, H, E = (4, 256, 128, 512, 8)
        gate_scores = x @ Wg + bg
        top1 = jnp.argmax(gate_scores, axis=-1)
        onehot = jax.nn.one_hot(top1, Wg.shape[-1], dtype=x.dtype)
        h = jax.nn.relu(jnp.einsum('btd,edh->beth', x, W1) + b1[None, :, None, :])
        y = jnp.einsum('beth,ehd->betd', h, W2) + b2[None, :, None, :]
        out = jnp.einsum('betd,bte->btd', y, onehot)
        return out

    def _L1_attn_ref(hidden_states, norm_w, norm_b, in_proj_w, conv_w, conv_b, x_proj_w, dt_proj_w, dt_proj_b, A_log, D_param, out_proj_w):
        import jax, jax.numpy as jnp
        import numpy as np
        D_MODEL = 128
        D_INNER = 256
        D_STATE = 16
        D_CONV = 4
        DT_RANK = 64
        EPS = 1e-05

        def _causal_depthwise_conv(x, conv_w, conv_b):
            B, L, C = x.shape
            xt = jnp.transpose(x, (0, 2, 1))
            xt = jnp.pad(xt, ((0, 0), (0, 0), (D_CONV - 1, 0)))
            k = conv_w[:, None, :]
            y = jax.lax.conv_general_dilated(xt, k, window_strides=(1,), padding='VALID', dimension_numbers=('NCH', 'OIH', 'NCH'), feature_group_count=C)
            y = y + conv_b[None, :, None]
            return jnp.transpose(y, (0, 2, 1))

        def _selective_scan(u, delta, A, Bm, Cm, D_param):
            dA = jnp.exp(delta[..., None] * A[None, None])
            dBu = delta[..., None] * Bm[:, :, None, :] * u[..., None]
            h0 = jnp.zeros((u.shape[0], u.shape[2], A.shape[1]), u.dtype)

            def step(h, inp):
                dA_t, dBu_t, c_t = inp
                h = dA_t * h + dBu_t
                y = jnp.einsum('bdn,bn->bd', h, c_t)
                return (h, y)
            xs = (jnp.moveaxis(dA, 1, 0), jnp.moveaxis(dBu, 1, 0), jnp.moveaxis(Cm, 1, 0))
            _, ys = jax.lax.scan(step, h0, xs)
            y = jnp.moveaxis(ys, 0, 1)
            return y + u * D_param[None, None]
        h = hidden_states
        mu = jnp.mean(h, axis=-1, keepdims=True)
        var = jnp.mean(jnp.square(h - mu), axis=-1, keepdims=True)
        h = (h - mu) * jax.lax.rsqrt(var + EPS) * norm_w + norm_b
        xz = h @ in_proj_w
        x, z = jnp.split(xz, 2, axis=-1)
        x = _causal_depthwise_conv(x, conv_w, conv_b)
        x = jax.nn.silu(x)
        A = -jnp.exp(A_log)
        xp = x @ x_proj_w
        dt_r = xp[..., :DT_RANK]
        Bm = xp[..., DT_RANK:DT_RANK + D_STATE]
        Cm = xp[..., DT_RANK + D_STATE:]
        delta = jax.nn.softplus(dt_r @ dt_proj_w + dt_proj_b)
        y = _selective_scan(x, delta, A, Bm, Cm, D_param)
        y = y * jax.nn.silu(z)
        return y @ out_proj_w

    def _L1_ffn_ref(x, g_info, W_qkv, W_proj, b_proj):
        import jax, jax.numpy as jnp
        import numpy as np
        B, N, C, H, REG = (1, 2309, 128, 16, 5)
        D = C // H
        Bx, Nx, Cx = x.shape
        scale = D ** (-0.5)
        qkv = (x @ W_qkv).reshape(Bx, Nx, 3, H, D)
        q, k, v = (qkv[:, :, 0], qkv[:, :, 1], qkv[:, :, 2])
        g_layer = g_info[0].reshape(-1, H, D)
        q_g = g_layer[0]
        q_pure = q[:, REG:]
        q_n = q_pure / jnp.linalg.norm(q_pure, axis=-1, keepdims=True)
        qg_n = q_g / jnp.linalg.norm(q_g, axis=-1, keepdims=True)
        sim = (qg_n[None, None] * q_n).sum(-1).mean(-1)
        sim = (sim - sim.min()) / (sim.max() - sim.min())
        pos = sim > 0.9
        logits = jnp.einsum('bqhd,bkhd->bhqk', q * scale, k)

        def masked_attn(tok_mask):
            key_mask = jnp.concatenate([jnp.ones((Bx, REG), bool), tok_mask], axis=1)
            l = jnp.where(key_mask[:, None, None, :], logits, -jnp.inf)
            a = jax.nn.softmax(l, axis=-1)
            return jnp.einsum('bhqk,bkhd->bqhd', a, v)
        x_pos = masked_attn(pos)
        x_neg = masked_attn(~pos)
        reg_out = (x_pos[:, :REG] + x_neg[:, :REG]) * 0.5
        tok_out = jnp.where(pos[:, :, None, None], x_pos[:, REG:], x_neg[:, REG:])
        out = jnp.concatenate([reg_out, tok_out], axis=1).reshape(Bx, Nx, Cx)
        return out @ W_proj + b_proj
    x = L0_attn_x
    x = x + _layernorm(_L0_attn_ref(_layernorm(x, axis=-1), L0_attn_qkv_w, L0_attn_qkv_b, L0_attn_out_w, L0_attn_out_b, L0_attn_g_attn, L0_attn_b_attn, L0_attn_g1, L0_attn_b1, L0_attn_g2, L0_attn_b2, L0_attn_w_ctx, L0_attn_w_x, L0_attn_b_inl, L0_attn_ff_w1, L0_attn_ff_b1, L0_attn_ff_w2, L0_attn_ff_b2), axis=-1)
    x = x + _layernorm(_L0_ffn_ref(_layernorm(x, axis=-1), L0_ffn_Wg, L0_ffn_bg, L0_ffn_W1, L0_ffn_b1, L0_ffn_W2, L0_ffn_b2), axis=-1)
    x = x + _layernorm(_L1_attn_ref(_layernorm(x, axis=-1), L1_attn_norm_w, L1_attn_norm_b, L1_attn_in_proj_w, L1_attn_conv_w, L1_attn_conv_b, L1_attn_x_proj_w, L1_attn_dt_proj_w, L1_attn_dt_proj_b, L1_attn_A_log, L1_attn_D_param, L1_attn_out_proj_w), axis=-1)
    x = x + _layernorm(_L1_ffn_ref(_layernorm(x, axis=-1), L1_ffn_g_info, L1_ffn_W_qkv, L1_ffn_W_proj, L1_ffn_b_proj), axis=-1)
    return x

_drawn_inputs = setup_inputs


def setup_inputs(seed=0):
    import zlib

    import numpy as np

    out = dict(_drawn_inputs(seed))
    spreads = {'L0_attn_qkv_b': (0.0, 0.1),
     'L0_attn_out_b': (0.0, 0.1),
     'L0_attn_g_attn': (1.0, 0.2),
     'L0_attn_b_attn': (0.0, 0.1),
     'L0_attn_g1': (1.0, 0.2),
     'L0_attn_b1': (0.0, 0.1),
     'L0_attn_g2': (1.0, 0.2),
     'L0_attn_b2': (0.0, 0.1),
     'L0_attn_b_inl': (0.0, 0.1),
     'L0_attn_ff_b1': (0.0, 0.1),
     'L0_attn_ff_b2': (0.0, 0.1),
     'L1_attn_norm_w': (1.0, 0.2),
     'L1_attn_norm_b': (0.0, 0.274),
     'L1_attn_conv_b': (0.0, 0.1),
     'L1_attn_D_param': (1.0, 0.2),
     'L1_ffn_b_proj': (0.0, 0.1)}
    factors = {'L0_ffn_b1': 8.0,
     'L0_ffn_b2': 8.0,
     'L1_attn_x_proj_w': 8.0,
     'L1_attn_dt_proj_w': 8.0,
     'L1_attn_dt_proj_b': 26.868,
     'L1_attn_A_log': 64.0,
     'L1_ffn_g_info': 64.0}
    for name, (base, spread) in spreads.items():
        noise = np.random.default_rng([zlib.crc32(name.encode()), seed]).standard_normal(out[name].shape)
        drawn = base * np.exp(spread * noise) if base else spread * noise
        out[name] = jnp.asarray(drawn.astype(out[name].dtype))
    for name, factor in factors.items():
        out[name] = (out[name] * factor).astype(out[name].dtype)
    return out
```

```python
from contextlib import ExitStack

import concourse.bass as bass
from concourse import mybir

F32 = mybir.dt.float32
BF16 = mybir.dt.bfloat16
ALU = mybir.AluOpType
ACT = mybir.ActivationFunctionType
AX = mybir.AxisListType

P = 128
B, S, D = 4, 1024, 128
CH = 512
H, HD = 16, 8
SCALE = float(HD) ** -0.5
GH = 4
GROUPS = B * H // GH
SLOTS_Q = (0, 0, 0, 1, 1, 2)
SLOTS_K = (0, 1, 2, 0, 1, 0)
NS = len(SLOTS_Q)
R_MASK = NS * HD
HR = R_MASK + 2
R_MAX = 2 * HR
R_END = R_MAX + 3
NEG = -1.0e30
QT = S // P
REG = 5
XQ = 32
FF = 512
E = 8
DI, DS, DR, KC = 256, 16, 64, 4
CI = DI // P
STEPS = 8
EPS = 1e-5

COLS = {}
for _name, _n in (("q_b", 1), ("k_b", 1), ("out_b", 1), ("g_attn", 1), ("b_attn", 1), ("g1", 1), ("b1", 1),
                  ("g2", 1), ("b2", 1), ("b_inl", 1), ("ff_b1", FF // P), ("ff_b2", 1), ("moe_b1", E * FF // P),
                  ("moe_b2", E), ("norm_w", 1), ("norm_b", 1), ("conv_w", CI * KC), ("conv_b", CI), ("dt_b", CI),
                  ("A_log", CI * DS), ("D_param", CI), ("q_gate", 1), ("proj_b", 1), ("part12", 1), ("part2", 1)):
    COLS[_name] = (sum(n for _, n in COLS.values()), _n)
NCOLS = sum(n for _, n in COLS.values())


def build(nc, a, out):
    scratch_q = nc.dram_tensor("scratch_q", [B * H, HR, S], BF16).ap()
    scratch_k = nc.dram_tensor("scratch_k", [B * H, HR, S], BF16).ap()
    scratch_o = nc.dram_tensor("scratch_o", [B, H // GH, P, S], F32).ap()
    scratch_x = nc.dram_tensor("scratch_x", [B, H // GH, P, XQ], F32).ap()

    with ExitStack() as ctx:
        def sb(name, shape, dt=F32):
            return ctx.enter_context(nc.sbuf_tensor(name, shape, dt))

        phase_sems = []

        def sem(name):
            phase_sems.append(nc.alloc_semaphore(name))
            return phase_sems[-1]

        def end_phase():
            nc.clear_and_free_semaphores(phase_sems)
            phase_sems.clear()
            nc.all_engine_barrier()

        x_res = sb("x_res", [P, B * S])
        h0 = sb("h0", [P, B * S])
        v_tok = sb("v_tok", [P, B * QT * D])
        w = {}
        for name, shape, dt in (
                ("cols", [P, NCOLS], F32), ("qkv_w", [P, 3 * D], F32), ("v_bias", [P, CH], F32),
                ("out_w", [P, H // GH, D], F32), ("w_ctx", [P, D], F32), ("w_x", [P, D], F32),
                ("ff_w1", [P, FF], F32), ("ff_w2", [P, FF // P, D], F32), ("Wg", [P, E], F32), ("bg", [P, CH // P * E], F32),
                ("W1", [P, E, FF], F32), ("W2", [P, E, FF // P, D], F32), ("in_proj_w", [P, 2 * DI], F32),
                ("x_proj_dt", [P, CI, DR], F32), ("x_proj_bc", [P, CI, 3 * 2 * DS], F32), ("dt_proj_w", [DR, DI], F32),
                ("out_proj_w", [P, CI, D], F32), ("qkv2_w", [P, 3 * D], F32), ("proj_w", [P, H // GH, D], F32),
                ("ident", [P, P], F32), ("mean_w", [P, P], F32), ("den_sel", [P, P], F32),
                ("head_sel", [P, H], F32), ("head_back", [H, P], F32), ("sim_sum", [H, P], F32), ("iota", [P, CH // P, E], F32),
                ("ident_b", [P, P], BF16), ("mask_qk", [P, P], BF16), ("mask_kq", [P, P], BF16),
                ("exp_sel", [E, E, P], BF16), ("bc_sel", [6 * DS, 2 * DS, P], BF16)):
            w[name] = sb("w_" + name, shape, dt)

        def col(name, i=0):
            at = COLS[name][0] + i
            return w["cols"][:, at:at + 1]

        eps_col = sb("eps_col", [P, 1])
        a_neg = sb("a_neg", [P, CI * DS])
        q_gate_sel = sb("q_gate_sel", [P, H])
        gate_tmp = sb("gate_tmp", [P, 4])
        bc_parts = sb("bc_parts", [6 * DS, S], BF16)
        m_cat = sb("m_cat", [P, 2, 40])
        m_col = sb("m_col", [P, P])
        m_neg = sb("m_neg", [40, 2, P])
        m_parts = sb("m_parts", [40, 2, 3, P], BF16)
        qx = sb("qx", [P, 2, GH, XQ], BF16)
        small = sb("small", [P, 2, 160])
        onehot_b = sb("onehot_b", [E, 2, CH], BF16)
        NWK = 21
        work = sb("work", [P, NWK, S])

        ps = ctx.enter_context(nc.psum_tensor("ps", [P, 8, CH], F32))

        def chunks(slot):
            return [work[:, slot, c * CH:(c + 1) * CH] for c in range(2)]

        def bank(c, i):
            return ps[:, 4 * c + i, :]

        XR, DEV, SQ, RSTD, NRM = (chunks(i) for i in range(5))
        CTX, XA, XS, CW, GV, TT_ = (chunks(i) for i in range(5, 11))
        OL = [work[:, 11 + 2 * c:13 + 2 * c, :].rearrange("p a n -> p (a n)").rearrange("p (g n) -> p g n", g=4)
              for c in range(2)]
        HID = [work[:, 15 + 2 * c:17 + 2 * c, :].rearrange("p a n -> p (a n)").rearrange("p (m n) -> p m n", m=4)
               for c in range(2)]
        XIN = [work[:, 12, c * CH:(c + 1) * CH].rearrange("p (t f) -> p t f", t=4) for c in range(2)]
        QK32 = [work[:, 5 + c, :].rearrange("p (a n) -> p a n", a=2) for c in range(2)]
        REST = [work[:, 7 + c, :].rearrange("p (a n) -> p a n", a=2) for c in range(2)]
        PARTS = [work[:, 9:12, :].rearrange("p a n -> p (a n)")[:, 1536 * c:1536 * (c + 1)].bitcast(BF16)
                 .rearrange("p (t a n) -> p t a n", t=3, a=2) for c in range(2)]
        MOE_Y, ACC = chunks(5), chunks(6)
        XN = chunks(13)
        CONV = work[:, 17:20, :].rearrange("p a n -> p (a n)")[:, 0:CI * (KC - 1 + S)].rearrange("p (i n) -> p i n", i=CI)

        def norm_sems(tag):
            return {k: sem(f"{tag}_{k}") for k in ("mean", "centred", "squared", "var", "log", "rstd", "out", "affine")}

        def norm_pe(pe, s, n, src, ready):
            for c in range(2):
                ready(pe, c)
                nc.tensor.matmul(bank(c, 0), w["mean_w"][:, :], src[c], start=True, stop=True).then_inc(s["mean"], 1)
            for c in range(2):
                pe.wait_ge(s["squared"], n + c)
                nc.tensor.matmul(bank(c, 0), w["mean_w"][:, :], SQ[c], start=True, stop=True).then_inc(s["var"], 1)

        def norm_act(act, s, n):
            for c in range(2):
                act.wait_ge(s["centred"], n + c)
                nc.scalar.activation(SQ[c], DEV[c], ACT.Square).then_inc(s["squared"], 1)
            for c in range(2):
                act.wait_ge(s["var"], n + c)
                nc.scalar.activation(RSTD[c], bank(c, 0), ACT.Ln, bias=eps_col[:, :]).then_inc(s["log"], 1)
                act.wait_ge(s["log"], n + c)
                nc.scalar.activation(RSTD[c], RSTD[c], ACT.Exp, scale=-0.5).then_inc(s["rstd"], 1)

        def norm_dve(dve, s, n, src, dst, gain=None, shift=None, n_affine=None):
            for c in range(2):
                dve.wait_ge(s["mean"], n + c)
                nc.vector.tensor_tensor(DEV[c], src[c], bank(c, 0), ALU.subtract).then_inc(s["centred"], 1)
            for c in range(2):
                dve.wait_ge(s["rstd"], n + c)
                nc.vector.tensor_tensor(dst[c], DEV[c], RSTD[c], ALU.mult).then_inc(s["out"], 1)
                if gain:
                    dve.wait_ge(s["out"], n + c)
                    nc.vector.tensor_scalar(dst[c], dst[c], col(gain), col(shift), ALU.mult,
                                            ALU.add).then_inc(s["affine"], 1)

        def qkv_sems(tag):
            d = {k: sem(f"{tag}_{k}") for k in ("qk", "v", "qk_sb", "part1", "rest", "part2", "part3", "v_kept")}
            d["stored"] = [sem(f"{tag}_stored{c}") for c in range(2)]
            return d

        def qkv_pe(pe, s, n, weights, src, ready):
            for c in range(2):
                ready(pe, c)
                for i in range(2):
                    mm = nc.tensor.matmul(bank(c, 1 + i), weights[:, i * D:(i + 1) * D], src[c], start=True, stop=True)
                mm.then_inc(s["qk"], 1)
                for t in range(CH // P):
                    mm = nc.tensor.matmul(ps[:, 4 * c + 3, t * P:(t + 1) * P], src[c][:, t * P:(t + 1) * P],
                                          weights[:, 2 * D:3 * D], start=True, stop=True)
                mm.then_inc(s["v"], 1)

        def qkv_act(act, s, n, biased):
            for c in range(2):
                act.wait_ge(s["qk"], n + c)
                for i, name in enumerate(("q_b", "k_b")):
                    bias = col(name) if biased else 0.0
                    nc.scalar.activation(QK32[c][:, i, :], bank(c, 1 + i), ACT.Identity,
                                         bias=bias).then_inc(s["qk_sb"], 1)
                act.wait_ge(s["qk_sb"], 2 * (n + c))
                nc.scalar.copy(PARTS[c][:, 0, :, :], QK32[c]).then_inc(s["part1"], 1)
            for c in range(2):
                act.wait_ge(s["rest"], n + c)
                nc.scalar.copy(PARTS[c][:, 1, :, :], REST[c]).then_inc(s["part2"], 1)

        def qkv_dve(dve, s, n, b, biased):
            for c in range(2):
                dve.wait_ge(s["v"], n + c)
                dst = v_tok[:, bass.ds(b * S + c * CH, CH)]
                if biased:
                    ins = nc.vector.tensor_tensor(dst, bank(c, 3), w["v_bias"][:, :], ALU.add)
                else:
                    ins = nc.vector.tensor_scalar(dst, bank(c, 3), 1.0, None, ALU.mult)
                ins.then_inc(s["v_kept"], 1)
                dve.wait_ge(s["part1"], n + c)
                nc.vector.tensor_tensor(REST[c], QK32[c], PARTS[c][:, 0, :, :], ALU.subtract).then_inc(s["rest"], 1)
            for c in range(2):
                dve.wait_ge(s["part2"], n + c)
                nc.vector.tensor_tensor(PARTS[c][:, 2, :, :], REST[c], PARTS[c][:, 1, :, :],
                                        ALU.subtract).then_inc(s["part3"], 1)

        def qkv_store(sp, s, n, b):
            for c in range(2):
                sp.wait_ge(s["part3"], n + c)
                for i, (dram, slots) in enumerate(((scratch_q, SLOTS_Q), (scratch_k, SLOTS_K))):
                    for k, part in enumerate(slots):
                        sp.dma_start(dram[bass.ds(b * H, H), k * HD:(k + 1) * HD, c * CH:(c + 1) * CH],
                                     PARTS[c][:, part, i, :]).then_inc(s["stored"][c], 16)

        STORED = 2 * NS * 16

        QZ = [work[:, 2 * i:2 * i + 2, :].rearrange("p a n -> p (a n)").bitcast(BF16).rearrange("p (j n) -> p j n", j=GH)
              for i in range(2)]
        KP = [work[:, 4 + i, :].bitcast(BF16).rearrange("p (r n) -> p r n", r=2) for i in range(2)]
        VP = [work[:, 6 + i, :].rearrange("p (k j d) -> p k j d", k=QT, j=GH) for i in range(2)]
        EB = [work[:, 8 + i, :].rearrange("p (a n) -> p a n", a=2) for i in range(4)]
        OS, RD, ONT = chunks(12), chunks(13), chunks(14)
        SX = work[:, 15, 0:3 * XQ].rearrange("p (a n) -> p a n", a=3)
        SA = [ps[:, i, :] for i in range(2)]
        SB = [ps[:, 2 + 2 * i:4 + 2 * i, :] for i in range(2)]
        OB = [ps[:, 6 + i, :] for i in range(2)]

        def attention(tag, causal):
            NX = 0 if causal else 1
            s1 = []
            for j in range(GH):
                for qt in range(QT):
                    for half in range(2):
                        width = min(CH, P * (qt + 1) - CH * half) if causal else CH
                        if width > 0:
                            s1.append((j, qt, half, width, causal and width == P * (qt + 1) - CH * half))
            for half in range(2 * NX):
                s1.append(("x", None, half, CH, False))
            NU = len(s1)
            assert NU % 2 == 0
            s2 = []
            for qh in range(2):
                for kc in range(QT):
                    for pr in range(2):
                        off = max(0, P * kc - CH * qh) if causal else 0
                        if off < CH:
                            s2.append((qh, kc, pr, off, causal and P * kc >= CH * qh))
            last = [max(i for i, u in enumerate(s2) if u[0] == qh) for qh in range(2)]
            lastk = [max(u[1] for u in s2 if u[0] == qh) for qh in range(2)]
            s2 += [("x", None, None, 0, False)] * NX
            NV = len(s2)
            NO = 2 + NX
            DELAY = 5

            sems = {k: sem(f"{tag}_{k}") for k in (
                "scores1", "scores1_read", "max", "m_ready", "m_turned", "m_chain", "m_split",
                "v_ready", "scores2", "exp_done", "pv_done", "o_sb", "den", "log", "inv", "normed", "o_free")}
            loaded = [sem(f"{tag}_loaded{p}") for p in range(2)]
            m_rows = [sem(f"{tag}_m_rows{p}") for p in range(2)]
            o_stored = [sem(f"{tag}_o_stored{q}") for q in range(NO)]
            LOAD = 16 * (GH + GH // 2 + GH * NX)
            MROWS = 16 * (3 + 3 * NX)

            def sp_load(sp, gi, p):
                for pr in range(GH // 2):
                    heads = scratch_k[bass.ds(gi * GH + 2 * pr, 2), :, :].rearrange("h r n -> (h r) n")
                    sp.dma_start(KP[p][0:R_MAX, pr, :], heads).then_inc(loaded[p], 16)
                for j in range(GH):
                    r = HR * (j % 2)
                    sp.dma_start(QZ[p][r:r + HR, j, :], scratch_q[gi * GH + j, :, :]).then_inc(loaded[p], 16)
                    if NX:
                        sp.dma_start(qx[r:r + R_MASK, p, j, :],
                                     scratch_q[gi * GH + j, 0:R_MASK, 0:XQ]).then_inc(loaded[p], 16)

            def sp_rows(sp, gi, p):
                sp.wait_ge(sems["m_split"], gi + 1)
                for t in range(3):
                    sp.dma_start(QZ[p][R_MAX + t:R_MAX + t + 1, :, :], m_parts[0:GH * QT, p, t, :]).then_inc(m_rows[p], 16)
                    if NX:
                        sp.dma_start(qx[R_MAX + t:R_MAX + t + 1, p, :, :],
                                     m_parts[32:33, p, t, :]).then_inc(m_rows[p], 16)

            def sp_store(sp, gi):
                for q in range(2):
                    sp.wait_ge(sems["normed"], gi * NO + q + 1)
                    dst = scratch_o.rearrange("b g p n -> (b g) p n")[gi, :, q * CH:(q + 1) * CH]
                    sp.dma_start(dst, ONT[q]).then_inc(o_stored[q], 16)
                if NX:
                    sp.wait_ge(sems["normed"], gi * NO + 3)
                    sp.dma_start(scratch_x.rearrange("b g p n -> (b g) p n")[gi, :, :], SX[:, 2, :]).then_inc(o_stored[2], 16)

            def pe_max(pe, gi, p, k, u):
                base = gi * (NU + 1)
                if u == 0:
                    pe.wait_ge(loaded[p], k * LOAD)
                pe.wait_ge(sems["scores1_read"], base + 1 + max(0, u - 1))
                if u == NU:
                    pe.wait_ge(sems["m_ready"], gi + 1)
                    nc.tensor.transpose(SA[0][:, 0:P], m_col[:, :], w["ident"][:, :]).then_inc(sems["m_turned"], 1)
                    return
                j, qt, half, width, diag = s1[u]
                dst = SA[u % 2]
                if j == "x":
                    for j in range(GH):
                        mm = nc.tensor.matmul(dst[32 * j:32 * j + XQ, :], qx[0:R_MAX, p, j, :],
                                              KP[p][0:R_MAX, j // 2, half * CH:(half + 1) * CH], start=True, stop=True)
                    mm.then_inc(sems["scores1"], 1)
                    return
                mm = nc.tensor.matmul(dst[:, 0:width], QZ[p][0:R_MAX, j, qt * P:(qt + 1) * P],
                                      KP[p][0:R_MAX, j // 2, half * CH:half * CH + width], start=True, stop=not diag)
                if diag:
                    mm = nc.tensor.matmul(dst[:, width - P:width], w["ident_b"][:, :], w["mask_qk"][:, :],
                                          start=False, stop=True)
                mm.then_inc(sems["scores1"], 1)

            def pe_scores(pe, gi, p, k, v):
                base = gi * NV
                if v == 0:
                    pe.wait_ge(m_rows[p], k * MROWS)
                pe.wait_ge(sems["exp_done"], base + 1 + max(0, v - 1))
                qh, kc, pr, off, diag = s2[v]
                dst = SB[v % 2]
                if qh == "x":
                    for kc in range(QT):
                        for j in range(GH):
                            at = XQ * (2 * kc + j // 2)
                            mm = nc.tensor.matmul(dst[:, j % 2, at:at + XQ], KP[p][0:R_END, j // 2, kc * P:(kc + 1) * P],
                                                  qx[0:R_END, p, j, :], start=True, stop=True)
                    mm.then_inc(sems["scores2"], 1)
                    return
                for i in range(2):
                    mm = nc.tensor.matmul(dst[:, i, off:CH], KP[p][0:R_END, pr, kc * P:(kc + 1) * P],
                                          QZ[p][0:R_END, 2 * pr + i, qh * CH + off:(qh + 1) * CH], start=True, stop=not diag)
                    if diag:
                        mm = nc.tensor.matmul(dst[:, i, off:off + P], w["ident_b"][:, :], w["mask_kq"][:, :],
                                              start=False, stop=True)
                mm.then_inc(sems["scores2"], 1)

            def pe_values(pe, gi, p, v):
                if v == 0:
                    pe.wait_ge(sems["v_ready"], gi + 1)
                pe.wait_ge(sems["exp_done"], gi * NV + v + 2)
                qh, kc, pr, off, _ = s2[v]
                if qh == "x":
                    pe.wait_ge(sems["o_free"], o_need(gi, 2))
                    for kc in range(QT):
                        for j in range(GH):
                            at = XQ * (2 * kc + j // 2)
                            mm = nc.tensor.matmul(OB[0][32 * j:32 * j + 32, 0:XQ], VP[p][:, kc, j, :],
                                                  EB[v % 4][:, j % 2, at:at + XQ],
                                                  start=(kc == 0), stop=(kc == QT - 1))
                    mm.then_inc(sems["pv_done"], 1)
                    return
                if kc == 0 and pr == 0:
                    pe.wait_ge(sems["o_free"], o_need(gi, qh))
                for i in range(2):
                    j = 2 * pr + i
                    mm = nc.tensor.matmul(OB[qh][32 * j:32 * j + 32, off:CH], VP[p][:, kc, j, :], EB[v % 4][:, i, off:CH],
                                          start=(kc == 0), stop=(kc == lastk[qh]))
                mm.then_inc(sems["pv_done"], 1)

            def pe_den(pe, gi, o):
                pe.wait_ge(sems["o_sb"], gi * NO + o + 1)
                dst, src = (OB[0][:, 0:XQ], SX[:, 0, :]) if o == 2 else (OB[o], OS[o])
                nc.tensor.matmul(dst, w["den_sel"][:, :], src, start=True, stop=True).then_inc(sems["den"], 1)

            def o_need(gi, o):
                return gi * NO + ((NO if NX else 1), 2, NO + 1)[o]

            def due(v):
                return max(0, -(-NU * (v - DELAY + 1) // (NV - DELAY)))

            def pe_step(pe, gi, p, k, ahead):
                u = 0
                pe_scores(pe, gi, p, k, 0)
                pe_scores(pe, gi, p, k, 1)
                for v in range(NV):
                    while ahead and u < due(v):
                        pe_max(pe, gi + 1, 1 - p, k + p, u)
                        u += 1
                    pe_values(pe, gi, p, v)
                    if v + 2 < NV:
                        pe_scores(pe, gi, p, k, v + 2)
                    if v == last[0] + 3:
                        pe_den(pe, gi, 0)
                    if NX and v == last[1]:
                        pe_den(pe, gi, 1)
                if ahead:
                    pe_max(pe, gi + 1, 1 - p, k + p, NU)
                pe_den(pe, gi, NO - 1)

            def act_step(act, gi, p):
                for v in range(NV):
                    qh, kc, pr, off, _ = s2[v]
                    act.wait_ge(sems["scores2"], gi * NV + v + 1)
                    act.wait_ge(sems["pv_done"], gi * NV + 1 + max(0, v - 3))
                    nc.scalar.activation(EB[v % 4][:, :, off:CH], SB[v % 2][:, :, off:CH], ACT.Exp,
                                         scale=SCALE).then_inc(sems["exp_done"], 1)
                    if v == last[0] + 2:
                        act_copy(act, gi, 0)
                    if v == last[0] + 4:
                        act_inv(act, gi, 0)
                    if NX and v == last[1]:
                        act_copy(act, gi, 1)
                act_copy(act, gi, NO - 1)
                for o in range(1, NO):
                    act_inv(act, gi, o)

            def act_copy(act, gi, o):
                act.wait_ge(sems["pv_done"], gi * NV + (NV if o == 2 else last[o] + 1) + 1)
                dst, src = (SX[:, 0, :], OB[0][:, 0:XQ]) if o == 2 else (OS[o], OB[o])
                act.wait_ge(sems["o_free"], gi * NO + o + 1)
                nc.scalar.copy(dst, src).then_inc(sems["o_sb"], 1)

            def act_inv(act, gi, o):
                act.wait_ge(sems["den"], gi * NO + o + 1)
                den, inv = (OB[0][:, 0:XQ], SX[:, 1, :]) if o == 2 else (OB[o], RD[o])
                nc.scalar.activation(inv, den, ACT.Ln).then_inc(sems["log"], 1)
                act.wait_ge(sems["log"], gi * NO + o + 1)
                nc.scalar.activation(inv, inv, ACT.Exp, scale=-1.0).then_inc(sems["inv"], 1)

            def dve_max(dve, gi, u):
                dve.wait_ge(sems["scores1"], gi * NU + u + 1)
                j, qt, half, width, _ = s1[u]
                at = 32 if j == "x" else QT * j + qt
                nc.vector.tensor_reduce(m_cat[:, half, at:at + 1], SA[u % 2][:, 0:width], AX.X,
                                        ALU.max).then_inc(sems["scores1_read"], 1)

            def dve_rows(dve, gi, p):
                n = 33 if NX else 32
                dve.wait_ge(sems["scores1_read"], gi * (NU + 1) + NU + 1)
                nc.vector.tensor_tensor(m_col[:, 0:n], m_cat[:, 0, 0:n], m_cat[:, 1, 0:n],
                                        ALU.max).then_inc(sems["m_ready"], 1)
                dve.wait_ge(sems["m_turned"], gi + 1)
                nc.vector.tensor_scalar(m_neg[:, 0, :], SA[0][0:40, 0:P], -1.0, None,
                                        ALU.mult).then_inc(sems["scores1_read"], 1)
                k = gi * 3
                dve.wait_ge(sems["scores1_read"], (gi + 1) * (NU + 1) + 1)
                nc.vector.tensor_copy(m_parts[:, p, 0, :], m_neg[:, 0, :]).then_inc(sems["m_chain"], 1)
                dve.wait_ge(sems["m_chain"], k + 1)
                nc.vector.tensor_tensor(m_neg[:, 1, :], m_neg[:, 0, :], m_parts[:, p, 0, :],
                                        ALU.subtract).then_inc(sems["m_chain"], 1)
                dve.wait_ge(sems["m_chain"], k + 2)
                nc.vector.tensor_copy(m_parts[:, p, 1, :], m_neg[:, 1, :]).then_inc(sems["m_chain"], 1)
                dve.wait_ge(sems["m_chain"], k + 3)
                nc.vector.tensor_tensor(m_parts[:, p, 2, :], m_neg[:, 1, :], m_parts[:, p, 1, :],
                                        ALU.subtract).then_inc(sems["m_split"], 1)

            def dve_out(dve, gi, o):
                dve.wait_ge(sems["inv"], gi * NO + o + 1)
                inv, src, dst = (SX[:, 1, :], SX[:, 0, :], SX[:, 2, :]) if o == 2 else (RD[o], OS[o], ONT[o])
                if o < 2:
                    dve.wait_ge(o_stored[o], gi * 16 + 16)
                else:
                    dve.wait_ge(o_stored[2], gi * 16 + 16)
                nc.vector.tensor_tensor(dst, src, inv, ALU.mult).then_inc(sems["normed"], 1)
                dve.wait_ge(sems["normed"], gi * NO + o + 1)
                dve.sem_inc(sems["o_free"], 1)

            def dve_step(dve, gi, p, ahead):
                u = 0
                for v in range(NV):
                    while ahead and u < due(v):
                        dve_max(dve, gi + 1, u)
                        u += 1
                    if v == last[0] + 6:
                        dve_out(dve, gi, 0)
                if NX:
                    dve_out(dve, gi, 1)
                if ahead:
                    dve_rows(dve, gi + 1, 1 - p)
                dve_out(dve, gi, 2 if NX else 1)

            return dict(locals())

        def run_attention(tag, causal):
            t = attention(tag, causal)
            sems, NO, NX, NV = t["sems"], t["NO"], t["NX"], t["NV"]
            steps = GROUPS // 2 - 1
            v_init, s_init, s_xrows = sem(f"{tag}_v_init"), sem(f"{tag}_init"), sem(f"{tag}_xrows")
            with nc.Block() as block:
                @block.sync
                def _(sp):
                    sp.wait_ge(s_init, 6)
                    if NX:
                        for p in range(2):
                            for j in range(GH):
                                r = HR * (j % 2) + R_MASK
                                sp.dma_start(qx[r:r + 2, p, j, :], a["x_rows"]).then_inc(s_xrows, 16)
                        sp.wait_ge(s_xrows, 16 * 2 * GH)
                    for q in range(NO):
                        sp.sem_inc(t["o_stored"][q], 16)
                    t["sp_load"](sp, 0, 0)
                    t["sp_load"](sp, 1, 1)
                    t["sp_rows"](sp, 0, 0)
                    with sp.Fori(0, steps) as i:
                        for s in range(2):
                            g = i * 2 + s
                            t["sp_rows"](sp, g + 1, 1 - s)
                            t["sp_store"](sp, g)
                            sp.wait_ge(sems["pv_done"], g * NV + NV + 1)
                            t["sp_load"](sp, g + 2, s)
                    t["sp_rows"](sp, GROUPS - 1, 1)
                    t["sp_store"](sp, GROUPS - 2)
                    t["sp_store"](sp, GROUPS - 1)
                    for q in range(NO):
                        sp.wait_ge(t["o_stored"][q], 16 * (GROUPS + 1))

                @block.tensor
                def _(pe):
                    pe.sem_inc(sems["pv_done"], 1)
                    for u in range(t["NU"] + 1):
                        t["pe_max"](pe, 0, 0, 1, u)
                    with pe.Fori(0, steps) as i:
                        for s in range(2):
                            t["pe_step"](pe, i * 2 + s, s, i + 1, True)
                    t["pe_step"](pe, GROUPS - 2, 0, GROUPS // 2, True)
                    t["pe_step"](pe, GROUPS - 1, 1, GROUPS // 2, False)

                @block.scalar
                def _(act):
                    act.preload_act_table_set("natural_log_exp_and_others")
                    act.sem_inc(sems["exp_done"], 1)
                    with act.Fori(0, steps) as i:
                        for s in range(2):
                            t["act_step"](act, i * 2 + s, s)
                    for g in range(GROUPS - 2, GROUPS):
                        t["act_step"](act, g, g % 2)

                @block.vector
                def _(dve):
                    dve.sem_inc(sems["scores1_read"], 1)
                    dve.sem_inc(sems["o_free"], NO)
                    for u in range(t["NU"]):
                        t["dve_max"](dve, 0, u)
                    t["dve_rows"](dve, 0, 0)
                    with dve.Fori(0, steps) as i:
                        for s in range(2):
                            t["dve_step"](dve, i * 2 + s, s, True)
                    t["dve_step"](dve, GROUPS - 2, 0, True)
                    t["dve_step"](dve, GROUPS - 1, 1, False)


                def pool_v(pool, b, g, p):
                    rows = v_tok[:, bass.ds(b * S, S)].rearrange("p (k f) -> p k f", k=QT)
                    for j in range(GH):
                        at = (g * GH + j) * HD
                        ins = nc.gpsimd.tensor_copy(VP[p][:, :, j, 0:HD], rows[:, :, at:at + HD])
                    ins.then_inc(sems["v_ready"], 1)

                @block.gpsimd
                def _(pool):
                    for p in range(2):
                        pool.memset(QZ[p], 0.0).then_inc(s_init, 1)
                        pool.wait_ge(s_init, 3 * p + 1)
                        pool.memset(KP[p][96:P, :, :], 1.0).then_inc(s_init, 1)
                        pool.wait_ge(s_init, 3 * p + 2)
                        pool.memset(qx[:, p, :, :], 0.0).then_inc(s_init, 1)
                        pool.wait_ge(s_init, 3 * p + 3)
                    for p in range(2):
                        pool.memset(VP[p], 0.0).then_inc(v_init, 1)
                        pool.wait_ge(v_init, 2 * p + 1)
                        pool.memset(VP[p][:, :, :, HD:HD + 1], 1.0).then_inc(v_init, 1)
                        pool.wait_ge(v_init, 2 * p + 2)
                    for g in range(2):
                        pool_v(pool, 0, g, g)
                    with pool.Fori(0, B - 1) as b:
                        for g in range(4):
                            pool.wait_ge(sems["pv_done"], b * (4 * NV) + (g + 1) * NV + 1)
                            pool_v(pool, b + (g + 2) // 4, (g + 2) % 4, g % 2)
                    for g in range(2):
                        pool.wait_ge(sems["pv_done"], (GROUPS - 4 + g) * NV + NV + 1)
                        pool_v(pool, B - 1, 2 + g, g)

        s_w, s_small, s_zero = sem("s_w"), sem("s_small"), sem("s_zero")
        s_gate, s_rows0 = [sem(f"s_gate{i}") for i in range(8)], sem("s_rows0")
        zero_tile = work[:, 1, :].bitcast(BF16)[:, 0:S]
        with nc.Block() as block:
            @block.sync
            def _(sp):
                for name, t in w.items():
                    dst = t[tuple(slice(None) for _ in t.shape)]
                    sp.dma_start(dst, a[name]).then_inc(s_w, 16)
                sp.wait_ge(s_zero, 1)
                for b in range(B):
                    hs = slice(b * H, (b + 1) * H)
                    for dram in (scratch_q, scratch_k):
                        sp.dma_start(dram[hs, R_MASK:HR, :], zero_tile[0:2 * H, :]).then_inc(s_rows0, 16)
                sp.wait_ge(s_rows0, 16 * 2 * B)

            @block.gpsimd
            def _(pool):
                pool.memset(zero_tile, 0.0).then_inc(s_zero, 1)
                pool.memset(eps_col[:, :], EPS).then_inc(s_zero, 1)
                pool.memset(m_cat[:, :, :], -3.0e38)
                pool.memset(m_col[:, :], 0.0)

            @block.scalar
            def _(act):
                act.preload_act_table_set("natural_log_exp_and_others")
                act.wait_ge(s_w, 16 * len(w))
                act.wait_ge(s_gate[7], 1)
                nc.scalar.activation(a_neg[:, :], a_neg[:, :],
                                     ACT.Exp).then_inc(s_gate[0], 1)
                nc.scalar.activation(gate_tmp[:, 0:1], col("q_gate"), ACT.Square).then_inc(s_gate[1], 1)
                act.wait_ge(s_gate[2], 1)
                nc.scalar.activation(gate_tmp[0:H, 1:2], ps[0:H, 0, 0:1], ACT.Ln).then_inc(s_gate[3], 1)
                act.wait_ge(s_gate[3], 1)
                nc.scalar.activation(gate_tmp[0:H, 2:3], gate_tmp[0:H, 1:2], ACT.Exp, scale=-0.5).then_inc(s_gate[4], 1)

            @block.tensor
            def _(pe):
                pe.wait_ge(s_w, 16 * len(w))
                pe.wait_ge(s_gate[1], 1)
                nc.tensor.matmul(ps[0:H, 0, 0:1], w["head_sel"][:, :], gate_tmp[:, 0:1], start=True,
                                 stop=True).then_inc(s_gate[2], 1)
                pe.wait_ge(s_gate[4], 1)
                nc.tensor.matmul(ps[:, 1, 0:1], w["head_back"][:, :], gate_tmp[0:H, 2:3], start=True,
                                 stop=True).then_inc(s_gate[5], 1)

            @block.vector
            def _(dve):
                dve.wait_ge(s_w, 16 * len(w))
                nc.vector.tensor_scalar(a_neg[:, :], w["cols"][:, COLS["A_log"][0]:COLS["A_log"][0] + CI * DS], 80.0,
                                        None, ALU.min).then_inc(s_gate[7], 1)
                dve.wait_ge(s_gate[0], 1)
                nc.vector.tensor_scalar(a_neg[:, :], a_neg[:, :], -1.0, None, ALU.mult)
                dve.wait_ge(s_gate[5], 1)
                nc.vector.tensor_tensor(gate_tmp[:, 3:4], col("q_gate"), ps[:, 1, 0:1], ALU.mult).then_inc(s_gate[6], 1)
                dve.wait_ge(s_gate[6], 1)
                nc.vector.tensor_scalar(q_gate_sel[:, :], w["head_sel"][:, :], gate_tmp[:, 3:4], None, ALU.mult)

        end_phase()

        a_norm, a_qkv = norm_sems("a_norm"), qkv_sems("a_qkv")
        a_x = [sem(f"a_x{c}") for c in range(2)]
        a_free, a_turned, a_copied, a_kept = sem("a_free"), sem("a_turned"), sem("a_copied"), sem("a_kept")
        x_dram = a["x"]
        with nc.Block() as block:
            @block.sync
            def _(sp):
                with sp.Fori(0, B) as b:
                    for c in range(2):
                        sp.wait_ge(a_free, b * 2 + c + 1)
                        sp.dma_start(XIN[c], x_dram[bass.ds(b * QT + 4 * c, 4), :, :].rearrange("t p f -> p t f")
                                     ).then_inc(a_x[c], 16)
                    qkv_store(sp, a_qkv, b * 2 + 1, b)
                for c in range(2):
                    sp.wait_ge(a_qkv["stored"][c], STORED * B)

            @block.tensor
            def _(pe):
                pe.sem_inc(a_free, 2)
                with pe.Fori(0, B) as b:
                    for c in range(2):
                        pe.wait_ge(a_x[c], b * 16 + 16)
                        for t in range(4):
                            mm = nc.tensor.transpose(ps[:, 4 * c, t * P:(t + 1) * P], XIN[c][:, t, :], w["ident"][:, :])
                        mm.then_inc(a_turned, 1)
                        pe.wait_ge(a_turned, b * 2 + c + 1)
                        pe.sem_inc(a_free, 1)
                    norm_pe(pe, a_norm, b * 4 + 1, XR, lambda e, c: e.wait_ge(a_copied, b * 2 + c + 1))
                    norm_pe(pe, a_norm, b * 4 + 3, NRM, lambda e, c: e.wait_ge(a_norm["out"], b * 4 + 1 + c))
                    qkv_pe(pe, a_qkv, b * 2 + 1, w["qkv_w"], XN, lambda e, c: e.wait_ge(a_norm["affine"], b * 2 + c + 1))

            @block.scalar
            def _(act):
                act.preload_act_table_set("natural_log_exp_and_others")
                with act.Fori(0, B) as b:
                    norm_act(act, a_norm, b * 4 + 1)
                    norm_act(act, a_norm, b * 4 + 3)
                    qkv_act(act, a_qkv, b * 2 + 1, True)
                    for c in range(2):
                        act.wait_ge(a_qkv["stored"][c], b * STORED + STORED)

            @block.vector
            def _(dve):
                with dve.Fori(0, B) as b:
                    for c in range(2):
                        dve.wait_ge(a_turned, b * 2 + c + 1)
                        nc.vector.tensor_copy(XR[c], bank(c, 0)).then_inc(a_copied, 1)
                    norm_dve(dve, a_norm, b * 4 + 1, XR, NRM)
                    norm_dve(dve, a_norm, b * 4 + 3, NRM, XN, "g_attn", "b_attn", n_affine=b * 2 + 1)
                    qkv_dve(dve, a_qkv, b * 2 + 1, b, True)
                    dve.wait_ge(a_kept, b * 4 + 4)

            @block.gpsimd
            def _(pool):
                with pool.Fori(0, B) as b:
                    for c in range(2):
                        pool.wait_ge(a_copied, b * 2 + c + 1)
                        nc.gpsimd.tensor_copy(x_res[:, bass.ds(b * S + c * CH, CH)], XR[c]).then_inc(a_kept, 1)
                    for c in range(2):
                        pool.wait_ge(a_norm["out"], b * 4 + c + 1)
                        nc.gpsimd.tensor_copy(h0[:, bass.ds(b * S + c * CH, CH)], NRM[c]).then_inc(a_kept, 1)

        end_phase()
        run_attention("b", True)
        end_phase()

        CV = [[work[:, 13 + c, i * CH:(i + 1) * CH] for i in range(CI)] for c in range(2)]
        SZ, U, DL, DU, DA, DBU, HS, HC = ([work[:, k + i, :] for i in range(CI)] for k in (5, 7, 9, 11, 13, 15, 17, 19))
        SP1 = [[work[:, 15 + c, i * CH:(i + 1) * CH] for i in range(CI)] for c in range(2)]
        SP2 = chunks(20)
        YT = DBU
        B_HI = [SQ[c].bitcast(BF16)[0:6 * DS, 0:CH] for c in range(2)]
        B_MID = [SQ[c].bitcast(BF16)[0:6 * DS, CH:2 * CH] for c in range(2)]
        B_REST = [DEV[c][0:6 * DS, :] for c in range(2)]
        DT = [RSTD[c][0:DR, :] for c in range(2)]
        SIM16 = [work[0:H, 14, c * CH:(c + 1) * CH] for c in range(2)]

        def gate(c, k):
            return small[:, c, 32 * k:32 * k + 32].rearrange("p (t e) -> p t e", t=4)

        gmax = [small[:, c, 128:132] for c in range(2)]
        gmin = [small[:, c, 132:136] for c in range(2)]
        iota = w["iota"]

        NLN = 9
        ln = norm_sems("c_norm")
        qs = qkv_sems("c_qkv")
        cs = {k: sem("c_" + k) for k in (
            "trip_end", "att", "ctx", "xa", "ctxw", "cw", "rec", "tsum", "tanh", "diff", "vel", "xs", "xa2",
            "ffh", "gelu", "ffy", "xa3", "xr1", "gates", "g_sb", "g_max", "g_less", "g_cand", "g_min", "onehot",
            "oh_turned", "oh_b", "mask", "moe_h", "relu", "moe_y", "moe_y_sb", "masked", "acc", "xr2",
            "pad", "inp", "in_sb", "tap", "u", "xp", "bc_hi", "bc_rest", "bc_mid", "bc", "dt", "dtp", "sp_abs",
            "sp_exp", "sp", "dl", "du", "b_row", "c_row", "da", "dbu", "state", "hc", "y_sum", "yy", "yg", "op", "ao",
            "xr3", "kept", "q_sq", "sim_parts", "sim_log", "sim_inv", "sim_prod", "sim", "sim_kept")}
        c_ol = [sem(f"c_ol{c}") for c in range(2)]

        def cols_of(b, c):
            return bass.ds(b * S + c * CH, CH)

        with nc.Block() as block:
            @block.sync
            def _(sp):
                with sp.Fori(0, B) as b:
                    sp.wait_ge(cs["trip_end"], b + 1)
                    for c in range(2):
                        src = scratch_o.rearrange("b g p n -> b p g n")[b, :, :, c * CH:(c + 1) * CH]
                        sp.dma_start(OL[c], src).then_inc(c_ol[c], 16)
                    qkv_store(sp, qs, b * 2 + 1, b)
                for c in range(2):
                    sp.wait_ge(qs["stored"][c], STORED * B)

            @block.tensor
            def _(pe):
                with pe.Fori(0, B) as b:
                    n = b * 2 + 1

                    def lnv(i):
                        return b * (2 * NLN) + 2 * i + 1

                    def ready(s, value):
                        return lambda e, c: e.wait_ge(s, value + c)

                    for c in range(2):
                        pe.wait_ge(c_ol[c], b * 16 + 16)
                        for g in range(H // GH):
                            mm = nc.tensor.matmul(bank(c, 1), w["out_w"][:, g, :], OL[c][:, g, :], start=(g == 0),
                                                  stop=(g == H // GH - 1))
                        mm.then_inc(cs["att"], 1)
                    norm_pe(pe, ln, lnv(0), XA, ready(cs["xa"], n))
                    for c in range(2):
                        pe.wait_ge(cs["ctx"], n + c)
                        nc.tensor.matmul(bank(c, 1), w["w_ctx"][:, :], CTX[c], start=True, stop=True).then_inc(cs["ctxw"], 1)
                    for s in range(STEPS):
                        for c in range(2):
                            if s == 0:
                                pe.wait_ge(ln["affine"], b * 6 + 1 + c)
                            else:
                                pe.wait_ge(cs["xs"], b * (2 * STEPS) + 2 * s - 1 + c)
                            nc.tensor.matmul(bank(c, 2), w["w_x"][:, :], XS[c], start=True, stop=True).then_inc(cs["rec"], 1)
                    norm_pe(pe, ln, lnv(1), XA, ready(cs["xa2"], n))
                    M = FF // P
                    for m in range(M):
                        for c in range(2):
                            if m == 0:
                                pe.wait_ge(ln["affine"], b * 6 + 3 + c)
                            if m >= 2:
                                pe.wait_ge(cs["gelu"], b * (2 * M) + 2 * (m - 2) + c + 1)
                            nc.tensor.matmul(bank(c, 1 + m % 2), w["ff_w1"][:, m * P:(m + 1) * P], NRM[c], start=True,
                                             stop=True).then_inc(cs["ffh"], 1)
                    for m in range(M):
                        for c in range(2):
                            pe.wait_ge(cs["gelu"], b * (2 * M) + 2 * m + c + 1)
                            mm = nc.tensor.matmul(bank(c, 3), w["ff_w2"][:, m, :], HID[c][:, m, :], start=(m == 0),
                                                  stop=(m == M - 1))
                            if m == M - 1:
                                mm.then_inc(cs["ffy"], 1)
                    norm_pe(pe, ln, lnv(2), XA, ready(cs["xa3"], n))
                    norm_pe(pe, ln, lnv(3), XR, ready(cs["xr1"], n))
                    for c in range(2):
                        pe.wait_ge(ln["out"], lnv(3) + c)
                        for t in range(CH // P):
                            mm = nc.tensor.matmul(bank(c, 1)[:, t * E:(t + 1) * E], NRM[c][:, t * P:(t + 1) * P],
                                                  w["Wg"][:, :], start=True, stop=True)
                        mm.then_inc(cs["gates"], 1)
                    for c in range(2):
                        pe.wait_ge(cs["onehot"], n + c)
                        for t in range(CH // P):
                            mm = nc.tensor.matmul(bank(c, 2)[0:E, t * P:(t + 1) * P], gate(c, 3)[:, t, :],
                                                  w["ident"][:, :], start=True, stop=True)
                        mm.then_inc(cs["oh_turned"], 1)
                    for e in range(E):
                        for c in range(2):
                            if e == 0:
                                pe.wait_ge(cs["oh_b"], n + c)
                            else:
                                pe.wait_ge(cs["masked"], b * (2 * E) + 2 * (e - 1) + c + 1)
                            nc.tensor.matmul(bank(c, 0), w["exp_sel"][:, e, :], onehot_b[:, c, :], start=True,
                                             stop=True).then_inc(cs["mask"], 1)
                            for m in range(M):
                                if m >= 2:
                                    pe.wait_ge(cs["relu"], b * (2 * E * M) + (2 * e + c) * M + m - 1)
                                nc.tensor.matmul(bank(c, 1 + m % 2), w["W1"][:, e, m * P:(m + 1) * P], NRM[c],
                                                 start=True, stop=True).then_inc(cs["moe_h"], 1)
                        for c in range(2):
                            if e:
                                pe.wait_ge(cs["moe_y_sb"], b * (2 * E) + 2 * (e - 1) + c + 1)
                            for m in range(M):
                                pe.wait_ge(cs["relu"], b * (2 * E * M) + (2 * e + c) * M + m + 1)
                                mm = nc.tensor.matmul(bank(c, 3), w["W2"][:, e, m, :], HID[c][:, m, :], start=(m == 0),
                                                      stop=(m == M - 1))
                            mm.then_inc(cs["moe_y"], 1)
                    norm_pe(pe, ln, lnv(4), ACC, ready(cs["acc"], b * (2 * (E - 1)) + 2 * (E - 2) + 1))
                    norm_pe(pe, ln, lnv(5), XR, ready(cs["xr2"], n))
                    norm_pe(pe, ln, lnv(6), NRM, ready(ln["out"], lnv(5)))
                    for o in range(2 * CI):
                        for c in range(2):
                            if o == 0:
                                pe.wait_ge(ln["affine"], b * 6 + 5 + c)
                            if o >= 2:
                                pe.wait_ge(cs["in_sb"], b * (4 * CI) + 2 * (o - 2) + c + 1)
                            nc.tensor.matmul(bank(c, 1 + o % 2), w["in_proj_w"][:, o * P:(o + 1) * P], NRM[c], start=True,
                                             stop=True).then_inc(cs["inp"], 1)
                    for c in range(2):
                        pe.wait_ge(cs["u"], b * 4 + 2 * c + 2)
                        at = slice(c * CH, (c + 1) * CH)
                        for i in range(CI):
                            nc.tensor.matmul(bank(c, 1)[0:DR, :], w["x_proj_dt"][:, i, :], U[i][:, at], start=(i == 0),
                                             stop=(i == CI - 1))
                        for i in range(CI):
                            mm = nc.tensor.matmul(bank(c, 2)[0:6 * DS, :], w["x_proj_bc"][:, i, :], U[i][:, at],
                                                  start=(i == 0), stop=(i == CI - 1))
                        mm.then_inc(cs["xp"], 1)
                    for c in range(2):
                        pe.wait_ge(cs["dt"], n + c)
                        for i in range(CI):
                            mm = nc.tensor.matmul(bank(c, 1 + 2 * i), w["dt_proj_w"][:, i * P:(i + 1) * P], DT[c],
                                                  start=True, stop=True)
                        mm.then_inc(cs["dtp"], 1)

                    def row(k, bank0, s):
                        for c in range(2):
                            mm = nc.tensor.matmul(ps[:, bank0 + c, :], w["bc_sel"][:, k, :],
                                                  bc_parts[:, c * CH:(c + 1) * CH], start=True, stop=True)
                        mm.then_inc(s, 1)

                    def add_state(k, i):
                        pe.wait_ge(cs["hc"], b * (DS * CI) + 2 * k + i + 1)
                        for c in range(2):
                            mm = nc.tensor.matmul(ps[:, 4 + 2 * i + c, :], w["ident"][:, :], HC[i][:, c * CH:(c + 1) * CH],
                                                  start=(k == 0), stop=(k == DS - 1))
                        mm.then_inc(cs["y_sum"], 1)

                    pe.wait_ge(cs["bc"], n + 1)
                    pe.wait_ge(cs["du"], b * 4 + 4)
                    row(0, 0, cs["b_row"])
                    row(DS, 2, cs["c_row"])
                    for k in range(DS):
                        if k + 1 < DS:
                            pe.wait_ge(cs["dbu"], b * (DS * CI) + 2 * k + 2)
                            row(k + 1, 0, cs["b_row"])
                        add_state(k, 0)
                        if k + 1 < DS:
                            pe.wait_ge(cs["hc"], b * (DS * CI) + 2 * k + 2)
                            row(DS + k + 1, 2, cs["c_row"])
                        add_state(k, 1)
                    for c in range(2):
                        pe.wait_ge(cs["yg"], b * 4 + 2 * c + 2)
                        for i in range(CI):
                            mm = nc.tensor.matmul(bank(c, 1), w["out_proj_w"][:, i, :], YT[i][:, c * CH:(c + 1) * CH],
                                                  start=(i == 0), stop=(i == CI - 1))
                        mm.then_inc(cs["op"], 1)
                    norm_pe(pe, ln, lnv(7), TT_, ready(cs["ao"], n))
                    norm_pe(pe, ln, lnv(8), XR, ready(cs["xr3"], n))
                    qkv_pe(pe, qs, n, w["qkv2_w"], XN, ready(ln["out"], lnv(8)))
                    for c in range(2):
                        pe.wait_ge(cs["q_sq"], n + c)
                        nc.tensor.matmul(bank(c, 0)[0:H, :], w["head_sel"][:, :], SQ[c], start=True, stop=True)
                        nc.tensor.matmul(bank(c, 1)[0:H, :], q_gate_sel[:, :], QK32[c][:, 0, :], start=True,
                                         stop=True).then_inc(cs["sim_parts"], 1)
                    for c in range(2):
                        pe.wait_ge(cs["sim_prod"], n + c)
                        nc.tensor.matmul(bank(c, 2), w["sim_sum"][:, :], SIM16[c], start=True,
                                         stop=True).then_inc(cs["sim"], 1)

            @block.scalar
            def _(act):
                with act.Fori(0, B) as b:
                    n = b * 2 + 1

                    def lnv(i):
                        return b * (2 * NLN) + 2 * i + 1

                    act.preload_act_table_set("natural_log_exp_and_others")
                    norm_act(act, ln, lnv(0))
                    for c in range(2):
                        act.wait_ge(cs["ctxw"], n + c)
                        nc.scalar.activation(CW[c], bank(c, 1), ACT.Identity, bias=col("b_inl")).then_inc(cs["cw"], 1)
                    for s in range(STEPS):
                        for c in range(2):
                            act.wait_ge(cs["tsum"], b * (2 * STEPS) + 2 * s + c + 1)
                            nc.scalar.activation(TT_[c], TT_[c], ACT.Tanh).then_inc(cs["tanh"], 1)
                    act.preload_act_table_set("natural_log_exp_and_others")
                    norm_act(act, ln, lnv(1))
                    M = FF // P
                    for m in range(M):
                        for c in range(2):
                            act.wait_ge(cs["ffh"], b * (2 * M) + 2 * m + c + 1)
                            nc.scalar.activation(HID[c][:, m, :], bank(c, 1 + m % 2), ACT.Gelu,
                                                 bias=col("ff_b1", m)).then_inc(cs["gelu"], 1)
                    act.preload_act_table_set("natural_log_exp_and_others")
                    norm_act(act, ln, lnv(2))
                    norm_act(act, ln, lnv(3))
                    for e in range(E):
                        for c in range(2):
                            if e:
                                act.wait_ge(cs["moe_y"], b * (2 * E) + 2 * (e - 1) + c + 1)
                            for m in range(M):
                                act.wait_ge(cs["moe_h"], b * (2 * E * M) + (2 * e + c) * M + m + 1)
                                nc.scalar.activation(HID[c][:, m, :], bank(c, 1 + m % 2), ACT.Relu,
                                                     bias=col("moe_b1", e * M + m)).then_inc(cs["relu"], 1)
                        for c in range(2):
                            act.wait_ge(cs["moe_y"], b * (2 * E) + 2 * e + c + 1)
                            if e:
                                act.wait_ge(cs["masked"], b * (2 * E) + 2 * (e - 1) + c + 1)
                            nc.scalar.activation(MOE_Y[c], bank(c, 3), ACT.Identity,
                                                 bias=col("moe_b2", e)).then_inc(cs["moe_y_sb"], 1)
                    for i in (4, 5, 6):
                        norm_act(act, ln, lnv(i))
                    for o in range(2 * CI):
                        for c in range(2):
                            act.wait_ge(cs["inp"], b * (4 * CI) + 2 * o + c + 1)
                            if o < CI:
                                at = KC - 1 + c * CH
                                ins = nc.scalar.copy(CONV[:, o, at:at + CH], bank(c, 1 + o % 2))
                            else:
                                ins = nc.scalar.activation(SZ[o - CI][:, c * CH:(c + 1) * CH], bank(c, 1 + o % 2), ACT.Silu)
                            ins.then_inc(cs["in_sb"], 1)
                    for c in range(2):
                        for i in range(CI):
                            act.wait_ge(cs["tap"], b * 16 + c * 8 + 2 * (KC - 1) + i + 1)
                            nc.scalar.activation(U[i][:, c * CH:(c + 1) * CH], CV[c][i], ACT.Silu).then_inc(cs["u"], 1)
                    act.preload_act_table_set("natural_log_exp_and_others")
                    for c in range(2):
                        act.wait_ge(cs["xp"], n + c)
                        nc.scalar.copy(DT[c], bank(c, 1)[0:DR, :]).then_inc(cs["dt"], 1)
                    for c in range(2):
                        act.wait_ge(cs["dtp"], n + c)
                        for i in range(CI):
                            k = b * 4 + 2 * c + i + 1
                            nc.scalar.activation(SP1[c][i], bank(c, 1 + 2 * i), ACT.Abs,
                                                 bias=col("dt_b", i)).then_inc(cs["sp_abs"], 1)
                            if c:
                                act.wait_ge(cs["dl"], b * 4 + i + 1)
                            nc.scalar.activation(SP2[i], bank(c, 1 + 2 * i), ACT.Relu, bias=col("dt_b", i))
                            act.wait_ge(cs["sp_abs"], k)
                            nc.scalar.activation(SP1[c][i], SP1[c][i], ACT.Exp, scale=-1.0).then_inc(cs["sp_exp"], 1)
                            act.wait_ge(cs["sp_exp"], k)
                            nc.scalar.activation(SP1[c][i], SP1[c][i], ACT.Ln, bias=1.0).then_inc(cs["sp"], 1)
                    act.wait_ge(cs["du"], b * 4 + 4)
                    for k in range(DS):
                        for i in range(CI):
                            if k:
                                act.wait_ge(cs["state"], b * (DS * CI) + 2 * (k - 1) + i + 1)
                            nc.scalar.activation(DA[i], DL[i], ACT.Exp,
                                                 scale=a_neg[:, i * DS + k:i * DS + k + 1]).then_inc(cs["da"], 1)
                    norm_act(act, ln, lnv(7))
                    norm_act(act, ln, lnv(8))
                    qkv_act(act, qs, n, False)
                    for c in range(2):
                        nc.scalar.activation(SQ[c], QK32[c][:, 0, :], ACT.Square).then_inc(cs["q_sq"], 1)
                    for c in range(2):
                        act.wait_ge(cs["sim_parts"], n + c)
                        nc.scalar.activation(RSTD[c][0:H, :], bank(c, 0)[0:H, :], ACT.Ln).then_inc(cs["sim_log"], 1)
                        act.wait_ge(cs["sim_log"], n + c)
                        nc.scalar.activation(RSTD[c][0:H, :], RSTD[c][0:H, :], ACT.Exp, scale=-0.5).then_inc(cs["sim_inv"], 1)

            @block.vector
            def _(dve):
                dve.sem_inc(cs["trip_end"], 1)
                with dve.Fori(0, B) as b:
                    n = b * 2 + 1

                    def lnv(i):
                        return b * (2 * NLN) + 2 * i + 1

                    for c in range(2):
                        dve.wait_ge(cs["att"], n + c)
                        nc.vector.tensor_scalar(CTX[c], bank(c, 1), col("out_b"), None, ALU.add).then_inc(cs["ctx"], 1)
                        dve.wait_ge(cs["ctx"], n + c)
                        nc.vector.tensor_tensor(XA[c], CTX[c], h0[:, cols_of(b, c)], ALU.add).then_inc(cs["xa"], 1)
                    norm_dve(dve, ln, lnv(0), XA, XS, "g1", "b1")
                    for s in range(STEPS):
                        k = b * (2 * STEPS) + 2 * s + 1
                        for c in range(2):
                            dve.wait_ge(cs["rec"], k + c)
                            if s == 0:
                                dve.wait_ge(cs["cw"], n + c)
                            nc.vector.tensor_tensor(TT_[c], bank(c, 2), CW[c], ALU.add).then_inc(cs["tsum"], 1)
                        for c in range(2):
                            dve.wait_ge(cs["tanh"], k + c)
                            dst = TT_[c] if s else GV[c]
                            nc.vector.tensor_tensor(dst, TT_[c], XS[c], ALU.subtract).then_inc(cs["diff"], 1)
                        for c in range(2):
                            dve.wait_ge(cs["diff"], k + c)
                            if s:
                                nc.vector.scalar_tensor_tensor(out=GV[c], in0=GV[c], scalar=0.9, in1=TT_[c], op0=ALU.mult,
                                                               op1=ALU.add).then_inc(cs["vel"], 1)
                        for c in range(2):
                            if s:
                                dve.wait_ge(cs["vel"], b * (2 * STEPS - 2) + 2 * s - 1 + c)
                            nc.vector.scalar_tensor_tensor(out=XS[c], in0=GV[c], scalar=0.01, in1=XS[c], op0=ALU.mult,
                                                           op1=ALU.add).then_inc(cs["xs"], 1)
                    for c in range(2):
                        dve.wait_ge(cs["xs"], b * (2 * STEPS) + 2 * STEPS - 1 + c)
                        nc.vector.tensor_tensor(XA[c], XA[c], XS[c], ALU.add).then_inc(cs["xa2"], 1)
                    norm_dve(dve, ln, lnv(1), XA, NRM, "g2", "b2")
                    for c in range(2):
                        dve.wait_ge(cs["ffy"], n + c)
                        nc.vector.scalar_tensor_tensor(out=XA[c], in0=bank(c, 3), scalar=col("ff_b2"), in1=XA[c],
                                                       op0=ALU.add, op1=ALU.add).then_inc(cs["xa3"], 1)
                    norm_dve(dve, ln, lnv(2), XA, NRM)
                    for c in range(2):
                        dve.wait_ge(ln["out"], lnv(2) + c)
                        nc.vector.tensor_tensor(XR[c], NRM[c], x_res[:, cols_of(b, c)], ALU.add).then_inc(cs["xr1"], 1)
                    norm_dve(dve, ln, lnv(3), XR, NRM)
                    for c in range(2):
                        dve.wait_ge(cs["gates"], n + c)
                        nc.vector.tensor_tensor(small[:, c, 0:32], bank(c, 1)[:, 0:32], w["bg"][:, :],
                                                ALU.add).then_inc(cs["g_sb"], 1)
                        dve.wait_ge(cs["g_sb"], n + c)
                        nc.vector.tensor_reduce(gmax[c], gate(c, 0), AX.X, ALU.max).then_inc(cs["g_max"], 1)
                        dve.wait_ge(cs["g_max"], n + c)
                        for t in range(4):
                            ins = nc.vector.tensor_scalar(gate(c, 1)[:, t, :], gate(c, 0)[:, t, :], gmax[c][:, t:t + 1], None,
                                                          ALU.is_lt)
                        ins.then_inc(cs["g_less"], 1)
                        dve.wait_ge(cs["g_less"], n + c)
                        nc.vector.scalar_tensor_tensor(out=gate(c, 2), in0=gate(c, 1), scalar=float(E), in1=iota[:, :, :],
                                                       op0=ALU.mult, op1=ALU.add).then_inc(cs["g_cand"], 1)
                        dve.wait_ge(cs["g_cand"], n + c)
                        nc.vector.tensor_reduce(gmin[c], gate(c, 2), AX.X, ALU.min).then_inc(cs["g_min"], 1)
                        dve.wait_ge(cs["g_min"], n + c)
                        for t in range(4):
                            ins = nc.vector.tensor_scalar(gate(c, 3)[:, t, :], iota[:, t, :], gmin[c][:, t:t + 1], None,
                                                          ALU.is_equal)
                        ins.then_inc(cs["onehot"], 1)
                    for c in range(2):
                        dve.wait_ge(cs["oh_turned"], n + c)
                        nc.vector.tensor_copy(onehot_b[:, c, :], bank(c, 2)[0:E, :]).then_inc(cs["oh_b"], 1)
                    for e in range(E):
                        for c in range(2):
                            k = b * (2 * E) + 2 * e + c + 1
                            dve.wait_ge(cs["moe_y_sb"], k)
                            dve.wait_ge(cs["mask"], k)
                            dst = TT_[c] if e else ACC[c]
                            nc.vector.tensor_tensor(dst, MOE_Y[c], bank(c, 0), ALU.mult).then_inc(cs["masked"], 1)
                            if e:
                                dve.wait_ge(cs["masked"], k)
                                nc.vector.tensor_tensor(ACC[c], ACC[c], TT_[c], ALU.add).then_inc(cs["acc"], 1)
                    norm_dve(dve, ln, lnv(4), ACC, NRM)
                    for c in range(2):
                        dve.wait_ge(ln["out"], lnv(4) + c)
                        nc.vector.tensor_tensor(XR[c], XR[c], NRM[c], ALU.add).then_inc(cs["xr2"], 1)
                    norm_dve(dve, ln, lnv(5), XR, NRM)
                    norm_dve(dve, ln, lnv(6), NRM, NRM, "norm_w", "norm_b")
                    nc.vector.memset(CONV[:, :, 0:KC - 1], 0.0).then_inc(cs["pad"], 1)
                    dve.wait_ge(cs["pad"], b + 1)
                    for c in range(2):
                        for tap in range(KC):
                            for i in range(CI):
                                k = b * 16 + c * 8 + 2 * tap + i + 1
                                src = CONV[:, i, c * CH + tap:c * CH + tap + CH]
                                if tap == 0:
                                    dve.wait_ge(cs["in_sb"], b * (4 * CI) + 2 * i + c + 1)
                                    ins = nc.vector.tensor_scalar(CV[c][i], src, col("conv_w", i * KC), col("conv_b", i),
                                                                  ALU.mult, ALU.add)
                                else:
                                    dve.wait_ge(cs["tap"], k - 2)
                                    ins = nc.vector.scalar_tensor_tensor(out=CV[c][i], in0=src, scalar=col("conv_w", i * KC + tap),
                                                                         in1=CV[c][i], op0=ALU.mult, op1=ALU.add)
                                ins.then_inc(cs["tap"], 1)
                    for c in range(2):
                        dve.wait_ge(cs["xp"], n + c)
                        rows = slice(0, 6 * DS)
                        nc.vector.tensor_copy(B_HI[c], bank(c, 2)[rows, :]).then_inc(cs["bc_hi"], 1)
                        dve.wait_ge(cs["bc_hi"], n + c)
                        nc.vector.scalar_tensor_tensor(out=B_REST[c], in0=B_HI[c], scalar=col("part12")[rows, :],
                                                       in1=bank(c, 2)[rows, :], op0=ALU.mult, op1=ALU.add).then_inc(cs["bc_rest"], 1)
                        dve.wait_ge(cs["bc_rest"], n + c)
                        nc.vector.tensor_copy(B_MID[c], B_REST[c]).then_inc(cs["bc_mid"], 1)
                        dve.wait_ge(cs["bc_mid"], n + c)
                        nc.vector.scalar_tensor_tensor(out=bc_parts[:, c * CH:(c + 1) * CH], in0=B_MID[c],
                                                       scalar=col("part2")[rows, :], in1=B_REST[c], op0=ALU.mult,
                                                       op1=ALU.add).then_inc(cs["bc"], 1)
                    for c in range(2):
                        at = slice(c * CH, (c + 1) * CH)
                        for i in range(CI):
                            k = b * 4 + 2 * c + i + 1
                            dve.wait_ge(cs["sp"], k)
                            nc.vector.tensor_tensor(DL[i][:, at], SP1[c][i], SP2[i], ALU.add).then_inc(cs["dl"], 1)
                            dve.wait_ge(cs["dl"], k)
                            nc.vector.tensor_tensor(DU[i][:, at], DL[i][:, at], U[i][:, at], ALU.mult).then_inc(cs["du"], 1)
                    b_rows = ps[:, 0:2, :].rearrange("p a n -> p (a n)")
                    c_rows = ps[:, 2:4, :].rearrange("p a n -> p (a n)")
                    for k in range(DS):
                        at = b * (DS * CI) + 2 * k + 1
                        for i in range(CI):
                            if k == 0:
                                dve.wait_ge(cs["du"], b * 4 + 4)
                            dve.wait_ge(cs["b_row"], b * DS + k + 1)
                            nc.vector.tensor_tensor(DBU[i], DU[i], b_rows, ALU.mult).then_inc(cs["dbu"], 1)
                        for i in range(CI):
                            dve.wait_ge(cs["da"], at + i)
                            dve.wait_ge(cs["dbu"], at + i)
                            nc.vector.tensor_tensor_scan(HS[i], DA[i], DBU[i], 0.0, ALU.mult, ALU.add).then_inc(cs["state"], 1)
                        for i in range(CI):
                            dve.wait_ge(cs["c_row"], b * DS + k + 1)
                            dve.wait_ge(cs["state"], at + i)
                            if k:
                                dve.wait_ge(cs["y_sum"], at - 2 + i)
                            nc.vector.tensor_tensor(HC[i], HS[i], c_rows, ALU.mult).then_inc(cs["hc"], 1)
                    dve.wait_ge(cs["y_sum"], b * (DS * CI) + DS * CI)
                    for c in range(2):
                        at = slice(c * CH, (c + 1) * CH)
                        for i in range(CI):
                            nc.vector.scalar_tensor_tensor(out=YT[i][:, at], in0=U[i][:, at], scalar=col("D_param", i),
                                                           in1=ps[:, 4 + 2 * i + c, :], op0=ALU.mult,
                                                           op1=ALU.add).then_inc(cs["yy"], 1)
                        for i in range(CI):
                            dve.wait_ge(cs["yy"], b * 4 + 2 * c + i + 1)
                            nc.vector.tensor_tensor(YT[i][:, at], YT[i][:, at], SZ[i][:, at], ALU.mult).then_inc(cs["yg"], 1)
                    for c in range(2):
                        dve.wait_ge(cs["op"], n + c)
                        nc.vector.tensor_copy(TT_[c], bank(c, 1)).then_inc(cs["ao"], 1)
                    norm_dve(dve, ln, lnv(7), TT_, NRM)
                    for c in range(2):
                        dve.wait_ge(ln["out"], lnv(7) + c)
                        nc.vector.tensor_tensor(XR[c], XR[c], NRM[c], ALU.add).then_inc(cs["xr3"], 1)
                    norm_dve(dve, ln, lnv(8), XR, XN)
                    qkv_dve(dve, qs, n, b, False)
                    for c in range(2):
                        dve.wait_ge(cs["sim_inv"], n + c)
                        nc.vector.tensor_tensor(SIM16[c], bank(c, 1)[0:H, :], RSTD[c][0:H, :], ALU.mult).then_inc(cs["sim_prod"], 1)
                    for c in range(2):
                        dve.wait_ge(cs["sim"], n + c)
                        nc.vector.tensor_scalar(h0[:, cols_of(b, c)], bank(c, 2), 1.0, None, ALU.mult).then_inc(cs["sim_kept"], 1)
                    dve.wait_ge(cs["kept"], n + 1)
                    for c in range(2):
                        dve.wait_ge(qs["stored"][c], b * STORED + STORED)
                    dve.sem_inc(cs["trip_end"], 1)

            @block.gpsimd
            def _(pool):
                with pool.Fori(0, B) as b:
                    for c in range(2):
                        pool.wait_ge(cs["xr3"], b * 2 + c + 1)
                        nc.gpsimd.tensor_copy(x_res[:, cols_of(b, c)], XR[c]).then_inc(cs["kept"], 1)

        end_phase()

        d_chain, d_rows, d_stored = sem("d_chain"), sem("d_rows"), sem("d_stored")
        lim = small[:, 0, 0:4]
        rows_bf = [work[:, 2 * k:2 * k + 2, :].rearrange("p a n -> p (a n)").bitcast(BF16) for k in range(4)]
        with nc.Block() as block:
            @block.vector
            def _(dve):
                count = [0]

                def link(ins):
                    count[0] += 1
                    ins.then_inc(d_chain, 1)
                    dve.wait_ge(d_chain, count[0])

                sims = h0[:, :].rearrange("p (b n) -> p b n", b=B)
                link(nc.vector.tensor_reduce(lim[:, 0:1], sims[:, :, REG:S], AX.XY, ALU.min))
                link(nc.vector.tensor_reduce(lim[:, 1:2], sims[:, :, REG:S], AX.XY, ALU.max))
                link(nc.vector.tensor_tensor(lim[:, 2:3], lim[:, 1:2], lim[:, 0:1], ALU.subtract))
                link(nc.vector.reciprocal(lim[:, 3:4], lim[:, 2:3]))
                link(nc.vector.tensor_scalar(h0[:, :], h0[:, :], lim[:, 0:1], lim[:, 3:4], ALU.subtract, ALU.mult))
                link(nc.vector.tensor_scalar(h0[:, :], h0[:, :], 0.9, None, ALU.is_gt))
                for k, (mul, add, reg) in enumerate(((1.0, 0.0, 1.0), (-1.0, 1.0, 0.0), (-NEG, NEG, 0.0), (NEG, 0.0, 0.0))):
                    link(nc.vector.tensor_scalar(rows_bf[k][0:H, :], h0[0:H, :], mul, add, ALU.mult, ALU.add))
                    nc.vector.memset(rows_bf[k][0:H, :].rearrange("p (b n) -> p b n", b=B)[:, :, 0:REG],
                                     reg).then_inc(d_rows, 1)

            @block.sync
            def _(sp):
                sp.wait_ge(d_rows, 4)
                for k, (dram, row) in enumerate(((scratch_q, R_MASK), (scratch_q, R_MASK + 1), (scratch_k, R_MASK),
                                                 (scratch_k, R_MASK + 1))):
                    for b in range(B):
                        sp.dma_start(dram[b * H:(b + 1) * H, row, :], rows_bf[k][0:H, b * S:(b + 1) * S]).then_inc(d_stored, 16)
                sp.wait_ge(d_stored, 16 * 4 * B)

        end_phase()
        run_attention("e", False)
        end_phase()

        fs = {k: sem("f_" + k) for k in ("reg_sum", "reg", "proj", "ao", "xr", "turned", "y_sb", "trip_end")}
        f_norm = norm_sems("f_norm")
        f_ol = [sem(f"f_ol{c}") for c in range(2)]
        f_out = [sem(f"f_out{c}") for c in range(2)]
        f_ox = sem("f_ox")
        OX = work[:, 19, 0:4 * XQ].rearrange("p (g n) -> p g n", g=4)
        YO = [work[:, 20, c * CH:(c + 1) * CH] for c in range(2)]
        out_rows = out.rearrange("b (t p) f -> (b t) p f", p=P)
        with nc.Block() as block:
            @block.sync
            def _(sp):
                with sp.Fori(0, B) as b:
                    sp.wait_ge(fs["trip_end"], b + 1)
                    sp.dma_start(OX, scratch_x.rearrange("b g p n -> b p g n")[b, :, :, :]).then_inc(f_ox, 16)
                    for c in range(2):
                        src = scratch_o.rearrange("b g p n -> b p g n")[b, :, :, c * CH:(c + 1) * CH]
                        sp.dma_start(OL[c], src).then_inc(f_ol[c], 16)
                    for c in range(2):
                        sp.wait_ge(fs["y_sb"], b * 2 + c + 1)
                        sp.dma_start(out_rows[bass.ds(b * QT + 4 * c, 4), :, :].rearrange("t p f -> p t f"),
                                     YO[c].rearrange("p (t f) -> p t f", t=4)).then_inc(f_out[c], 16)
                for c in range(2):
                    sp.wait_ge(f_out[c], 16 * B)

            @block.tensor
            def _(pe):
                with pe.Fori(0, B) as b:
                    n = b * 2 + 1
                    for c in range(2):
                        pe.wait_ge(f_ol[c], b * 16 + 16)
                        if c == 0:
                            pe.wait_ge(fs["reg"], b + 1)
                        for g in range(H // GH):
                            mm = nc.tensor.matmul(bank(c, 1), w["proj_w"][:, g, :], OL[c][:, g, :], start=(g == 0),
                                                  stop=(g == H // GH - 1))
                        mm.then_inc(fs["proj"], 1)
                    norm_pe(pe, f_norm, n, XA, lambda e, c: e.wait_ge(fs["ao"], n + c))
                    for c in range(2):
                        pe.wait_ge(fs["xr"], n + c)
                        for t in range(CH // P):
                            mm = nc.tensor.transpose(bank(c, 2)[:, t * P:(t + 1) * P], XR[c][:, t * P:(t + 1) * P],
                                                     w["ident"][:, :])
                        mm.then_inc(fs["turned"], 1)

            @block.scalar
            def _(act):
                act.preload_act_table_set("natural_log_exp_and_others")
                with act.Fori(0, B) as b:
                    norm_act(act, f_norm, b * 2 + 1)
                    for c in range(2):
                        act.wait_ge(fs["turned"], b * 2 + c + 1)
                        nc.scalar.copy(YO[c], bank(c, 2)).then_inc(fs["y_sb"], 1)

            @block.vector
            def _(dve):
                dve.sem_inc(fs["trip_end"], 1)
                with dve.Fori(0, B) as b:
                    n = b * 2 + 1
                    dve.wait_ge(f_ol[0], b * 16 + 16)
                    dve.wait_ge(f_ox, b * 16 + 16)
                    nc.vector.tensor_tensor(OX[:, :, 0:REG], OX[:, :, 0:REG], OL[0][:, :, 0:REG], ALU.add).then_inc(fs["reg_sum"], 1)
                    dve.wait_ge(fs["reg_sum"], b + 1)
                    nc.vector.tensor_scalar(OL[0][:, :, 0:REG], OX[:, :, 0:REG], 0.5, None, ALU.mult).then_inc(fs["reg"], 1)
                    for c in range(2):
                        dve.wait_ge(fs["proj"], n + c)
                        nc.vector.tensor_scalar(XA[c], bank(c, 1), col("proj_b"), None, ALU.add).then_inc(fs["ao"], 1)
                    norm_dve(dve, f_norm, n, XA, NRM)
                    for c in range(2):
                        dve.wait_ge(f_norm["out"], n + c)
                        nc.vector.tensor_tensor(XR[c], NRM[c], x_res[:, cols_of(b, c)], ALU.add).then_inc(fs["xr"], 1)
                    for c in range(2):
                        dve.wait_ge(f_out[c], b * 16 + 16)
                    dve.sem_inc(fs["trip_end"], 1)

def kernel(**inputs):
    import numpy as np
    import concourse.bacc as _bacc
    from concourse.bass_utils import run_bass_kernel_spmd as _run

    x = {k: np.asarray(v) for k, v in inputs.items()}
    f32, bf16 = np.float32, mybir.dt.np(BF16)

    def vec(v):
        return v.reshape(-1, P).T

    def padded_heads(weight):
        m = np.zeros((H // GH, GH, 32, weight.shape[1]), f32)
        m[:, :, 0:HD] = weight.reshape(H // GH, GH, HD, -1)
        return np.ascontiguousarray(m.reshape(H // GH, P, -1).transpose(1, 0, 2))

    rows = np.arange(6 * DS)
    part = lambda n: np.pad((rows >= n * 2 * DS).astype(f32), (0, P - 6 * DS)).reshape(1, P)
    columns = {
        "q_b": vec(x["L0_attn_qkv_b"][0:D]), "k_b": vec(x["L0_attn_qkv_b"][D:2 * D]), "out_b": vec(x["L0_attn_out_b"]),
        "g_attn": vec(x["L0_attn_g_attn"]), "b_attn": vec(x["L0_attn_b_attn"]), "g1": vec(x["L0_attn_g1"]),
        "b1": vec(x["L0_attn_b1"]), "g2": vec(x["L0_attn_g2"]), "b2": vec(x["L0_attn_b2"]),
        "b_inl": vec(x["L0_attn_b_inl"]), "ff_b1": vec(x["L0_attn_ff_b1"]), "ff_b2": vec(x["L0_attn_ff_b2"]),
        "moe_b1": vec(x["L0_ffn_b1"]), "moe_b2": vec(x["L0_ffn_b2"]), "norm_w": vec(x["L1_attn_norm_w"]),
        "norm_b": vec(x["L1_attn_norm_b"]),
        "conv_w": x["L1_attn_conv_w"].reshape(CI, P, KC).transpose(1, 0, 2).reshape(P, -1),
        "conv_b": vec(x["L1_attn_conv_b"]), "dt_b": vec(x["L1_attn_dt_proj_b"]),
        "A_log": x["L1_attn_A_log"].reshape(CI, P, DS).transpose(1, 0, 2).reshape(P, -1),
        "D_param": vec(x["L1_attn_D_param"]), "q_gate": vec(x["L1_ffn_g_info"][0, 0]), "proj_b": vec(x["L1_ffn_b_proj"]),
        "part12": -part(1).T, "part2": -part(2).T,
    }
    for name, (_, n) in COLS.items():
        assert columns[name].shape == (P, n), name
    eye = np.eye(P, dtype=f32)
    q = np.arange(P)
    head = (q[:, None] // HD == np.arange(H)[None, :]).astype(f32)
    den = np.zeros((P, P), f32)
    den[q // 32 * 32 + HD, q] = 1.0
    bc = x["L1_attn_x_proj_w"][:, DR:].reshape(CI, P, 2 * DS).transpose(1, 0, 2)
    arrays = {
        "x": x["L0_attn_x"].reshape(B * QT, P, D),
        "cols": np.concatenate([columns[name] for name in COLS], axis=1),
        "qkv_w": x["L0_attn_qkv_w"], "v_bias": np.tile(x["L0_attn_qkv_b"][2 * D:], (P, CH // D)),
        "out_w": padded_heads(x["L0_attn_out_w"]), "w_ctx": x["L0_attn_w_ctx"], "w_x": x["L0_attn_w_x"],
        "ff_w1": x["L0_attn_ff_w1"], "ff_w2": x["L0_attn_ff_w2"].reshape(FF // P, P, D).transpose(1, 0, 2),
        "Wg": x["L0_ffn_Wg"], "bg": np.tile(x["L0_ffn_bg"], (P, CH // P)), "W1": x["L0_ffn_W1"].transpose(1, 0, 2),
        "W2": x["L0_ffn_W2"].reshape(E, FF // P, P, D).transpose(2, 0, 1, 3), "in_proj_w": x["L1_attn_in_proj_w"],
        "x_proj_dt": x["L1_attn_x_proj_w"][:, 0:DR].reshape(CI, P, DR).transpose(1, 0, 2),
        "x_proj_bc": np.concatenate([bc, bc, bc], axis=2), "dt_proj_w": x["L1_attn_dt_proj_w"],
        "out_proj_w": x["L1_attn_out_proj_w"].reshape(CI, P, D).transpose(1, 0, 2),
        "qkv2_w": x["L1_ffn_W_qkv"], "proj_w": padded_heads(x["L1_ffn_W_proj"]),
        "ident": eye, "mean_w": np.full((P, P), 1.0 / D, f32), "den_sel": den, "head_sel": head, "head_back": head.T,
        "sim_sum": np.full((H, P), 1.0 / H, f32), "iota": np.broadcast_to(np.arange(E, dtype=f32), (P, CH // P, E)),
        "ident_b": eye.astype(bf16), "mask_qk": np.where(q[None, :] > q[:, None], NEG, 0.0).astype(bf16),
        "mask_kq": np.where(q[:, None] > q[None, :], NEG, 0.0).astype(bf16),
        "exp_sel": np.repeat(np.eye(E, dtype=f32)[:, :, None], P, axis=2).astype(bf16),
        "bc_sel": np.repeat((rows[:, None] % (2 * DS) == np.arange(2 * DS)[None, :])[:, :, None], P, axis=2).astype(bf16),
        "x_rows": np.repeat(np.array([[0.0], [1.0]], f32), XQ, axis=1).astype(bf16),
    }
    arrays = {k: np.ascontiguousarray(v) for k, v in arrays.items()}
    nc = _bacc.Bacc("TRN2", target_bir_lowering=False, num_devices=1)
    handles = {k: nc.dram_tensor(f"in_{k}", v.shape, mybir.dt.from_np(v.dtype), kind="ExternalInput").ap()
               for k, v in arrays.items()}
    out = nc.dram_tensor("out_0", (B, S, D), F32, kind="ExternalOutput").ap()
    build(nc, handles, out)
    r = _run(nc, [{f"in_{k}": v for k, v in arrays.items()}], core_ids=[0])
    return r.results[0]["out_0"]
```

```python
from contextlib import ExitStack

import concourse.bass as bass
from concourse import mybir

F32 = mybir.dt.float32
BF16 = mybir.dt.bfloat16
ALU = mybir.AluOpType
ACT = mybir.ActivationFunctionType
AX = mybir.AxisListType

P = 128
B, S, D = 4, 1024, 128
CH = 512
H, HD = 16, 8
SCALE = float(HD) ** -0.5
GH = 4
GROUPS = B * H // GH
SLOTS_Q = (0, 0, 0, 1, 1, 2)
SLOTS_K = (0, 1, 2, 0, 1, 0)
NS = len(SLOTS_Q)
R_MASK = NS * HD
HR = R_MASK + 2
R_MAX = 2 * HR
R_END = R_MAX + 3
NEG = -1.0e30
QT = S // P
REG = 5
XQ = 32
FF = 512
E = 8
DI, DS, DR, KC = 256, 16, 64, 4
CI = DI // P
STEPS = 8
EPS = 1e-5

COLS = {}
for _name, _n in (("q_b", 1), ("k_b", 1), ("out_b", 1), ("g_attn", 1), ("b_attn", 1), ("g1", 1), ("b1", 1),
                  ("g2", 1), ("b2", 1), ("b_inl", 1), ("ff_b1", FF // P), ("ff_b2", 1), ("moe_b1", E * FF // P),
                  ("moe_b2", E), ("norm_w", 1), ("norm_b", 1), ("conv_w", CI * KC), ("conv_b", CI), ("dt_b", CI),
                  ("A_log", CI * DS), ("D_param", CI), ("q_gate", 1), ("proj_b", 1), ("part12", 1), ("part2", 1)):
    COLS[_name] = (sum(n for _, n in COLS.values()), _n)
NCOLS = sum(n for _, n in COLS.values())


def build(nc, a, out):
    scratch_q = nc.dram_tensor("scratch_q", [B * H, HR, S], BF16).ap()
    scratch_k = nc.dram_tensor("scratch_k", [B * H, HR, S], BF16).ap()
    scratch_o = nc.dram_tensor("scratch_o", [B, H // GH, P, S], F32).ap()
    scratch_x = nc.dram_tensor("scratch_x", [B, H // GH, P, XQ], F32).ap()

    with ExitStack() as ctx:
        def sb(name, shape, dt=F32):
            return ctx.enter_context(nc.sbuf_tensor(name, shape, dt))

        phase_sems = []

        def sem(name):
            phase_sems.append(nc.alloc_semaphore(name))
            return phase_sems[-1]

        def end_phase():
            nc.clear_and_free_semaphores(phase_sems)
            phase_sems.clear()
            nc.all_engine_barrier()

        x_res = sb("x_res", [P, B * S])
        h0 = sb("h0", [P, B * S])
        v_tok = sb("v_tok", [P, B * QT * D])
        w = {}
        for name, shape, dt in (
                ("cols", [P, NCOLS], F32), ("qkv_w", [P, 3 * D], F32), ("v_bias", [P, CH], F32),
                ("out_w", [P, H // GH, D], F32), ("w_ctx", [P, D], F32), ("w_x", [P, D], F32),
                ("ff_w1", [P, FF], F32), ("ff_w2", [P, FF // P, D], F32), ("Wg", [P, E], F32), ("bg", [P, CH // P * E], F32),
                ("W1", [P, E, FF], F32), ("W2", [P, E, FF // P, D], F32), ("in_proj_w", [P, 2 * DI], F32),
                ("x_proj_dt", [P, CI, DR], F32), ("x_proj_bc", [P, CI, 3 * 2 * DS], F32), ("dt_proj_w", [DR, DI], F32),
                ("out_proj_w", [P, CI, D], F32), ("qkv2_w", [P, 3 * D], F32), ("proj_w", [P, H // GH, D], F32),
                ("ident", [P, P], F32), ("mean_w", [P, P], F32), ("den_sel", [P, P], F32),
                ("head_sel", [P, H], F32), ("head_back", [H, P], F32), ("sim_sum", [H, P], F32), ("iota", [P, CH // P, E], F32),
                ("ident_b", [P, P], BF16), ("mask_qk", [P, P], BF16), ("mask_kq", [P, P], BF16),
                ("exp_sel", [E, E, P], BF16), ("bc_sel", [6 * DS, 2 * DS, P], BF16)):
            w[name] = sb("w_" + name, shape, dt)

        def col(name, i=0):
            at = COLS[name][0] + i
            return w["cols"][:, at:at + 1]

        eps_col = sb("eps_col", [P, 2])
        a_neg = sb("a_neg", [P, CI * DS])
        q_gate_sel = sb("q_gate_sel", [P, H])
        gate_tmp = sb("gate_tmp", [P, 4])
        bc_parts = sb("bc_parts", [6 * DS, S], BF16)
        m_cat = sb("m_cat", [P, 2, 40])
        m_col = sb("m_col", [P, P])
        m_neg = sb("m_neg", [40, 2, P])
        m_parts = sb("m_parts", [40, 3, 3, P], BF16)
        small = sb("small", [P, 2, 160])
        onehot_b = sb("onehot_b", [E, 2, CH], BF16)
        NWK = 21
        work = sb("work", [P, NWK, S])

        ps = ctx.enter_context(nc.psum_tensor("ps", [P, 8, CH], F32))

        def chunks(slot):
            return [work[:, slot, c * CH:(c + 1) * CH] for c in range(2)]

        def bank(c, i):
            return ps[:, 4 * c + i, :]

        XR, DEV, SQ, RSTD, NRM = (chunks(i) for i in range(5))
        CTX, XA, XS, CW, GV, TT_ = (chunks(i) for i in range(5, 11))
        OL = [work[:, 15 + 2 * c:17 + 2 * c, :].rearrange("p a n -> p (a n)").rearrange("p (g n) -> p g n", g=4)
              for c in range(2)]
        HID = [work[:, 15 + 2 * c:17 + 2 * c, :].rearrange("p a n -> p (a n)").rearrange("p (m n) -> p m n", m=4)
               for c in range(2)]
        XIN = [work[:, 12, c * CH:(c + 1) * CH].rearrange("p (t f) -> p t f", t=4) for c in range(2)]
        QK32 = [work[:, 5 + c, :].rearrange("p (a n) -> p a n", a=2) for c in range(2)]
        REST = [work[:, 7 + c, :].rearrange("p (a n) -> p a n", a=2) for c in range(2)]
        PARTS = [work[:, 9:12, :].rearrange("p a n -> p (a n)")[:, 1536 * c:1536 * (c + 1)].bitcast(BF16)
                 .rearrange("p (t a n) -> p t a n", t=3, a=2) for c in range(2)]
        MOE_Y, ACC = chunks(5), chunks(6)
        XN = chunks(13)
        CONV = work[:, 17:20, :].rearrange("p a n -> p (a n)")[:, 0:CI * (KC - 1 + S)].rearrange("p (i n) -> p i n", i=CI)

        def norm_sems(tag):
            return {k: sem(f"{tag}_{k}") for k in ("mean", "centred", "squared", "var", "log", "rstd", "out", "affine")}

        def norm_pe(pe, s, n, src, ready):
            for c in range(2):
                ready(pe, c)
                nc.tensor.matmul(bank(c, 0), w["mean_w"][:, :], src[c], start=True, stop=True).then_inc(s["mean"], 1)
            for c in range(2):
                pe.wait_ge(s["squared"], n + c)
                nc.tensor.matmul(bank(c, 0), w["mean_w"][:, :], SQ[c], start=True, stop=True).then_inc(s["var"], 1)

        def norm_act(act, s, n, twice=False, both=None):
            for c in range(2):
                act.wait_ge(s["centred"], n + c)
                nc.scalar.activation(SQ[c], DEV[c], ACT.Square).then_inc(s["squared"], 1)
            for c in range(2):
                act.wait_ge(s["var"], n + c)
                if both:
                    nc.scalar.activation(both[c], bank(c, 0), ACT.Ln, bias=eps_col[:, 1:2],
                                         scale=1.0 + EPS).then_inc(s["log2"], 1)
                    act.wait_ge(s["log2"], n + c)
                    nc.scalar.activation(both[c], both[c], ACT.Exp, scale=-0.5).then_inc(s["rstd2"], 1)
                bias, scale = (eps_col[:, 1:2], 1.0 + EPS) if twice else (eps_col[:, 0:1], 1.0)
                nc.scalar.activation(RSTD[c], bank(c, 0), ACT.Ln, bias=bias, scale=scale).then_inc(s["log"], 1)
                act.wait_ge(s["log"], n + c)
                nc.scalar.activation(RSTD[c], RSTD[c], ACT.Exp, scale=-0.5).then_inc(s["rstd"], 1)

        def norm_dve(dve, s, n, src, dst, gain=None, shift=None, n_affine=None):
            for c in range(2):
                dve.wait_ge(s["mean"], n + c)
                nc.vector.tensor_tensor(DEV[c], src[c], bank(c, 0), ALU.subtract).then_inc(s["centred"], 1)
            for c in range(2):
                dve.wait_ge(s["rstd"], n + c)
                nc.vector.tensor_tensor(dst[c], DEV[c], RSTD[c], ALU.mult).then_inc(s["out"], 1)
                if gain:
                    dve.wait_ge(s["out"], n + c)
                    nc.vector.tensor_scalar(dst[c], dst[c], col(gain), col(shift), ALU.mult,
                                            ALU.add).then_inc(s["affine"], 1)

        def qkv_sems(tag):
            d = {k: sem(f"{tag}_{k}") for k in ("qk", "v", "qk_sb", "part1", "rest", "part2", "part3", "v_kept")}
            d["stored"] = [sem(f"{tag}_stored{c}") for c in range(2)]
            return d

        def qkv_pe(pe, s, n, weights, src, ready):
            for c in range(2):
                ready(pe, c)
                for i in range(2):
                    mm = nc.tensor.matmul(bank(c, 1 + i), weights[:, i * D:(i + 1) * D], src[c], start=True, stop=True)
                mm.then_inc(s["qk"], 1)
                for t in range(CH // P):
                    mm = nc.tensor.matmul(ps[:, 4 * c + 3, t * P:(t + 1) * P], src[c][:, t * P:(t + 1) * P],
                                          weights[:, 2 * D:3 * D], start=True, stop=True)
                mm.then_inc(s["v"], 1)

        def qkv_act(act, s, n, biased):
            for c in range(2):
                act.wait_ge(s["qk"], n + c)
                for i, name in enumerate(("q_b", "k_b")):
                    bias = col(name) if biased else 0.0
                    nc.scalar.activation(QK32[c][:, i, :], bank(c, 1 + i), ACT.Identity,
                                         bias=bias).then_inc(s["qk_sb"], 1)
                act.wait_ge(s["qk_sb"], 2 * (n + c))
                nc.scalar.copy(PARTS[c][:, 0, :, :], QK32[c]).then_inc(s["part1"], 1)
            for c in range(2):
                act.wait_ge(s["rest"], n + c)
                nc.scalar.copy(PARTS[c][:, 1, :, :], REST[c]).then_inc(s["part2"], 1)

        def qkv_dve(dve, s, n, b, biased):
            for c in range(2):
                dve.wait_ge(s["v"], n + c)
                dst = v_tok[:, bass.ds(b * S, S)].rearrange("p (g k f) -> p g k f", g=H // GH, k=QT)[:, :, 4 * c:4 * c + 4, :]
                src = bank(c, 3).rearrange("p (k g f) -> p g k f", k=4, g=H // GH)
                if biased:
                    shift = w["v_bias"][:, :].rearrange("p (k g f) -> p g k f", k=4, g=H // GH)
                    ins = nc.vector.tensor_tensor(dst, src, shift, ALU.add)
                else:
                    ins = nc.vector.tensor_scalar(dst, src, 1.0, None, ALU.mult)
                ins.then_inc(s["v_kept"], 1)
                dve.wait_ge(s["part1"], n + c)
                nc.vector.tensor_tensor(REST[c], QK32[c], PARTS[c][:, 0, :, :], ALU.subtract).then_inc(s["rest"], 1)
            for c in range(2):
                dve.wait_ge(s["part2"], n + c)
                nc.vector.tensor_tensor(PARTS[c][:, 2, :, :], REST[c], PARTS[c][:, 1, :, :],
                                        ALU.subtract).then_inc(s["part3"], 1)

        def qkv_store(sp, s, n, b):
            for c in range(2):
                sp.wait_ge(s["part3"], n + c)
                for i, (dram, slots) in enumerate(((scratch_q, SLOTS_Q), (scratch_k, SLOTS_K))):
                    for k, part in enumerate(slots):
                        sp.dma_start(dram[bass.ds(b * H, H), k * HD:(k + 1) * HD, c * CH:(c + 1) * CH],
                                     PARTS[c][:, part, i, :]).then_inc(s["stored"][c], 16)

        STORED = 2 * NS * 16

        NB = 3
        QW = GH * S + GH * XQ
        flat = work[:, :, :].rearrange("p a n -> p (a n)")
        QF = [flat[:, i * (QW // 2):(i + 1) * (QW // 2)].bitcast(BF16) for i in range(NB)]
        KP = [work[:, 7 + i, :].bitcast(BF16).rearrange("p (r n) -> p r n", r=2) for i in range(NB)]
        VP = [work[:, 10 + i, :].rearrange("p (k j d) -> p k j d", k=QT, j=GH) for i in range(NB)]
        EB = [work[:, 13 + i, :].rearrange("p (a n) -> p a n", a=2) for i in range(4)]
        OS, RD, ONT = chunks(17), chunks(18), chunks(19)
        SX = work[:, 20, 0:3 * XQ].rearrange("p (a n) -> p a n", a=3)
        SA = [ps[:, i, :] for i in range(2)]
        SB = [ps[:, 2 + 2 * i:4 + 2 * i, :] for i in range(2)]
        OB = [ps[:, 6 + i, :] for i in range(2)]
        assert 2 * S * 7 >= NB * QW

        def q_cols(p, j, at, n):
            return QF[p][:, j * S + at:j * S + at + n]

        def x_cols(p, j):
            return QF[p][:, GH * S + j * XQ:GH * S + (j + 1) * XQ]

        def attention(tag, causal):
            NX = 0 if causal else 1
            s1 = []
            for j in range(GH):
                for qt in range(QT):
                    for half in range(2):
                        width = min(CH, P * (qt + 1) - CH * half) if causal else CH
                        if width > 0:
                            s1.append((j, qt, half, width, causal and width == P * (qt + 1) - CH * half))
            for half in range(2 * NX):
                s1.append(("x", None, half, CH, False))
            NU = len(s1)
            assert NU % 2 == 0
            s2 = []
            for qh in range(2):
                for kc in range(QT):
                    for pr in range(2):
                        off = max(0, P * kc - CH * qh) if causal else 0
                        if off < CH:
                            s2.append((qh, kc, pr, off, causal and P * kc >= CH * qh))
            lastk = [max(u[1] for u in s2 if u[0] == qh) for qh in range(2)]
            ends = [max(i for i, u in enumerate(s2) if u[0] == 0)]
            if NX:
                ends.append(ends[0] + 8)
                s2.insert(ends[1], ("x", None, None, 0, False))
            NV = len(s2)
            ends.append(NV - 1)
            NO = len(ends)
            BACK = 7
            AHEAD = 2 * (NU * BACK // NV // 2)
            plan = [[] for _ in range(2 * NV)]
            items = [(1, u) for u in range(AHEAD, NU)] + [None, (1, NU), None] + [(2, u) for u in range(AHEAD)]
            for n, item in enumerate(items):
                if item:
                    plan[n * 2 * NV // len(items)].append(item)

            sems = {k: sem(f"{tag}_{k}") for k in (
                "scores1", "scores1_read", "max", "m_ready", "m_turned", "m_chain", "m_split",
                "v_ready", "scores2", "exp_done", "pv_done", "o_sb", "den", "log", "inv", "normed", "o_free")}
            loaded = [sem(f"{tag}_loaded{p}") for p in range(NB)]
            m_rows = [sem(f"{tag}_m_rows{p}") for p in range(NB)]
            o_stored = [sem(f"{tag}_o_stored{q}") for q in range(NO)]
            LOAD = 16 * (GH + GH // 2 + GH * NX)
            MROWS = 16 * 3
            NM = 32 + NX

            def sp_load(sp, gi, p):
                for pr in range(GH // 2):
                    heads = scratch_k[bass.ds(gi * GH + 2 * pr, 2), :, :].rearrange("h r n -> (h r) n")
                    sp.dma_start(KP[p][0:R_MAX, pr, :], heads).then_inc(loaded[p], 16)
                for j in range(GH):
                    r = HR * (j % 2)
                    sp.dma_start(q_cols(p, j, 0, S)[r:r + HR, :], scratch_q[gi * GH + j, :, :]).then_inc(loaded[p], 16)
                    if NX:
                        sp.dma_start(x_cols(p, j)[r:r + R_MASK, :],
                                     scratch_q[gi * GH + j, 0:R_MASK, 0:XQ]).then_inc(loaded[p], 16)

            def sp_rows(sp, gi, p):
                sp.wait_ge(sems["m_split"], gi + 1)
                for t in range(3):
                    sp.dma_start(QF[p][R_MAX + t:R_MAX + t + 1, 0:NM * P], m_parts[0:NM, p, t, :]).then_inc(m_rows[p], 16)

            def sp_store(sp, gi, o):
                sp.wait_ge(sems["normed"], gi * NO + o + 1)
                if NX and o == 1:
                    sp.dma_start(scratch_x.rearrange("b g p n -> (b g) p n")[gi, :, :], SX[:, 2, :]).then_inc(o_stored[o], 16)
                else:
                    q = 1 if o else 0
                    dst = scratch_o.rearrange("b g p n -> (b g) p n")[gi, :, q * CH:(q + 1) * CH]
                    sp.dma_start(dst, ONT[q]).then_inc(o_stored[o], 16)

            def sp_step(sp, gi, p, rows, load):
                sp_store(sp, gi, 0)
                if rows:
                    sp_rows(sp, gi + 1, (p + 1) % NB)
                if NX:
                    sp_store(sp, gi, 1)
                if load:
                    sp.wait_ge(sems["pv_done"], gi * NV + NV + 1)
                    sp_load(sp, gi + NB, p)
                sp_store(sp, gi, NO - 1)

            def pe_max(pe, gi, p, k, u):
                base = gi * (NU + 1)
                if u == 0:
                    pe.wait_ge(loaded[p], k * LOAD)
                pe.wait_ge(sems["scores1_read"], base + 1 + max(0, u - 1))
                if u == NU:
                    pe.wait_ge(sems["m_ready"], gi + 1)
                    nc.tensor.transpose(SA[0][:, 0:P], m_col[:, :], w["ident"][:, :]).then_inc(sems["m_turned"], 1)
                    return
                j, qt, half, width, diag = s1[u]
                dst = SA[u % 2]
                if j == "x":
                    for j in range(GH):
                        mm = nc.tensor.matmul(dst[32 * j:32 * j + XQ, :], x_cols(p, j)[0:R_MAX, :],
                                              KP[p][0:R_MAX, j // 2, half * CH:(half + 1) * CH], start=True, stop=True)
                    mm.then_inc(sems["scores1"], 1)
                    return
                mm = nc.tensor.matmul(dst[:, 0:width], q_cols(p, j, qt * P, P)[0:R_MAX, :],
                                      KP[p][0:R_MAX, j // 2, half * CH:half * CH + width], start=True, stop=not diag)
                if diag:
                    mm = nc.tensor.matmul(dst[:, width - P:width], w["ident_b"][:, :], w["mask_qk"][:, :],
                                          start=False, stop=True)
                mm.then_inc(sems["scores1"], 1)

            def pe_scores(pe, gi, p, k, v):
                base = gi * NV
                if v == 0:
                    pe.wait_ge(m_rows[p], k * MROWS)
                pe.wait_ge(sems["exp_done"], base + 1 + max(0, v - 1))
                qh, kc, pr, off, diag = s2[v]
                dst = SB[v % 2]
                if qh == "x":
                    for kc in range(QT):
                        for j in range(GH):
                            at = XQ * (2 * kc + j // 2)
                            mm = nc.tensor.matmul(dst[:, j % 2, at:at + XQ], KP[p][0:R_END, j // 2, kc * P:(kc + 1) * P],
                                                  x_cols(p, j)[0:R_END, :], start=True, stop=True)
                    mm.then_inc(sems["scores2"], 1)
                    return
                for i in range(2):
                    mm = nc.tensor.matmul(dst[:, i, off:CH], KP[p][0:R_END, pr, kc * P:(kc + 1) * P],
                                          q_cols(p, 2 * pr + i, qh * CH + off, CH - off)[0:R_END, :],
                                          start=True, stop=not diag)
                    if diag:
                        mm = nc.tensor.matmul(dst[:, i, off:off + P], w["ident_b"][:, :], w["mask_kq"][:, :],
                                              start=False, stop=True)
                mm.then_inc(sems["scores2"], 1)

            def pe_values(pe, gi, p, v):
                if v == 0:
                    pe.wait_ge(sems["v_ready"], gi + 1)
                pe.wait_ge(sems["exp_done"], gi * NV + v + 2)
                qh, kc, pr, off, _ = s2[v]
                if qh == "x":
                    pe.wait_ge(sems["o_free"], gi * NO + 3)
                    for kc in range(QT):
                        for j in range(GH):
                            at = XQ * (2 * kc + j // 2)
                            mm = nc.tensor.matmul(OB[0][32 * j:32 * j + 32, 0:XQ], VP[p][:, kc, j, :],
                                                  EB[v % 4][:, j % 2, at:at + XQ],
                                                  start=(kc == 0), stop=(kc == QT - 1))
                    mm.then_inc(sems["pv_done"], 1)
                    return
                if kc == 0 and pr == 0:
                    pe.wait_ge(sems["o_free"], gi * NO + 1 + qh)
                for i in range(2):
                    j = 2 * pr + i
                    mm = nc.tensor.matmul(OB[qh][32 * j:32 * j + 32, off:CH], VP[p][:, kc, j, :], EB[v % 4][:, i, off:CH],
                                          start=(kc == 0), stop=(kc == lastk[qh]))
                mm.then_inc(sems["pv_done"], 1)

            def out_of(o):
                if NX and o == 1:
                    return OB[0][:, 0:XQ], SX[:, 0, :], SX[:, 1, :], SX[:, 2, :]
                q = 1 if o else 0
                return OB[q], OS[q], RD[q], ONT[q]

            def pe_den(pe, gi, o):
                pe.wait_ge(sems["o_sb"], gi * NO + o + 1)
                dst, src, _, _ = out_of(o)
                nc.tensor.matmul(dst, w["den_sel"][:, :], src, start=True, stop=True).then_inc(sems["den"], 1)

            def outputs_at(gi, v, lag, previous, do):
                for o in range(NO - 1):
                    if v == ends[o] + lag:
                        do(gi, o)
                if previous and v == lag - 1:
                    do(gi - 1, NO - 1)

            def pe_step(pe, gi, p, k, previous, ahead):
                def maxima(items):
                    for d, u in items:
                        if d <= ahead:
                            pe_max(pe, gi + d, (p + d) % NB, k + (p + d) // NB, u)

                pe_scores(pe, gi, p, k, 0)
                pe_scores(pe, gi, p, k, 1)
                for v in range(NV):
                    maxima(plan[2 * v])
                    pe_values(pe, gi, p, v)
                    maxima(plan[2 * v + 1])
                    if v + 2 < NV:
                        pe_scores(pe, gi, p, k, v + 2)
                    outputs_at(gi, v, 3, previous, lambda g, o: pe_den(pe, g, o))

            def act_step(act, gi, p, previous):
                for v in range(NV):
                    qh, kc, pr, off, _ = s2[v]
                    act.wait_ge(sems["scores2"], gi * NV + v + 1)
                    act.wait_ge(sems["pv_done"], gi * NV + 1 + max(0, v - 3))
                    nc.scalar.activation(EB[v % 4][:, :, off:CH], SB[v % 2][:, :, off:CH], ACT.Exp,
                                         scale=SCALE).then_inc(sems["exp_done"], 1)
                    outputs_at(gi, v, 2, previous, lambda g, o: act_copy(act, g, o))
                    outputs_at(gi, v, 4, previous, lambda g, o: act_inv(act, g, o))

            def act_copy(act, gi, o):
                act.wait_ge(sems["pv_done"], gi * NV + ends[o] + 2)
                src, dst, _, _ = out_of(o)
                nc.scalar.copy(dst, src).then_inc(sems["o_sb"], 1)

            def act_inv(act, gi, o):
                act.wait_ge(sems["den"], gi * NO + o + 1)
                den, _, inv, _ = out_of(o)
                nc.scalar.activation(inv, den, ACT.Ln).then_inc(sems["log"], 1)
                act.wait_ge(sems["log"], gi * NO + o + 1)
                nc.scalar.activation(inv, inv, ACT.Exp, scale=-1.0).then_inc(sems["inv"], 1)

            def dve_max(dve, gi, p, u):
                if u == NU:
                    dve_rows(dve, gi, p)
                    return
                dve.wait_ge(sems["scores1"], gi * NU + u + 1)
                j, qt, half, width, _ = s1[u]
                at = 32 if j == "x" else QT * j + qt
                nc.vector.tensor_reduce(m_cat[:, half, at:at + 1], SA[u % 2][:, 0:width], AX.X,
                                        ALU.max).then_inc(sems["scores1_read"], 1)

            def dve_rows(dve, gi, p):
                dve.wait_ge(sems["scores1_read"], gi * (NU + 1) + NU + 1)
                nc.vector.tensor_tensor(m_col[:, 0:NM], m_cat[:, 0, 0:NM], m_cat[:, 1, 0:NM],
                                        ALU.max).then_inc(sems["m_ready"], 1)
                dve.wait_ge(sems["m_turned"], gi + 1)
                nc.vector.tensor_scalar(m_neg[:, 0, :], SA[0][0:40, 0:P], -1.0, None,
                                        ALU.mult).then_inc(sems["scores1_read"], 1)
                k = gi * 3
                dve.wait_ge(sems["scores1_read"], (gi + 1) * (NU + 1) + 1)
                nc.vector.tensor_copy(m_parts[:, p, 0, :], m_neg[:, 0, :]).then_inc(sems["m_chain"], 1)
                dve.wait_ge(sems["m_chain"], k + 1)
                nc.vector.tensor_tensor(m_neg[:, 1, :], m_neg[:, 0, :], m_parts[:, p, 0, :],
                                        ALU.subtract).then_inc(sems["m_chain"], 1)
                dve.wait_ge(sems["m_chain"], k + 2)
                nc.vector.tensor_copy(m_parts[:, p, 1, :], m_neg[:, 1, :]).then_inc(sems["m_chain"], 1)
                dve.wait_ge(sems["m_chain"], k + 3)
                nc.vector.tensor_tensor(m_parts[:, p, 2, :], m_neg[:, 1, :], m_parts[:, p, 1, :],
                                        ALU.subtract).then_inc(sems["m_split"], 1)

            def dve_out(dve, gi, o):
                dve.wait_ge(sems["inv"], gi * NO + o + 1)
                _, src, inv, dst = out_of(o)
                dve.wait_ge(o_stored[o], gi * 16 + 16)
                nc.vector.tensor_tensor(dst, src, inv, ALU.mult).then_inc(sems["normed"], 1)
                dve.wait_ge(sems["normed"], gi * NO + o + 1)
                dve.sem_inc(sems["o_free"], 1)

            def dve_step(dve, gi, p, previous, ahead):
                for v in range(NV):
                    for d, u in plan[2 * v] + plan[2 * v + 1]:
                        if d <= ahead:
                            dve_max(dve, gi + d, (p + d) % NB, u)
                    outputs_at(gi, v, 6, previous, lambda g, o: dve_out(dve, g, o))

            return dict(locals())

        def run_attention(tag, causal):
            t = attention(tag, causal)
            sems, NO, NX, NV, NU, AHEAD = t["sems"], t["NO"], t["NX"], t["NV"], t["NU"], t["AHEAD"]
            trips = (GROUPS - 4) // NB
            tail = range(1 + trips * NB, GROUPS)
            ahead = [min(2, GROUPS - 1 - g) for g in range(GROUPS)]
            assert ahead[tail[0] - 1] == 2
            v_init, s_init, s_xrows = sem(f"{tag}_v_init"), sem(f"{tag}_init"), sem(f"{tag}_xrows")
            with nc.Block() as block:
                @block.sync
                def _(sp):
                    sp.wait_ge(s_init, 2 * NB)
                    if NX:
                        for p in range(NB):
                            for j in range(GH):
                                r = HR * (j % 2) + R_MASK
                                sp.dma_start(x_cols(p, j)[r:r + 2, :], a["x_rows"]).then_inc(s_xrows, 16)
                        sp.wait_ge(s_xrows, 16 * NB * GH)
                    for q in range(NO):
                        sp.sem_inc(t["o_stored"][q], 16)
                    for g in range(NB):
                        t["sp_load"](sp, g, g)
                    t["sp_rows"](sp, 0, 0)
                    t["sp_step"](sp, 0, 0, True, True)
                    with sp.Fori(0, trips) as i:
                        for s in range(1, NB + 1):
                            t["sp_step"](sp, i * NB + s, s % NB, True, True)
                    for g in tail:
                        t["sp_step"](sp, g, g % NB, g + 1 < GROUPS, g + NB < GROUPS)
                    for q in range(NO):
                        sp.wait_ge(t["o_stored"][q], 16 * (GROUPS + 1))

                @block.tensor
                def _(pe):
                    pe.sem_inc(sems["pv_done"], 1)
                    for u in range(NU + 1):
                        t["pe_max"](pe, 0, 0, 1, u)
                    for u in range(AHEAD):
                        t["pe_max"](pe, 1, 1, 1, u)
                    t["pe_step"](pe, 0, 0, 1, False, 2)
                    with pe.Fori(0, trips) as i:
                        for s in range(1, NB + 1):
                            t["pe_step"](pe, i * NB + s, s % NB, i + (1 + s // NB), True, 2)
                    for g in tail:
                        t["pe_step"](pe, g, g % NB, g // NB + 1, True, ahead[g])
                    t["pe_den"](pe, GROUPS - 1, NO - 1)

                @block.scalar
                def _(act):
                    act.preload_act_table_set("natural_log_exp_and_others")
                    act.sem_inc(sems["exp_done"], 1)
                    t["act_step"](act, 0, 0, False)
                    with act.Fori(0, trips) as i:
                        for s in range(1, NB + 1):
                            t["act_step"](act, i * NB + s, s % NB, True)
                    for g in tail:
                        t["act_step"](act, g, g % NB, True)
                    t["act_copy"](act, GROUPS - 1, NO - 1)
                    t["act_inv"](act, GROUPS - 1, NO - 1)

                @block.vector
                def _(dve):
                    dve.sem_inc(sems["scores1_read"], 1)
                    dve.sem_inc(sems["o_free"], 2)
                    for u in range(NU + 1):
                        t["dve_max"](dve, 0, 0, u)
                    for u in range(AHEAD):
                        t["dve_max"](dve, 1, 1, u)
                    t["dve_step"](dve, 0, 0, False, 2)
                    with dve.Fori(0, trips) as i:
                        for s in range(1, NB + 1):
                            t["dve_step"](dve, i * NB + s, s % NB, True, 2)
                    for g in tail:
                        t["dve_step"](dve, g, g % NB, True, ahead[g])
                    t["dve_out"](dve, GROUPS - 1, NO - 1)

                def pool_v(pool, gi, p):
                    rows = v_tok[:, bass.ds(gi * (QT * GH * HD), QT * GH * HD)].rearrange(
                        "p (k j d) -> p k j d", k=QT, j=GH)
                    nc.gpsimd.tensor_copy(VP[p][:, :, :, 0:HD], rows).then_inc(sems["v_ready"], 1)

                @block.gpsimd
                def _(pool):
                    for p in range(NB):
                        pool.memset(QF[p], 0.0).then_inc(s_init, 1)
                        pool.wait_ge(s_init, 2 * p + 1)
                        pool.memset(KP[p][96:P, :, :], 1.0).then_inc(s_init, 1)
                        pool.wait_ge(s_init, 2 * p + 2)
                    for p in range(NB):
                        pool.memset(VP[p], 0.0).then_inc(v_init, 1)
                        pool.wait_ge(v_init, 2 * p + 1)
                        pool.memset(VP[p][:, :, :, HD:HD + 1], 1.0).then_inc(v_init, 1)
                        pool.wait_ge(v_init, 2 * p + 2)
                    for g in range(NB):
                        pool_v(pool, g, g)
                    with pool.Fori(0, (GROUPS - 1) // NB - 1) as i:
                        for s in range(NB):
                            pool.wait_ge(sems["pv_done"], i * (NB * NV) + (s + 1) * NV + 1)
                            pool_v(pool, i * NB + (s + NB), s)
                    pool.wait_ge(sems["pv_done"], (GROUPS - NB) * NV + 1)
                    pool_v(pool, GROUPS - 1, (GROUPS - 1) % NB)

        s_w, s_small, s_zero = sem("s_w"), sem("s_small"), sem("s_zero")
        s_gate, s_rows0 = [sem(f"s_gate{i}") for i in range(8)], sem("s_rows0")
        zero_tile = work[:, 1, :].bitcast(BF16)[:, 0:S]
        with nc.Block() as block:
            @block.sync
            def _(sp):
                for name, t in w.items():
                    dst = t[tuple(slice(None) for _ in t.shape)]
                    sp.dma_start(dst, a[name]).then_inc(s_w, 16)
                sp.wait_ge(s_zero, 1)
                for b in range(B):
                    hs = slice(b * H, (b + 1) * H)
                    for dram in (scratch_q, scratch_k):
                        sp.dma_start(dram[hs, R_MASK:HR, :], zero_tile[0:2 * H, :]).then_inc(s_rows0, 16)
                sp.wait_ge(s_rows0, 16 * 2 * B)

            @block.gpsimd
            def _(pool):
                pool.memset(zero_tile, 0.0).then_inc(s_zero, 1)
                pool.memset(eps_col[:, 0:1], EPS).then_inc(s_zero, 1)
                pool.memset(eps_col[:, 1:2], EPS * EPS).then_inc(s_zero, 1)
                pool.memset(m_cat[:, :, :], -3.0e38)
                pool.memset(m_col[:, :], 0.0)

            @block.scalar
            def _(act):
                act.preload_act_table_set("natural_log_exp_and_others")
                act.wait_ge(s_w, 16 * len(w))
                act.wait_ge(s_gate[7], 1)
                nc.scalar.activation(a_neg[:, :], a_neg[:, :],
                                     ACT.Exp).then_inc(s_gate[0], 1)
                nc.scalar.activation(gate_tmp[:, 0:1], col("q_gate"), ACT.Square).then_inc(s_gate[1], 1)
                act.wait_ge(s_gate[2], 1)
                nc.scalar.activation(gate_tmp[0:H, 1:2], ps[0:H, 0, 0:1], ACT.Ln).then_inc(s_gate[3], 1)
                act.wait_ge(s_gate[3], 1)
                nc.scalar.activation(gate_tmp[0:H, 2:3], gate_tmp[0:H, 1:2], ACT.Exp, scale=-0.5).then_inc(s_gate[4], 1)

            @block.tensor
            def _(pe):
                pe.wait_ge(s_w, 16 * len(w))
                pe.wait_ge(s_gate[1], 1)
                nc.tensor.matmul(ps[0:H, 0, 0:1], w["head_sel"][:, :], gate_tmp[:, 0:1], start=True,
                                 stop=True).then_inc(s_gate[2], 1)
                pe.wait_ge(s_gate[4], 1)
                nc.tensor.matmul(ps[:, 1, 0:1], w["head_back"][:, :], gate_tmp[0:H, 2:3], start=True,
                                 stop=True).then_inc(s_gate[5], 1)

            @block.vector
            def _(dve):
                dve.wait_ge(s_w, 16 * len(w))
                nc.vector.tensor_scalar(a_neg[:, :], w["cols"][:, COLS["A_log"][0]:COLS["A_log"][0] + CI * DS], 80.0,
                                        None, ALU.min).then_inc(s_gate[7], 1)
                dve.wait_ge(s_gate[0], 1)
                nc.vector.tensor_scalar(a_neg[:, :], a_neg[:, :], -1.0, None, ALU.mult)
                dve.wait_ge(s_gate[5], 1)
                nc.vector.tensor_tensor(gate_tmp[:, 3:4], col("q_gate"), ps[:, 1, 0:1], ALU.mult).then_inc(s_gate[6], 1)
                dve.wait_ge(s_gate[6], 1)
                nc.vector.tensor_scalar(q_gate_sel[:, :], w["head_sel"][:, :], gate_tmp[:, 3:4], None, ALU.mult)

        end_phase()

        a_norm, a_qkv = norm_sems("a_norm"), qkv_sems("a_qkv")
        a_norm.update({k: sem(f"a_norm_{k}") for k in ("log2", "rstd2", "out2")})
        RSTD2 = chunks(14)
        a_x = [sem(f"a_x{c}") for c in range(2)]
        a_free, a_turned, a_copied, a_kept = sem("a_free"), sem("a_turned"), sem("a_copied"), sem("a_kept")
        x_dram = a["x"]
        with nc.Block() as block:
            @block.sync
            def _(sp):
                for c in range(2):
                    sp.sem_inc(a_qkv["stored"][c], 16)
                with sp.Fori(0, B) as b:
                    for c in range(2):
                        sp.wait_ge(a_free, b * 2 + c + 1)
                        sp.dma_start(XIN[c], x_dram[bass.ds(b * QT + 4 * c, 4), :, :].rearrange("t p f -> p t f")
                                     ).then_inc(a_x[c], 16)
                    qkv_store(sp, a_qkv, b * 2 + 1, b)
                for c in range(2):
                    sp.wait_ge(a_qkv["stored"][c], STORED * B + 16)

            @block.tensor
            def _(pe):
                pe.sem_inc(a_free, 2)
                with pe.Fori(0, B) as b:
                    for c in range(2):
                        pe.wait_ge(a_x[c], b * 16 + 16)
                        for t in range(4):
                            mm = nc.tensor.transpose(ps[:, 4 * c, t * P:(t + 1) * P], XIN[c][:, t, :], w["ident"][:, :])
                        mm.then_inc(a_turned, 1)
                        pe.wait_ge(a_turned, b * 2 + c + 1)
                        pe.sem_inc(a_free, 1)
                    norm_pe(pe, a_norm, b * 2 + 1, XR, lambda e, c: e.wait_ge(a_copied, b * 2 + c + 1))
                    qkv_pe(pe, a_qkv, b * 2 + 1, w["qkv_w"], XN, lambda e, c: e.wait_ge(a_norm["affine"], b * 2 + c + 1))

            @block.scalar
            def _(act):
                act.preload_act_table_set("natural_log_exp_and_others")
                with act.Fori(0, B) as b:
                    norm_act(act, a_norm, b * 2 + 1, both=RSTD2)
                    for c in range(2):
                        act.wait_ge(a_qkv["stored"][c], b * STORED + 16)
                    qkv_act(act, a_qkv, b * 2 + 1, True)

            @block.vector
            def _(dve):
                with dve.Fori(0, B) as b:
                    for c in range(2):
                        dve.wait_ge(a_turned, b * 2 + c + 1)
                        nc.vector.tensor_copy(XR[c], bank(c, 0)).then_inc(a_copied, 1)
                    n = b * 2 + 1
                    for c in range(2):
                        dve.wait_ge(a_norm["mean"], n + c)
                        nc.vector.tensor_tensor(DEV[c], XR[c], bank(c, 0), ALU.subtract).then_inc(a_norm["centred"], 1)
                    for c in range(2):
                        dve.wait_ge(a_norm["rstd2"], n + c)
                        nc.vector.tensor_tensor(XN[c], DEV[c], RSTD2[c], ALU.mult).then_inc(a_norm["out2"], 1)
                        dve.wait_ge(a_norm["out2"], n + c)
                        nc.vector.tensor_scalar(XN[c], XN[c], col("g_attn"), col("b_attn"), ALU.mult,
                                                ALU.add).then_inc(a_norm["affine"], 1)
                        dve.wait_ge(a_norm["rstd"], n + c)
                        nc.vector.tensor_tensor(h0[:, bass.ds(b * S + c * CH, CH)], DEV[c], RSTD[c],
                                                ALU.mult).then_inc(a_norm["out"], 1)
                    qkv_dve(dve, a_qkv, b * 2 + 1, b, True)
                    dve.wait_ge(a_kept, b * 2 + 2)

            @block.gpsimd
            def _(pool):
                with pool.Fori(0, B) as b:
                    for c in range(2):
                        pool.wait_ge(a_copied, b * 2 + c + 1)
                        nc.gpsimd.tensor_copy(x_res[:, bass.ds(b * S + c * CH, CH)], XR[c]).then_inc(a_kept, 1)

        end_phase()
        run_attention("b", True)
        end_phase()

        CV = [[work[:, 13 + c, i * CH:(i + 1) * CH] for i in range(CI)] for c in range(2)]
        SZ, U, DL, DU, DA, DBU, HC = ([work[:, k + i, :] for i in range(CI)] for k in (5, 7, 9, 11, 13, 15, 19))
        HS = [[work[:, k, :] for k in ks] for ks in ((17, 18), (2, 4))]
        CR = [work[:, k, :] for k in (1, 3)]
        SP1 = [[work[:, 15 + c, i * CH:(i + 1) * CH] for i in range(CI)] for c in range(2)]
        SP2 = chunks(20)
        YT = DBU
        B_HI = [SQ[c].bitcast(BF16)[0:6 * DS, 0:CH] for c in range(2)]
        B_MID = [SQ[c].bitcast(BF16)[0:6 * DS, CH:2 * CH] for c in range(2)]
        B_REST = [DEV[c][0:6 * DS, :] for c in range(2)]
        DT = [RSTD[c][0:DR, :] for c in range(2)]
        SIM16 = [work[0:H, 14, c * CH:(c + 1) * CH] for c in range(2)]

        def gate(c, k):
            return small[:, c, 32 * k:32 * k + 32].rearrange("p (t e) -> p t e", t=4)

        gmax = [small[:, c, 128:132] for c in range(2)]
        gmin = [small[:, c, 132:136] for c in range(2)]
        iota = w["iota"]

        NLN = 8
        ln = norm_sems("c_norm")
        qs = qkv_sems("c_qkv")
        cs = {k: sem("c_" + k) for k in (
            "att", "ctx", "xa", "rec", "tanh", "vel", "drag", "xs", "xa2",
            "ffh", "gelu", "ffy", "xa3", "xr1", "gates", "g_sb", "g_max", "g_less", "g_cand", "g_min", "onehot",
            "oh_turned", "oh_b", "mask", "moe_h", "relu", "moe_y", "moe_y_sb", "masked", "acc", "xr2",
            "pad", "inp", "in_sb", "tap", "u", "xp", "bc_hi", "bc_rest", "bc_mid", "bc", "dt", "dtp", "sp_abs",
            "sp_exp", "sp", "dl", "du", "b_row", "c_row", "c_sb", "da", "dbu", "state", "hc", "y_sum", "yy", "yg", "op", "ao",
            "xr3", "kept", "q_sq", "sim_parts", "sim_log", "sim_inv", "sim_prod", "sim", "sim_kept")}
        c_ol = [sem(f"c_ol{c}") for c in range(2)]

        def cols_of(b, c):
            return bass.ds(b * S + c * CH, CH)

        with nc.Block() as block:
            @block.sync
            def _(sp):
                def load(b):
                    for c in range(2):
                        src = scratch_o.rearrange("b g p n -> b p g n")[b, :, :, c * CH:(c + 1) * CH]
                        sp.dma_start(OL[c], src).then_inc(c_ol[c], 16)

                for c in range(2):
                    sp.sem_inc(qs["stored"][c], 16)
                load(0)
                with sp.Fori(0, B - 1) as b:
                    sp.wait_ge(cs["op"], b * 2 + 2)
                    load(b + 1)
                    qkv_store(sp, qs, b * 2 + 1, b)
                qkv_store(sp, qs, B * 2 - 1, B - 1)
                for c in range(2):
                    sp.wait_ge(qs["stored"][c], STORED * B + 16)

            @block.tensor
            def _(pe):
                with pe.Fori(0, B) as b:
                    n = b * 2 + 1

                    def lnv(i):
                        return b * (2 * NLN) + 2 * i + 1

                    def ready(s, value):
                        return lambda e, c: e.wait_ge(s, value + c)

                    for c in range(2):
                        pe.wait_ge(c_ol[c], b * 16 + 16)
                        for g in range(H // GH):
                            mm = nc.tensor.matmul(bank(c, 1), w["out_w"][:, g, :], OL[c][:, g, :], start=(g == 0),
                                                  stop=(g == H // GH - 1))
                        mm.then_inc(cs["att"], 1)
                    norm_pe(pe, ln, lnv(0), XA, ready(cs["xa"], n))
                    def from_context(s, c):
                        if s >= 2:
                            pe.wait_ge(cs["tanh"], b * (2 * STEPS) + 2 * (s - 2) + c + 1)
                        nc.tensor.matmul(bank(c, 1 + s % 2), w["w_ctx"][:, :], CTX[c], start=True, stop=False)

                    for c in range(2):
                        pe.wait_ge(cs["ctx"], n + c)
                        from_context(0, c)
                    for s in range(STEPS):
                        for c in range(2):
                            if s == 0:
                                pe.wait_ge(ln["affine"], b * 6 + 1 + c)
                            else:
                                pe.wait_ge(cs["xs"], b * (2 * STEPS) + 2 * s - 1 + c)
                            nc.tensor.matmul(bank(c, 1 + s % 2), w["w_x"][:, :], XS[c], start=False,
                                             stop=True).then_inc(cs["rec"], 1)
                            if s + 1 < STEPS:
                                from_context(s + 1, c)
                    norm_pe(pe, ln, lnv(1), XA, ready(cs["xa2"], n))
                    M = FF // P
                    for m in range(M):
                        for c in range(2):
                            if m == 0:
                                pe.wait_ge(ln["affine"], b * 6 + 3 + c)
                            if m >= 2:
                                pe.wait_ge(cs["gelu"], b * (2 * M) + 2 * (m - 2) + c + 1)
                            nc.tensor.matmul(bank(c, 1 + m % 2), w["ff_w1"][:, m * P:(m + 1) * P], NRM[c], start=True,
                                             stop=True).then_inc(cs["ffh"], 1)
                    for m in range(M):
                        for c in range(2):
                            pe.wait_ge(cs["gelu"], b * (2 * M) + 2 * m + c + 1)
                            mm = nc.tensor.matmul(bank(c, 3), w["ff_w2"][:, m, :], HID[c][:, m, :], start=(m == 0),
                                                  stop=(m == M - 1))
                            if m == M - 1:
                                mm.then_inc(cs["ffy"], 1)
                    norm_pe(pe, ln, lnv(2), XA, ready(cs["xa3"], n))
                    norm_pe(pe, ln, lnv(3), XR, ready(cs["xr1"], n))
                    for c in range(2):
                        pe.wait_ge(ln["out"], lnv(3) + c)
                        for t in range(CH // P):
                            mm = nc.tensor.matmul(bank(c, 1)[:, t * E:(t + 1) * E], NRM[c][:, t * P:(t + 1) * P],
                                                  w["Wg"][:, :], start=True, stop=True)
                        mm.then_inc(cs["gates"], 1)
                    for c in range(2):
                        pe.wait_ge(cs["onehot"], n + c)
                        for t in range(CH // P):
                            mm = nc.tensor.matmul(bank(c, 2)[0:E, t * P:(t + 1) * P], gate(c, 3)[:, t, :],
                                                  w["ident"][:, :], start=True, stop=True)
                        mm.then_inc(cs["oh_turned"], 1)
                    for e in range(E):
                        for c in range(2):
                            if e == 0:
                                pe.wait_ge(cs["oh_b"], n + c)
                            else:
                                pe.wait_ge(cs["masked"], b * (2 * E) + 2 * (e - 1) + c + 1)
                            nc.tensor.matmul(bank(c, 0), w["exp_sel"][:, e, :], onehot_b[:, c, :], start=True,
                                             stop=True).then_inc(cs["mask"], 1)
                            for m in range(M):
                                if m >= 2:
                                    pe.wait_ge(cs["relu"], b * (2 * E * M) + (2 * e + c) * M + m - 1)
                                nc.tensor.matmul(bank(c, 1 + m % 2), w["W1"][:, e, m * P:(m + 1) * P], NRM[c],
                                                 start=True, stop=True).then_inc(cs["moe_h"], 1)
                        for c in range(2):
                            if e:
                                pe.wait_ge(cs["moe_y_sb"], b * (2 * E) + 2 * (e - 1) + c + 1)
                            for m in range(M):
                                pe.wait_ge(cs["relu"], b * (2 * E * M) + (2 * e + c) * M + m + 1)
                                mm = nc.tensor.matmul(bank(c, 3), w["W2"][:, e, m, :], HID[c][:, m, :], start=(m == 0),
                                                      stop=(m == M - 1))
                            mm.then_inc(cs["moe_y"], 1)
                    norm_pe(pe, ln, lnv(4), ACC, ready(cs["acc"], b * (2 * (E - 1)) + 2 * (E - 2) + 1))
                    norm_pe(pe, ln, lnv(5), XR, ready(cs["xr2"], n))
                    for o in range(2 * CI):
                        for c in range(2):
                            if o == 0:
                                pe.wait_ge(ln["affine"], b * 6 + 5 + c)
                            if o >= 2:
                                pe.wait_ge(cs["in_sb"], b * (4 * CI) + 2 * (o - 2) + c + 1)
                            nc.tensor.matmul(bank(c, 1 + o % 2), w["in_proj_w"][:, o * P:(o + 1) * P], NRM[c], start=True,
                                             stop=True).then_inc(cs["inp"], 1)
                    for c in range(2):
                        pe.wait_ge(cs["u"], b * 4 + 2 * c + 2)
                        at = slice(c * CH, (c + 1) * CH)
                        for i in range(CI):
                            nc.tensor.matmul(bank(c, 1)[0:DR, :], w["x_proj_dt"][:, i, :], U[i][:, at], start=(i == 0),
                                             stop=(i == CI - 1))
                        for i in range(CI):
                            mm = nc.tensor.matmul(bank(c, 2)[0:6 * DS, :], w["x_proj_bc"][:, i, :], U[i][:, at],
                                                  start=(i == 0), stop=(i == CI - 1))
                        mm.then_inc(cs["xp"], 1)
                    for c in range(2):
                        pe.wait_ge(cs["dt"], n + c)
                        for i in range(CI):
                            mm = nc.tensor.matmul(bank(c, 1 + 2 * i), w["dt_proj_w"][:, i * P:(i + 1) * P], DT[c],
                                                  start=True, stop=True)
                        mm.then_inc(cs["dtp"], 1)

                    def row(k, bank0, s):
                        for c in range(2):
                            mm = nc.tensor.matmul(ps[:, bank0 + c, :], w["bc_sel"][:, k, :],
                                                  bc_parts[:, c * CH:(c + 1) * CH], start=True, stop=True)
                        mm.then_inc(s, 1)

                    def add_state(k, i):
                        pe.wait_ge(cs["hc"], b * (DS * CI) + 2 * k + i + 1)
                        for c in range(2):
                            mm = nc.tensor.matmul(ps[:, 4 + 2 * i + c, :], w["ident"][:, :], HC[i][:, c * CH:(c + 1) * CH],
                                                  start=(k == 0), stop=(k == DS - 1))
                        mm.then_inc(cs["y_sum"], 1)

                    pe.wait_ge(cs["bc"], n + 1)
                    pe.wait_ge(cs["du"], b * 4 + 4)
                    row(0, 0, cs["b_row"])
                    row(DS, 2, cs["c_row"])
                    for k in range(DS):
                        if k:
                            add_state(k - 1, 0)
                        if k + 1 < DS:
                            pe.wait_ge(cs["dbu"], b * (DS * CI) + 2 * k + 2)
                            row(k + 1, 0, cs["b_row"])
                        if k:
                            add_state(k - 1, 1)
                        if k + 1 < DS:
                            pe.wait_ge(cs["c_sb"], b * DS + k + 1)
                            row(DS + k + 1, 2, cs["c_row"])
                    for i in range(CI):
                        add_state(DS - 1, i)
                    for c in range(2):
                        pe.wait_ge(cs["yg"], b * 4 + 2 * c + 2)
                        for i in range(CI):
                            mm = nc.tensor.matmul(bank(c, 1), w["out_proj_w"][:, i, :], YT[i][:, c * CH:(c + 1) * CH],
                                                  start=(i == 0), stop=(i == CI - 1))
                        mm.then_inc(cs["op"], 1)
                    norm_pe(pe, ln, lnv(6), TT_, ready(cs["ao"], n))
                    norm_pe(pe, ln, lnv(7), XR, ready(cs["xr3"], n))
                    qkv_pe(pe, qs, n, w["qkv2_w"], XN, ready(ln["out"], lnv(7)))
                    for c in range(2):
                        pe.wait_ge(cs["q_sq"], n + c)
                        nc.tensor.matmul(bank(c, 0)[0:H, :], w["head_sel"][:, :], SQ[c], start=True, stop=True)
                        nc.tensor.matmul(bank(c, 1)[0:H, :], q_gate_sel[:, :], QK32[c][:, 0, :], start=True,
                                         stop=True).then_inc(cs["sim_parts"], 1)
                    for c in range(2):
                        pe.wait_ge(cs["sim_prod"], n + c)
                        nc.tensor.matmul(bank(c, 2), w["sim_sum"][:, :], SIM16[c], start=True,
                                         stop=True).then_inc(cs["sim"], 1)

            @block.scalar
            def _(act):
                with act.Fori(0, B) as b:
                    n = b * 2 + 1

                    def lnv(i):
                        return b * (2 * NLN) + 2 * i + 1

                    act.preload_act_table_set("natural_log_exp_and_others")
                    norm_act(act, ln, lnv(0))
                    for c in range(2):
                        act.wait_ge(qs["stored"][c], b * STORED + 16)
                    for s in range(STEPS):
                        for c in range(2):
                            act.wait_ge(cs["rec"], b * (2 * STEPS) + 2 * s + c + 1)
                            nc.scalar.activation(TT_[c], bank(c, 1 + s % 2), ACT.Tanh, bias=col("b_inl")).then_inc(cs["tanh"], 1)
                    act.preload_act_table_set("natural_log_exp_and_others")
                    norm_act(act, ln, lnv(1))
                    M = FF // P
                    for m in range(M):
                        for c in range(2):
                            act.wait_ge(cs["ffh"], b * (2 * M) + 2 * m + c + 1)
                            nc.scalar.activation(HID[c][:, m, :], bank(c, 1 + m % 2), ACT.Gelu,
                                                 bias=col("ff_b1", m)).then_inc(cs["gelu"], 1)
                    act.preload_act_table_set("natural_log_exp_and_others")
                    norm_act(act, ln, lnv(2))
                    norm_act(act, ln, lnv(3))
                    for e in range(E):
                        for c in range(2):
                            if e:
                                act.wait_ge(cs["moe_y"], b * (2 * E) + 2 * (e - 1) + c + 1)
                            for m in range(M):
                                act.wait_ge(cs["moe_h"], b * (2 * E * M) + (2 * e + c) * M + m + 1)
                                nc.scalar.activation(HID[c][:, m, :], bank(c, 1 + m % 2), ACT.Relu,
                                                     bias=col("moe_b1", e * M + m)).then_inc(cs["relu"], 1)
                        for c in range(2):
                            act.wait_ge(cs["moe_y"], b * (2 * E) + 2 * e + c + 1)
                            if e:
                                act.wait_ge(cs["masked"], b * (2 * E) + 2 * (e - 1) + c + 1)
                            nc.scalar.activation(MOE_Y[c], bank(c, 3), ACT.Identity,
                                                 bias=col("moe_b2", e)).then_inc(cs["moe_y_sb"], 1)
                    norm_act(act, ln, lnv(4))
                    norm_act(act, ln, lnv(5), twice=True)
                    for o in range(2 * CI):
                        for c in range(2):
                            act.wait_ge(cs["inp"], b * (4 * CI) + 2 * o + c + 1)
                            if o < CI:
                                at = KC - 1 + c * CH
                                ins = nc.scalar.copy(CONV[:, o, at:at + CH], bank(c, 1 + o % 2))
                            else:
                                ins = nc.scalar.activation(SZ[o - CI][:, c * CH:(c + 1) * CH], bank(c, 1 + o % 2), ACT.Silu)
                            ins.then_inc(cs["in_sb"], 1)
                    for c in range(2):
                        for i in range(CI):
                            act.wait_ge(cs["tap"], b * 16 + c * 8 + 2 * (KC - 1) + i + 1)
                            nc.scalar.activation(U[i][:, c * CH:(c + 1) * CH], CV[c][i], ACT.Silu).then_inc(cs["u"], 1)
                    act.preload_act_table_set("natural_log_exp_and_others")
                    for c in range(2):
                        act.wait_ge(cs["xp"], n + c)
                        nc.scalar.copy(DT[c], bank(c, 1)[0:DR, :]).then_inc(cs["dt"], 1)
                    for c in range(2):
                        act.wait_ge(cs["dtp"], n + c)
                        for i in range(CI):
                            k = b * 4 + 2 * c + i + 1
                            nc.scalar.activation(SP1[c][i], bank(c, 1 + 2 * i), ACT.Abs,
                                                 bias=col("dt_b", i)).then_inc(cs["sp_abs"], 1)
                            if c:
                                act.wait_ge(cs["dl"], b * 4 + i + 1)
                            nc.scalar.activation(SP2[i], bank(c, 1 + 2 * i), ACT.Relu, bias=col("dt_b", i))
                            act.wait_ge(cs["sp_abs"], k)
                            nc.scalar.activation(SP1[c][i], SP1[c][i], ACT.Exp, scale=-1.0).then_inc(cs["sp_exp"], 1)
                            act.wait_ge(cs["sp_exp"], k)
                            nc.scalar.activation(SP1[c][i], SP1[c][i], ACT.Ln, bias=1.0).then_inc(cs["sp"], 1)
                    act.wait_ge(cs["du"], b * 4 + 4)
                    for k in range(DS):
                        for i in range(CI):
                            if k:
                                act.wait_ge(cs["state"], b * (DS * CI) + 2 * (k - 1) + i + 1)
                            nc.scalar.activation(DA[i], DL[i], ACT.Exp,
                                                 scale=a_neg[:, i * DS + k:i * DS + k + 1]).then_inc(cs["da"], 1)
                        act.wait_ge(cs["c_row"], b * DS + k + 1)
                        if k >= 2:
                            act.wait_ge(cs["hc"], b * (DS * CI) + 2 * (k - 2) + 2)
                        nc.scalar.copy(CR[k % 2], ps[:, 2:4, :].rearrange("p a n -> p (a n)")).then_inc(cs["c_sb"], 1)
                    norm_act(act, ln, lnv(6))
                    norm_act(act, ln, lnv(7))
                    qkv_act(act, qs, n, False)
                    for c in range(2):
                        nc.scalar.activation(SQ[c], QK32[c][:, 0, :], ACT.Square).then_inc(cs["q_sq"], 1)
                    for c in range(2):
                        act.wait_ge(cs["sim_parts"], n + c)
                        nc.scalar.activation(RSTD[c][0:H, :], bank(c, 0)[0:H, :], ACT.Ln).then_inc(cs["sim_log"], 1)
                        act.wait_ge(cs["sim_log"], n + c)
                        nc.scalar.activation(RSTD[c][0:H, :], RSTD[c][0:H, :], ACT.Exp, scale=-0.5).then_inc(cs["sim_inv"], 1)

            @block.vector
            def _(dve):
                with dve.Fori(0, B) as b:
                    n = b * 2 + 1

                    def lnv(i):
                        return b * (2 * NLN) + 2 * i + 1

                    for c in range(2):
                        dve.wait_ge(cs["att"], n + c)
                        nc.vector.tensor_scalar(CTX[c], bank(c, 1), col("out_b"), None, ALU.add).then_inc(cs["ctx"], 1)
                        dve.wait_ge(cs["ctx"], n + c)
                        nc.vector.tensor_tensor(XA[c], CTX[c], h0[:, cols_of(b, c)], ALU.add).then_inc(cs["xa"], 1)
                    norm_dve(dve, ln, lnv(0), XA, XS, "g1", "b1")
                    for s in range(STEPS):
                        k = b * (2 * STEPS) + 2 * s + 1
                        for c in range(2):
                            dve.wait_ge(cs["tanh"], k + c)
                            if s:
                                dve.wait_ge(cs["drag"], b * (2 * STEPS - 2) + 2 * s - 1 + c)
                                ins = nc.vector.tensor_tensor(GV[c], CW[c], TT_[c], ALU.add)
                            else:
                                ins = nc.vector.tensor_tensor(GV[c], TT_[c], XS[c], ALU.subtract)
                            ins.then_inc(cs["vel"], 1)
                            dve.wait_ge(cs["vel"], k + c)
                            nc.vector.scalar_tensor_tensor(out=XS[c], in0=GV[c], scalar=0.01, in1=XS[c], op0=ALU.mult,
                                                           op1=ALU.add).then_inc(cs["xs"], 1)
                        if s + 1 < STEPS:
                            for c in range(2):
                                dve.wait_ge(cs["xs"], k + c)
                                nc.vector.scalar_tensor_tensor(out=CW[c], in0=GV[c], scalar=0.9, in1=XS[c], op0=ALU.mult,
                                                               op1=ALU.subtract).then_inc(cs["drag"], 1)
                    for c in range(2):
                        dve.wait_ge(cs["xs"], b * (2 * STEPS) + 2 * STEPS - 1 + c)
                        nc.vector.tensor_tensor(XA[c], XA[c], XS[c], ALU.add).then_inc(cs["xa2"], 1)
                    norm_dve(dve, ln, lnv(1), XA, NRM, "g2", "b2")
                    for c in range(2):
                        dve.wait_ge(cs["ffy"], n + c)
                        nc.vector.scalar_tensor_tensor(out=XA[c], in0=bank(c, 3), scalar=col("ff_b2"), in1=XA[c],
                                                       op0=ALU.add, op1=ALU.add).then_inc(cs["xa3"], 1)
                    norm_dve(dve, ln, lnv(2), XA, NRM)
                    for c in range(2):
                        dve.wait_ge(ln["out"], lnv(2) + c)
                        nc.vector.tensor_tensor(XR[c], NRM[c], x_res[:, cols_of(b, c)], ALU.add).then_inc(cs["xr1"], 1)
                    norm_dve(dve, ln, lnv(3), XR, NRM)
                    for c in range(2):
                        dve.wait_ge(cs["gates"], n + c)
                        nc.vector.tensor_tensor(small[:, c, 0:32], bank(c, 1)[:, 0:32], w["bg"][:, :],
                                                ALU.add).then_inc(cs["g_sb"], 1)
                        dve.wait_ge(cs["g_sb"], n + c)
                        nc.vector.tensor_reduce(gmax[c], gate(c, 0), AX.X, ALU.max).then_inc(cs["g_max"], 1)
                        dve.wait_ge(cs["g_max"], n + c)
                        for t in range(4):
                            ins = nc.vector.tensor_scalar(gate(c, 1)[:, t, :], gate(c, 0)[:, t, :], gmax[c][:, t:t + 1], None,
                                                          ALU.is_lt)
                        ins.then_inc(cs["g_less"], 1)
                        dve.wait_ge(cs["g_less"], n + c)
                        nc.vector.scalar_tensor_tensor(out=gate(c, 2), in0=gate(c, 1), scalar=float(E), in1=iota[:, :, :],
                                                       op0=ALU.mult, op1=ALU.add).then_inc(cs["g_cand"], 1)
                        dve.wait_ge(cs["g_cand"], n + c)
                        nc.vector.tensor_reduce(gmin[c], gate(c, 2), AX.X, ALU.min).then_inc(cs["g_min"], 1)
                        dve.wait_ge(cs["g_min"], n + c)
                        for t in range(4):
                            ins = nc.vector.tensor_scalar(gate(c, 3)[:, t, :], iota[:, t, :], gmin[c][:, t:t + 1], None,
                                                          ALU.is_equal)
                        ins.then_inc(cs["onehot"], 1)
                    for c in range(2):
                        dve.wait_ge(cs["oh_turned"], n + c)
                        nc.vector.tensor_copy(onehot_b[:, c, :], bank(c, 2)[0:E, :]).then_inc(cs["oh_b"], 1)
                    for e in range(E):
                        for c in range(2):
                            k = b * (2 * E) + 2 * e + c + 1
                            dve.wait_ge(cs["moe_y_sb"], k)
                            dve.wait_ge(cs["mask"], k)
                            dst = TT_[c] if e else ACC[c]
                            nc.vector.tensor_tensor(dst, MOE_Y[c], bank(c, 0), ALU.mult).then_inc(cs["masked"], 1)
                            if e:
                                dve.wait_ge(cs["masked"], k)
                                nc.vector.tensor_tensor(ACC[c], ACC[c], TT_[c], ALU.add).then_inc(cs["acc"], 1)
                    norm_dve(dve, ln, lnv(4), ACC, NRM)
                    for c in range(2):
                        dve.wait_ge(ln["out"], lnv(4) + c)
                        nc.vector.tensor_tensor(XR[c], XR[c], NRM[c], ALU.add).then_inc(cs["xr2"], 1)
                    norm_dve(dve, ln, lnv(5), XR, NRM, "norm_w", "norm_b")
                    nc.vector.memset(CONV[:, :, 0:KC - 1], 0.0).then_inc(cs["pad"], 1)
                    dve.wait_ge(cs["pad"], b + 1)
                    for c in range(2):
                        for tap in range(KC):
                            for i in range(CI):
                                k = b * 16 + c * 8 + 2 * tap + i + 1
                                src = CONV[:, i, c * CH + tap:c * CH + tap + CH]
                                if tap == 0:
                                    dve.wait_ge(cs["in_sb"], b * (4 * CI) + 2 * i + c + 1)
                                    ins = nc.vector.tensor_scalar(CV[c][i], src, col("conv_w", i * KC), col("conv_b", i),
                                                                  ALU.mult, ALU.add)
                                else:
                                    dve.wait_ge(cs["tap"], k - 2)
                                    ins = nc.vector.scalar_tensor_tensor(out=CV[c][i], in0=src, scalar=col("conv_w", i * KC + tap),
                                                                         in1=CV[c][i], op0=ALU.mult, op1=ALU.add)
                                ins.then_inc(cs["tap"], 1)
                    for c in range(2):
                        dve.wait_ge(cs["xp"], n + c)
                        rows = slice(0, 6 * DS)
                        nc.vector.tensor_copy(B_HI[c], bank(c, 2)[rows, :]).then_inc(cs["bc_hi"], 1)
                        dve.wait_ge(cs["bc_hi"], n + c)
                        nc.vector.scalar_tensor_tensor(out=B_REST[c], in0=B_HI[c], scalar=col("part12")[rows, :],
                                                       in1=bank(c, 2)[rows, :], op0=ALU.mult, op1=ALU.add).then_inc(cs["bc_rest"], 1)
                        dve.wait_ge(cs["bc_rest"], n + c)
                        nc.vector.tensor_copy(B_MID[c], B_REST[c]).then_inc(cs["bc_mid"], 1)
                        dve.wait_ge(cs["bc_mid"], n + c)
                        nc.vector.scalar_tensor_tensor(out=bc_parts[:, c * CH:(c + 1) * CH], in0=B_MID[c],
                                                       scalar=col("part2")[rows, :], in1=B_REST[c], op0=ALU.mult,
                                                       op1=ALU.add).then_inc(cs["bc"], 1)
                    for c in range(2):
                        at = slice(c * CH, (c + 1) * CH)
                        for i in range(CI):
                            k = b * 4 + 2 * c + i + 1
                            dve.wait_ge(cs["sp"], k)
                            nc.vector.tensor_tensor(DL[i][:, at], SP1[c][i], SP2[i], ALU.add).then_inc(cs["dl"], 1)
                            dve.wait_ge(cs["dl"], k)
                            nc.vector.tensor_tensor(DU[i][:, at], DL[i][:, at], U[i][:, at], ALU.mult).then_inc(cs["du"], 1)
                    b_rows = ps[:, 0:2, :].rearrange("p a n -> p (a n)")
                    for k in range(DS):
                        at = b * (DS * CI) + 2 * k + 1
                        for i in range(CI):
                            if k == 0:
                                dve.wait_ge(cs["du"], b * 4 + 4)
                            dve.wait_ge(cs["b_row"], b * DS + k + 1)
                            if k:
                                dve.wait_ge(cs["state"], at - 2 + i)
                            nc.vector.tensor_tensor(DBU[i], DU[i], b_rows, ALU.mult).then_inc(cs["dbu"], 1)
                        for i in range(CI):
                            dve.wait_ge(cs["da"], at + i)
                            dve.wait_ge(cs["dbu"], at + i)
                            if k >= 2:
                                dve.wait_ge(cs["hc"], at - 4 + i)
                            nc.vector.tensor_tensor_scan(HS[k % 2][i], DA[i], DBU[i], 0.0, ALU.mult, ALU.add).then_inc(cs["state"], 1)
                    dve.wait_ge(cs["y_sum"], b * (DS * CI) + DS * CI)
                    for c in range(2):
                        at = slice(c * CH, (c + 1) * CH)
                        for i in range(CI):
                            nc.vector.scalar_tensor_tensor(out=YT[i][:, at], in0=U[i][:, at], scalar=col("D_param", i),
                                                           in1=ps[:, 4 + 2 * i + c, :], op0=ALU.mult,
                                                           op1=ALU.add).then_inc(cs["yy"], 1)
                        for i in range(CI):
                            dve.wait_ge(cs["yy"], b * 4 + 2 * c + i + 1)
                            nc.vector.tensor_tensor(YT[i][:, at], YT[i][:, at], SZ[i][:, at], ALU.mult).then_inc(cs["yg"], 1)
                    for c in range(2):
                        dve.wait_ge(cs["op"], n + c)
                        nc.vector.tensor_copy(TT_[c], bank(c, 1)).then_inc(cs["ao"], 1)
                    norm_dve(dve, ln, lnv(6), TT_, NRM)
                    for c in range(2):
                        dve.wait_ge(ln["out"], lnv(6) + c)
                        nc.vector.tensor_tensor(XR[c], XR[c], NRM[c], ALU.add).then_inc(cs["xr3"], 1)
                    norm_dve(dve, ln, lnv(7), XR, XN)
                    qkv_dve(dve, qs, n, b, False)
                    for c in range(2):
                        dve.wait_ge(cs["sim_inv"], n + c)
                        nc.vector.tensor_tensor(SIM16[c], bank(c, 1)[0:H, :], RSTD[c][0:H, :], ALU.mult).then_inc(cs["sim_prod"], 1)
                    for c in range(2):
                        dve.wait_ge(cs["sim"], n + c)
                        nc.vector.tensor_scalar(h0[:, cols_of(b, c)], bank(c, 2), 1.0, None, ALU.mult).then_inc(cs["sim_kept"], 1)
                    dve.wait_ge(cs["kept"], n + 1)

            @block.gpsimd
            def _(pool):
                with pool.Fori(0, B) as b:
                    for k in range(DS):
                        at = b * (DS * CI) + 2 * k + 1
                        pool.wait_ge(cs["c_sb"], b * DS + k + 1)
                        for i in range(CI):
                            pool.wait_ge(cs["state"], at + i)
                            if k:
                                pool.wait_ge(cs["y_sum"], at - 2 + i)
                            nc.gpsimd.tensor_tensor(HC[i], HS[k % 2][i], CR[k % 2], ALU.mult).then_inc(cs["hc"], 1)
                    for c in range(2):
                        pool.wait_ge(cs["xr3"], b * 2 + c + 1)
                        nc.gpsimd.tensor_copy(x_res[:, cols_of(b, c)], XR[c]).then_inc(cs["kept"], 1)

        end_phase()

        d_chain, d_rows, d_stored = sem("d_chain"), sem("d_rows"), sem("d_stored")
        lim = small[:, 0, 0:4]
        rows_bf = [work[:, 2 * k:2 * k + 2, :].rearrange("p a n -> p (a n)").bitcast(BF16) for k in range(4)]
        with nc.Block() as block:
            @block.vector
            def _(dve):
                count = [0]

                def link(ins):
                    count[0] += 1
                    ins.then_inc(d_chain, 1)
                    dve.wait_ge(d_chain, count[0])

                sims = h0[:, :].rearrange("p (b n) -> p b n", b=B)
                link(nc.vector.tensor_reduce(lim[:, 0:1], sims[:, :, REG:S], AX.XY, ALU.min))
                link(nc.vector.tensor_reduce(lim[:, 1:2], sims[:, :, REG:S], AX.XY, ALU.max))
                link(nc.vector.tensor_tensor(lim[:, 2:3], lim[:, 1:2], lim[:, 0:1], ALU.subtract))
                link(nc.vector.reciprocal(lim[:, 3:4], lim[:, 2:3]))
                link(nc.vector.tensor_scalar(h0[:, :], h0[:, :], lim[:, 0:1], lim[:, 3:4], ALU.subtract, ALU.mult))
                link(nc.vector.tensor_scalar(h0[:, :], h0[:, :], 0.9, None, ALU.is_gt))
                for k, (mul, add, reg) in enumerate(((1.0, 0.0, 1.0), (-1.0, 1.0, 0.0), (-NEG, NEG, 0.0), (NEG, 0.0, 0.0))):
                    link(nc.vector.tensor_scalar(rows_bf[k][0:H, :], h0[0:H, :], mul, add, ALU.mult, ALU.add))
                    nc.vector.memset(rows_bf[k][0:H, :].rearrange("p (b n) -> p b n", b=B)[:, :, 0:REG],
                                     reg).then_inc(d_rows, 1)

            @block.sync
            def _(sp):
                sp.wait_ge(d_rows, 4)
                for k, (dram, row) in enumerate(((scratch_q, R_MASK), (scratch_q, R_MASK + 1), (scratch_k, R_MASK),
                                                 (scratch_k, R_MASK + 1))):
                    for b in range(B):
                        sp.dma_start(dram[b * H:(b + 1) * H, row, :], rows_bf[k][0:H, b * S:(b + 1) * S]).then_inc(d_stored, 16)
                sp.wait_ge(d_stored, 16 * 4 * B)

        end_phase()
        run_attention("e", False)
        end_phase()

        fs = {k: sem("f_" + k) for k in ("reg_sum", "reg", "proj", "ao", "xr", "turned", "y_sb", "trip_end")}
        f_norm = norm_sems("f_norm")
        f_ol = [sem(f"f_ol{c}") for c in range(2)]
        f_out = [sem(f"f_out{c}") for c in range(2)]
        f_ox = sem("f_ox")
        OX = work[:, 19, 0:4 * XQ].rearrange("p (g n) -> p g n", g=4)
        YO = [work[:, 20, c * CH:(c + 1) * CH] for c in range(2)]
        out_rows = out.rearrange("b (t p) f -> (b t) p f", p=P)
        with nc.Block() as block:
            @block.sync
            def _(sp):
                with sp.Fori(0, B) as b:
                    sp.wait_ge(fs["trip_end"], b + 1)
                    sp.dma_start(OX, scratch_x.rearrange("b g p n -> b p g n")[b, :, :, :]).then_inc(f_ox, 16)
                    for c in range(2):
                        src = scratch_o.rearrange("b g p n -> b p g n")[b, :, :, c * CH:(c + 1) * CH]
                        sp.dma_start(OL[c], src).then_inc(f_ol[c], 16)
                    for c in range(2):
                        sp.wait_ge(fs["y_sb"], b * 2 + c + 1)
                        sp.dma_start(out_rows[bass.ds(b * QT + 4 * c, 4), :, :].rearrange("t p f -> p t f"),
                                     YO[c].rearrange("p (t f) -> p t f", t=4)).then_inc(f_out[c], 16)
                for c in range(2):
                    sp.wait_ge(f_out[c], 16 * B)

            @block.tensor
            def _(pe):
                with pe.Fori(0, B) as b:
                    n = b * 2 + 1
                    for c in range(2):
                        pe.wait_ge(f_ol[c], b * 16 + 16)
                        if c == 0:
                            pe.wait_ge(fs["reg"], b + 1)
                        for g in range(H // GH):
                            mm = nc.tensor.matmul(bank(c, 1), w["proj_w"][:, g, :], OL[c][:, g, :], start=(g == 0),
                                                  stop=(g == H // GH - 1))
                        mm.then_inc(fs["proj"], 1)
                    norm_pe(pe, f_norm, n, XA, lambda e, c: e.wait_ge(fs["ao"], n + c))
                    for c in range(2):
                        pe.wait_ge(fs["xr"], n + c)
                        for t in range(CH // P):
                            mm = nc.tensor.transpose(bank(c, 2)[:, t * P:(t + 1) * P], XR[c][:, t * P:(t + 1) * P],
                                                     w["ident"][:, :])
                        mm.then_inc(fs["turned"], 1)

            @block.scalar
            def _(act):
                act.preload_act_table_set("natural_log_exp_and_others")
                with act.Fori(0, B) as b:
                    norm_act(act, f_norm, b * 2 + 1)
                    for c in range(2):
                        act.wait_ge(fs["turned"], b * 2 + c + 1)
                        nc.scalar.copy(YO[c], bank(c, 2)).then_inc(fs["y_sb"], 1)

            @block.vector
            def _(dve):
                dve.sem_inc(fs["trip_end"], 1)
                with dve.Fori(0, B) as b:
                    n = b * 2 + 1
                    dve.wait_ge(f_ol[0], b * 16 + 16)
                    dve.wait_ge(f_ox, b * 16 + 16)
                    nc.vector.tensor_tensor(OX[:, :, 0:REG], OX[:, :, 0:REG], OL[0][:, :, 0:REG], ALU.add).then_inc(fs["reg_sum"], 1)
                    dve.wait_ge(fs["reg_sum"], b + 1)
                    nc.vector.tensor_scalar(OL[0][:, :, 0:REG], OX[:, :, 0:REG], 0.5, None, ALU.mult).then_inc(fs["reg"], 1)
                    for c in range(2):
                        dve.wait_ge(fs["proj"], n + c)
                        nc.vector.tensor_scalar(XA[c], bank(c, 1), col("proj_b"), None, ALU.add).then_inc(fs["ao"], 1)
                    norm_dve(dve, f_norm, n, XA, NRM)
                    for c in range(2):
                        dve.wait_ge(f_norm["out"], n + c)
                        nc.vector.tensor_tensor(XR[c], NRM[c], x_res[:, cols_of(b, c)], ALU.add).then_inc(fs["xr"], 1)
                    for c in range(2):
                        dve.wait_ge(f_out[c], b * 16 + 16)
                    dve.sem_inc(fs["trip_end"], 1)

def kernel(**inputs):
    import numpy as np
    import concourse.bacc as _bacc
    from concourse.bass_utils import run_bass_kernel_spmd as _run

    x = {k: np.asarray(v) for k, v in inputs.items()}
    f32, bf16 = np.float32, mybir.dt.np(BF16)

    def vec(v):
        return v.reshape(-1, P).T

    def padded_heads(weight):
        m = np.zeros((H // GH, GH, 32, weight.shape[1]), f32)
        m[:, :, 0:HD] = weight.reshape(H // GH, GH, HD, -1)
        return np.ascontiguousarray(m.reshape(H // GH, P, -1).transpose(1, 0, 2))

    rows = np.arange(6 * DS)
    part = lambda n: np.pad((rows >= n * 2 * DS).astype(f32), (0, P - 6 * DS)).reshape(1, P)
    columns = {
        "q_b": vec(x["L0_attn_qkv_b"][0:D]), "k_b": vec(x["L0_attn_qkv_b"][D:2 * D]), "out_b": vec(x["L0_attn_out_b"]),
        "g_attn": vec(x["L0_attn_g_attn"]), "b_attn": vec(x["L0_attn_b_attn"]), "g1": vec(x["L0_attn_g1"]),
        "b1": vec(x["L0_attn_b1"]), "g2": vec(x["L0_attn_g2"]), "b2": vec(x["L0_attn_b2"]),
        "b_inl": vec(x["L0_attn_b_inl"]), "ff_b1": vec(x["L0_attn_ff_b1"]), "ff_b2": vec(x["L0_attn_ff_b2"]),
        "moe_b1": vec(x["L0_ffn_b1"]), "moe_b2": vec(x["L0_ffn_b2"]), "norm_w": vec(x["L1_attn_norm_w"]),
        "norm_b": vec(x["L1_attn_norm_b"]),
        "conv_w": x["L1_attn_conv_w"].reshape(CI, P, KC).transpose(1, 0, 2).reshape(P, -1),
        "conv_b": vec(x["L1_attn_conv_b"]), "dt_b": vec(x["L1_attn_dt_proj_b"]),
        "A_log": x["L1_attn_A_log"].reshape(CI, P, DS).transpose(1, 0, 2).reshape(P, -1),
        "D_param": vec(x["L1_attn_D_param"]), "q_gate": vec(x["L1_ffn_g_info"][0, 0]), "proj_b": vec(x["L1_ffn_b_proj"]),
        "part12": -part(1).T, "part2": -part(2).T,
    }
    for name, (_, n) in COLS.items():
        assert columns[name].shape == (P, n), name
    eye = np.eye(P, dtype=f32)
    q = np.arange(P)
    head = (q[:, None] // HD == np.arange(H)[None, :]).astype(f32)
    den = np.zeros((P, P), f32)
    den[q // 32 * 32 + HD, q] = 1.0
    bc = x["L1_attn_x_proj_w"][:, DR:].reshape(CI, P, 2 * DS).transpose(1, 0, 2)
    arrays = {
        "x": x["L0_attn_x"].reshape(B * QT, P, D),
        "cols": np.concatenate([columns[name] for name in COLS], axis=1),
        "qkv_w": x["L0_attn_qkv_w"], "v_bias": np.tile(x["L0_attn_qkv_b"][2 * D:], (P, CH // D)),
        "out_w": padded_heads(x["L0_attn_out_w"]), "w_ctx": x["L0_attn_w_ctx"], "w_x": x["L0_attn_w_x"],
        "ff_w1": x["L0_attn_ff_w1"], "ff_w2": x["L0_attn_ff_w2"].reshape(FF // P, P, D).transpose(1, 0, 2),
        "Wg": x["L0_ffn_Wg"], "bg": np.tile(x["L0_ffn_bg"], (P, CH // P)), "W1": x["L0_ffn_W1"].transpose(1, 0, 2),
        "W2": x["L0_ffn_W2"].reshape(E, FF // P, P, D).transpose(2, 0, 1, 3), "in_proj_w": x["L1_attn_in_proj_w"],
        "x_proj_dt": x["L1_attn_x_proj_w"][:, 0:DR].reshape(CI, P, DR).transpose(1, 0, 2),
        "x_proj_bc": np.concatenate([bc, bc, bc], axis=2), "dt_proj_w": x["L1_attn_dt_proj_w"],
        "out_proj_w": x["L1_attn_out_proj_w"].reshape(CI, P, D).transpose(1, 0, 2),
        "qkv2_w": x["L1_ffn_W_qkv"], "proj_w": padded_heads(x["L1_ffn_W_proj"]),
        "ident": eye, "mean_w": np.full((P, P), 1.0 / D, f32), "den_sel": den, "head_sel": head, "head_back": head.T,
        "sim_sum": np.full((H, P), 1.0 / H, f32), "iota": np.broadcast_to(np.arange(E, dtype=f32), (P, CH // P, E)),
        "ident_b": eye.astype(bf16), "mask_qk": np.where(q[None, :] > q[:, None], NEG, 0.0).astype(bf16),
        "mask_kq": np.where(q[:, None] > q[None, :], NEG, 0.0).astype(bf16),
        "exp_sel": np.repeat(np.eye(E, dtype=f32)[:, :, None], P, axis=2).astype(bf16),
        "bc_sel": np.repeat((rows[:, None] % (2 * DS) == np.arange(2 * DS)[None, :])[:, :, None], P, axis=2).astype(bf16),
        "x_rows": np.repeat(np.array([[0.0], [1.0]], f32), XQ, axis=1).astype(bf16),
    }
    arrays = {k: np.ascontiguousarray(v) for k, v in arrays.items()}
    nc = _bacc.Bacc("TRN2", target_bir_lowering=False, num_devices=1)
    handles = {k: nc.dram_tensor(f"in_{k}", v.shape, mybir.dt.from_np(v.dtype), kind="ExternalInput").ap()
               for k, v in arrays.items()}
    out = nc.dram_tensor("out_0", (B, S, D), F32, kind="ExternalOutput").ap()
    build(nc, handles, out)
    r = _run(nc, [{f"in_{k}": v for k, v in arrays.items()}], core_ids=[0])
    return r.results[0]["out_0"]
```

```python
from contextlib import ExitStack

import concourse.bass as bass
from concourse import mybir

F32 = mybir.dt.float32
BF16 = mybir.dt.bfloat16
ALU = mybir.AluOpType
ACT = mybir.ActivationFunctionType
AX = mybir.AxisListType

P = 128
B, S, D = 4, 1024, 128
CH = 512
H, HD = 16, 8
SCALE = float(HD) ** -0.5
GH = 4
GROUPS = B * H // GH
SLOTS_Q = (0, 0, 0, 1, 1, 2)
SLOTS_K = (0, 1, 2, 0, 1, 0)
NS = len(SLOTS_Q)
R_MASK = NS * HD
HR = R_MASK + 2
R_MAX = 2 * HR
R_END = R_MAX + 3
NEG = -1.0e30
QT = S // P
REG = 5
XQ = 32
FF = 512
E = 8
DI, DS, DR, KC = 256, 16, 64, 4
CI = DI // P
STEPS = 8
EPS = 1e-5

COLS = {}
for _name, _n in (("q_b", 1), ("k_b", 1), ("out_b", 1), ("g_attn", 1), ("b_attn", 1), ("g1", 1), ("b1", 1),
                  ("g2", 1), ("b2", 1), ("b_inl", 1), ("ff_b1", FF // P), ("ff_b2", 1), ("moe_b1", E * FF // P),
                  ("moe_b2", E), ("norm_w", 1), ("norm_b", 1), ("conv_w", CI * KC), ("conv_b", CI), ("dt_b", CI),
                  ("A_log", CI * DS), ("D_param", CI), ("q_gate", 1), ("proj_b", 1), ("part12", 1), ("part2", 1),
                  ("mask_mul", 1), ("mask_add", 1), ("mask_reg", 1)):
    COLS[_name] = (sum(n for _, n in COLS.values()), _n)
NCOLS = sum(n for _, n in COLS.values())


def build(nc, a, out):
    scratch_q = nc.dram_tensor("scratch_q", [B * H, HR, S], BF16).ap()
    scratch_k = nc.dram_tensor("scratch_k", [B * H, HR, S], BF16).ap()
    scratch_o = nc.dram_tensor("scratch_o", [B, H // GH, P, S], F32).ap()
    scratch_x = nc.dram_tensor("scratch_x", [B, H // GH, P, XQ], F32).ap()
    heads_o, heads_x = (t.rearrange("b g (j r) n -> b (g j) r n", r=32)[:, :, 0:HD, :] for t in (scratch_o, scratch_x))

    with ExitStack() as ctx:
        def sb(name, shape, dt=F32):
            return ctx.enter_context(nc.sbuf_tensor(name, shape, dt))

        phase_sems = []

        def sem(name):
            phase_sems.append(nc.alloc_semaphore(name))
            return phase_sems[-1]

        def end_phase():
            nc.clear_and_free_semaphores(phase_sems)
            phase_sems.clear()
            nc.all_engine_barrier()

        x_res = sb("x_res", [P, B * S])
        h0 = sb("h0", [P, B * S])
        v_tok = sb("v_tok", [P, B * QT * D])
        w = {}
        for name, shape, dt in (
                ("cols", [P, NCOLS], F32), ("qkv_w", [P, 3 * D], F32), ("v_bias", [P, CH], F32),
                ("out_w", [P, D], F32), ("w_ctx", [P, D], F32), ("w_x", [P, D], F32),
                ("ff_w1", [P, FF], F32), ("ff_w2", [P, FF // P, D], F32), ("Wg", [P, E], F32), ("bg", [P, CH // P * E], F32),
                ("W1", [P, E, FF], F32), ("W2", [P, E, FF // P, D], F32), ("in_proj_w", [P, 2 * DI], F32),
                ("x_proj_dt", [P, CI, DR], F32), ("x_proj_bc", [P, CI, 3 * 2 * DS], F32), ("dt_proj_w", [DR, DI], F32),
                ("out_proj_w", [P, CI, D], F32), ("qkv2_w", [P, 3 * D], F32), ("proj_w", [P, D], F32),
                ("ident", [P, P], F32), ("mean_w", [P, P], F32), ("den_sel", [P, P], F32),
                ("head_sel", [P, H], F32), ("head_back", [H, P], F32), ("sim_sum", [H, P], F32), ("iota", [P, CH // P, E], F32),
                ("ident_b", [P, P], BF16), ("mask_qk", [P, P], BF16), ("mask_kq", [P, P], BF16),
                ("exp_sel", [E, E, P], BF16), ("bc_sel", [6 * DS, 2 * DS, P], BF16)):
            w[name] = sb("w_" + name, shape, dt)

        def col(name, i=0):
            at = COLS[name][0] + i
            return w["cols"][:, at:at + 1]

        eps_col = sb("eps_col", [P, 2])
        a_neg = sb("a_neg", [P, CI * DS])
        q_gate_sel = sb("q_gate_sel", [P, H])
        gate_tmp = sb("gate_tmp", [P, 4])
        bc_parts = sb("bc_parts", [6 * DS, S], BF16)
        m_cat = sb("m_cat", [P, 2, 40])
        m_col = sb("m_col", [P, P])
        m_neg = sb("m_neg", [40, 2, P])
        m_parts = sb("m_parts", [40, 3, 3, P], BF16)
        small = sb("small", [P, 2, 160])
        onehot_b = sb("onehot_b", [E, 2, CH], BF16)
        NWK = 21
        work = sb("work", [P, NWK, S])

        ps = ctx.enter_context(nc.psum_tensor("ps", [P, 8, CH], F32))

        def chunks(slot):
            return [work[:, slot, c * CH:(c + 1) * CH] for c in range(2)]

        def bank(c, i):
            return ps[:, 4 * c + i, :]

        XR, DEV, SQ, RSTD, NRM = (chunks(i) for i in range(5))
        CTX, XA, XS, CW, GV, TT_ = (chunks(i) for i in range(5, 11))
        OL = chunks(15)
        HID = [work[:, 15 + 2 * c:17 + 2 * c, :].rearrange("p a n -> p (a n)").rearrange("p (m n) -> p m n", m=4)
               for c in range(2)]
        XIN = [work[:, 12, c * CH:(c + 1) * CH].rearrange("p (t f) -> p t f", t=4) for c in range(2)]
        QK32 = [work[:, 5 + c, :].rearrange("p (a n) -> p a n", a=2) for c in range(2)]
        REST = [work[:, 7 + c, :].rearrange("p (a n) -> p a n", a=2) for c in range(2)]
        def parts_at(slot):
            return [work[:, slot:slot + 3, :].rearrange("p a n -> p (a n)")[:, 1536 * c:1536 * (c + 1)].bitcast(BF16)
                    .rearrange("p (t a n) -> p t a n", t=3, a=2) for c in range(2)]

        PARTS = parts_at(9)
        MOE_Y, ACC = chunks(5), chunks(6)
        XN = chunks(13)
        CONV = work[:, 17:20, :].rearrange("p a n -> p (a n)")[:, 0:CI * (KC - 1 + S)].rearrange("p (i n) -> p i n", i=CI)

        def norm_sems(tag):
            return {k: sem(f"{tag}_{k}") for k in ("mean", "centred", "squared", "var", "log", "rstd", "out", "affine")}

        pair = (DEV, SQ, RSTD, [bank(c, 0) for c in range(2)])

        def norm_pe(pe, s, n, src, ready, tiles=pair):
            _, sq, _, stat = tiles
            for c in range(len(sq)):
                ready(pe, c)
                nc.tensor.matmul(stat[c], w["mean_w"][:, :], src[c], start=True, stop=True).then_inc(s["mean"], 1)
            for c in range(len(sq)):
                pe.wait_ge(s["squared"], n + c)
                nc.tensor.matmul(stat[c], w["mean_w"][:, :], sq[c], start=True, stop=True).then_inc(s["var"], 1)

        def norm_act(act, s, n, twice=False, both=None, tiles=pair):
            dev, sq, rstd, stat = tiles
            for c in range(len(dev)):
                act.wait_ge(s["centred"], n + c)
                nc.scalar.activation(sq[c], dev[c], ACT.Square).then_inc(s["squared"], 1)
            for c in range(len(dev)):
                act.wait_ge(s["var"], n + c)
                if both:
                    nc.scalar.activation(both[c], stat[c], ACT.Ln, bias=eps_col[:, 1:2],
                                         scale=1.0 + EPS).then_inc(s["log2"], 1)
                    act.wait_ge(s["log2"], n + c)
                    nc.scalar.activation(both[c], both[c], ACT.Exp, scale=-0.5).then_inc(s["rstd2"], 1)
                bias, scale = (eps_col[:, 1:2], 1.0 + EPS) if twice else (eps_col[:, 0:1], 1.0)
                nc.scalar.activation(rstd[c], stat[c], ACT.Ln, bias=bias, scale=scale).then_inc(s["log"], 1)
                act.wait_ge(s["log"], n + c)
                nc.scalar.activation(rstd[c], rstd[c], ACT.Exp, scale=-0.5).then_inc(s["rstd"], 1)

        def norm_dve(dve, s, n, src, dst, gain=None, shift=None, tiles=pair):
            dev, _, rstd, stat = tiles
            for c in range(len(dev)):
                dve.wait_ge(s["mean"], n + c)
                nc.vector.tensor_tensor(dev[c], src[c], stat[c], ALU.subtract).then_inc(s["centred"], 1)
            for c in range(len(dev)):
                dve.wait_ge(s["rstd"], n + c)
                nc.vector.tensor_tensor(dst[c], dev[c], rstd[c], ALU.mult).then_inc(s["out"], 1)
                if gain:
                    dve.wait_ge(s["out"], n + c)
                    nc.vector.tensor_scalar(dst[c], dst[c], col(gain), col(shift), ALU.mult,
                                            ALU.add).then_inc(s["affine"], 1)

        def qkv_sems(tag):
            d = {k: sem(f"{tag}_{k}") for k in ("qk", "v", "qk_sb", "part1", "rest", "part2", "part3", "v_kept")}
            return d

        def qkv_pe(pe, s, n, weights, src, ready):
            for c in range(2):
                ready(pe, c)
                for i in range(2):
                    mm = nc.tensor.matmul(bank(c, 1 + i), weights[:, i * D:(i + 1) * D], src[c], start=True, stop=True)
                mm.then_inc(s["qk"], 1)
                for t in range(CH // P):
                    mm = nc.tensor.matmul(ps[:, 4 * c + 3, t * P:(t + 1) * P], src[c][:, t * P:(t + 1) * P],
                                          weights[:, 2 * D:3 * D], start=True, stop=True)
                mm.then_inc(s["v"], 1)

        def qkv_act(act, s, n, biased, parts):
            for c in range(2):
                act.wait_ge(s["qk"], n + c)
                for i, name in enumerate(("q_b", "k_b")):
                    bias = col(name) if biased else 0.0
                    nc.scalar.activation(QK32[c][:, i, :], bank(c, 1 + i), ACT.Identity,
                                         bias=bias).then_inc(s["qk_sb"], 1)
                act.wait_ge(s["qk_sb"], 2 * (n + c))
                nc.scalar.copy(parts[c][:, 0, :, :], QK32[c]).then_inc(s["part1"], 1)
            for c in range(2):
                act.wait_ge(s["rest"], n + c)
                nc.scalar.copy(parts[c][:, 1, :, :], REST[c]).then_inc(s["part2"], 1)

        def qkv_dve(dve, s, n, b, biased, parts):
            for c in range(2):
                dve.wait_ge(s["v"], n + c)
                dst = v_tok[:, bass.ds(b * S, S)].rearrange("p (g k f) -> p g k f", g=H // GH, k=QT)[:, :, 4 * c:4 * c + 4, :]
                src = bank(c, 3).rearrange("p (k g f) -> p g k f", k=4, g=H // GH)
                if biased:
                    shift = w["v_bias"][:, :].rearrange("p (k g f) -> p g k f", k=4, g=H // GH)
                    ins = nc.vector.tensor_tensor(dst, src, shift, ALU.add)
                else:
                    ins = nc.vector.tensor_scalar(dst, src, 1.0, None, ALU.mult)
                ins.then_inc(s["v_kept"], 1)
                dve.wait_ge(s["part1"], n + c)
                nc.vector.tensor_tensor(REST[c], QK32[c], parts[c][:, 0, :, :], ALU.subtract).then_inc(s["rest"], 1)
            for c in range(2):
                dve.wait_ge(s["part2"], n + c)
                nc.vector.tensor_tensor(parts[c][:, 2, :, :], REST[c], parts[c][:, 1, :, :],
                                        ALU.subtract).then_inc(s["part3"], 1)

        def qkv_store(sp, s, n, b, stored, parts):
            for t in range(3):
                for c in range(2):
                    sp.wait_ge(s[f"part{t + 1}"], n + c)
                    for i, (dram, slots) in enumerate(((scratch_q, SLOTS_Q), (scratch_k, SLOTS_K))):
                        for k, part in enumerate(slots):
                            if part == t:
                                sp.dma_start(dram[bass.ds(b * H, H), k * HD:(k + 1) * HD, c * CH:(c + 1) * CH],
                                             parts[c][:, part, i, :]).then_inc(stored[c], 16)

        STORED = 2 * NS * 16

        NB = 3
        QW = GH * S + GH * XQ
        flat = work[:, :, :].rearrange("p a n -> p (a n)")
        QF = [flat[:, i * (QW // 2):(i + 1) * (QW // 2)].bitcast(BF16) for i in range(NB)]
        KP = [work[:, 7 + i, :].bitcast(BF16).rearrange("p (r n) -> p r n", r=2) for i in range(NB)]
        VP = [work[:, 10 + i, :].rearrange("p (k j d) -> p k j d", k=QT, j=GH) for i in range(NB)]
        EB = [half for i in range(3) for half in chunks(13 + i)]
        OS, RD, ONT = chunks(17), chunks(18), chunks(19)
        SX = work[:, 20, 0:3 * XQ].rearrange("p (a n) -> p a n", a=3)
        SA = [ps[:, i, :] for i in range(3)]
        SB = [ps[:, 3 + i, :] for i in range(3)]
        OB = [ps[:, 6 + i, :] for i in range(2)]
        assert 2 * S * 7 >= NB * QW

        def q_cols(p, j, at, n):
            return QF[p][:, j * S + at:j * S + at + n]

        def x_cols(p, j):
            return QF[p][:, GH * S + j * XQ:GH * S + (j + 1) * XQ]

        def attention(tag, causal):
            NX = 0 if causal else 1
            s1 = []
            for j in range(GH):
                for qt in range(QT):
                    for half in range(2):
                        width = min(CH, P * (qt + 1) - CH * half) if causal else CH
                        if width > 0:
                            s1.append((j, qt, half, width, causal and width == P * (qt + 1) - CH * half))
            for half in range(2 * NX):
                s1.append(("x", None, half, CH, False))
            NU = len(s1)
            s2 = []
            for qh in range(2):
                for kc in range(QT):
                    for j in range(GH):
                        off = max(0, P * kc - CH * qh) if causal else 0
                        if off < CH:
                            s2.append((qh, kc, j, off, causal and P * kc >= CH * qh))
            lastk = [max(u[1] for u in s2 if u[0] == qh) for qh in range(2)]
            ends = [max(i for i, u in enumerate(s2) if u[0] == 0)]
            if NX:
                for pr in range(2):
                    s2.insert(ends[0] + 15 + pr, ("x", None, pr, 0, False))
                ends.append(ends[0] + 16)
            NV = len(s2)
            NS2, NE = len(SB), len(EB)
            assert NV % NS2 == 0 and NV % NE == 0 and NU % len(SA) == 0
            ends.append(NV - 1)
            NO = len(ends)
            BACK = 14
            AHEAD = 2 * (NU * BACK // NV // 2)
            plan = [[] for _ in range(2 * NV)]
            items = [(1, u) for u in range(AHEAD, NU)] + [None, (1, NU), None] + [(2, u) for u in range(AHEAD)]
            for n, item in enumerate(items):
                if item:
                    plan[n * 2 * NV // len(items)].append(item)

            sems = {k: sem(f"{tag}_{k}") for k in (
                "scores1", "scores1_read", "max", "m_ready", "m_turned", "m_chain", "m_split",
                "v_ready", "scores2", "exp_done", "pv_done", "o_sb", "den", "log", "inv", "normed", "o_free")}
            loaded = [sem(f"{tag}_loaded{p}") for p in range(NB)]
            m_rows = [sem(f"{tag}_m_rows{p}") for p in range(NB)]
            o_stored = [sem(f"{tag}_o_stored{q}") for q in range(NO)]
            LOAD = 16 * (GH + GH // 2 + GH * NX)
            MROWS = 16 * 3
            NM = 32 + NX

            def sp_load(sp, gi, p):
                for pr in range(GH // 2):
                    heads = scratch_k[bass.ds(gi * GH + 2 * pr, 2), :, :].rearrange("h r n -> (h r) n")
                    sp.dma_start(KP[p][0:R_MAX, pr, :], heads).then_inc(loaded[p], 16)
                for j in range(GH):
                    r = HR * (j % 2)
                    sp.dma_start(q_cols(p, j, 0, S)[r:r + HR, :], scratch_q[gi * GH + j, :, :]).then_inc(loaded[p], 16)
                    if NX:
                        sp.dma_start(x_cols(p, j)[r:r + R_MASK, :],
                                     scratch_q[gi * GH + j, 0:R_MASK, 0:XQ]).then_inc(loaded[p], 16)

            def sp_rows(sp, gi, p):
                sp.wait_ge(sems["m_split"], gi + 1)
                for t in range(3):
                    sp.dma_start(QF[p][R_MAX + t:R_MAX + t + 1, 0:NM * P], m_parts[0:NM, p, t, :]).then_inc(m_rows[p], 16)

            def sp_store(sp, gi, o):
                sp.wait_ge(sems["normed"], gi * NO + o + 1)
                if NX and o == 1:
                    sp.dma_start(scratch_x.rearrange("b g p n -> (b g) p n")[gi, :, :], SX[:, 2, :]).then_inc(o_stored[o], 16)
                else:
                    q = 1 if o else 0
                    dst = scratch_o.rearrange("b g p n -> (b g) p n")[gi, :, q * CH:(q + 1) * CH]
                    sp.dma_start(dst, ONT[q]).then_inc(o_stored[o], 16)

            def sp_step(sp, gi, p, rows, load):
                sp_store(sp, gi, 0)
                if rows:
                    sp_rows(sp, gi + 1, (p + 1) % NB)
                if NX:
                    sp_store(sp, gi, 1)
                if load:
                    sp.wait_ge(sems["pv_done"], gi * NV + NV + NE)
                    sp_load(sp, gi + NB, p)
                sp_store(sp, gi, NO - 1)

            def pe_max(pe, gi, p, k, u):
                base = gi * (NU + 1)
                if u == 0:
                    pe.wait_ge(loaded[p], k * LOAD)
                pe.wait_ge(sems["scores1_read"], base + 1 + max(0, u - 2))
                if u == NU:
                    pe.wait_ge(sems["m_ready"], gi + 1)
                    nc.tensor.transpose(SA[0][:, 0:P], m_col[:, :], w["ident"][:, :]).then_inc(sems["m_turned"], 1)
                    return
                j, qt, half, width, diag = s1[u]
                dst = SA[u % 3]
                if j == "x":
                    for j in range(GH):
                        mm = nc.tensor.matmul(dst[32 * j:32 * j + XQ, :], x_cols(p, j)[0:R_MAX, :],
                                              KP[p][0:R_MAX, j // 2, half * CH:(half + 1) * CH], start=True, stop=True)
                    mm.then_inc(sems["scores1"], 1)
                    return
                mm = nc.tensor.matmul(dst[:, 0:width], q_cols(p, j, qt * P, P)[0:R_MAX, :],
                                      KP[p][0:R_MAX, j // 2, half * CH:half * CH + width], start=True, stop=not diag)
                if diag:
                    mm = nc.tensor.matmul(dst[:, width - P:width], w["ident_b"][:, :], w["mask_qk"][:, :],
                                          start=False, stop=True)
                mm.then_inc(sems["scores1"], 1)

            def pe_scores(pe, gi, p, k, v):
                if v == 0:
                    pe.wait_ge(m_rows[p], k * MROWS)
                pe.wait_ge(sems["exp_done"], gi * NV + v + 1)
                qh, kc, j, off, diag = s2[v]
                dst = SB[v % NS2]
                if qh == "x":
                    for kc in range(QT):
                        for i in range(2):
                            at = XQ * (2 * kc + i)
                            mm = nc.tensor.matmul(dst[:, at:at + XQ], KP[p][0:R_END, j, kc * P:(kc + 1) * P],
                                                  x_cols(p, 2 * j + i)[0:R_END, :], start=True, stop=True)
                    mm.then_inc(sems["scores2"], 1)
                    return
                mm = nc.tensor.matmul(dst[:, off:CH], KP[p][0:R_END, j // 2, kc * P:(kc + 1) * P],
                                      q_cols(p, j, qh * CH + off, CH - off)[0:R_END, :], start=True, stop=not diag)
                if diag:
                    mm = nc.tensor.matmul(dst[:, off:off + P], w["ident_b"][:, :], w["mask_kq"][:, :],
                                          start=False, stop=True)
                mm.then_inc(sems["scores2"], 1)

            def pe_values(pe, gi, p, v):
                if v == 0:
                    pe.wait_ge(sems["v_ready"], gi + 1)
                pe.wait_ge(sems["exp_done"], gi * NV + v + 1 + NS2)
                qh, kc, j, off, _ = s2[v]
                src = EB[v % NE]
                if qh == "x":
                    if j == 0:
                        pe.wait_ge(sems["o_free"], gi * NO + 3)
                    for kc in range(QT):
                        for i in range(2):
                            at, h = XQ * (2 * kc + i), 2 * j + i
                            mm = nc.tensor.matmul(OB[0][32 * h:32 * h + 32, 0:XQ], VP[p][:, kc, h, :], src[:, at:at + XQ],
                                                  start=(kc == 0), stop=(kc == QT - 1))
                    mm.then_inc(sems["pv_done"], 1)
                    return
                if kc == 0 and j == 0:
                    pe.wait_ge(sems["o_free"], gi * NO + 1 + qh)
                nc.tensor.matmul(OB[qh][32 * j:32 * j + 32, off:CH], VP[p][:, kc, j, :], src[:, off:CH],
                                 start=(kc == 0), stop=(kc == lastk[qh])).then_inc(sems["pv_done"], 1)

            def out_of(o):
                if NX and o == 1:
                    return OB[0][:, 0:XQ], SX[:, 0, :], SX[:, 1, :], SX[:, 2, :]
                q = 1 if o else 0
                return OB[q], OS[q], RD[q], ONT[q]

            def pe_den(pe, gi, o):
                pe.wait_ge(sems["o_sb"], gi * NO + o + 1)
                dst, src, _, _ = out_of(o)
                nc.tensor.matmul(dst, w["den_sel"][:, :], src, start=True, stop=True).then_inc(sems["den"], 1)

            def outputs_at(gi, v, lag, previous, do):
                for o in range(NO - 1):
                    if v == ends[o] + lag:
                        do(gi, o)
                if previous and v == lag - 1:
                    do(gi - 1, NO - 1)

            def pe_step(pe, gi, p, k, previous, ahead):
                def maxima(items):
                    for d, u in items:
                        if d <= ahead:
                            pe_max(pe, gi + d, (p + d) % NB, k + (p + d) // NB, u)

                for v in range(NV):
                    maxima(plan[2 * v])
                    pe_values(pe, gi, p, v)
                    maxima(plan[2 * v + 1])
                    if v + NS2 < NV:
                        pe_scores(pe, gi, p, k, v + NS2)
                    elif ahead:
                        pe_scores(pe, gi + 1, (p + 1) % NB, k + (p + 1) // NB, v + NS2 - NV)
                    outputs_at(gi, v, 6, previous, lambda g, o: pe_den(pe, g, o))

            def act_step(act, gi, p, previous):
                for v in range(NV):
                    off = s2[v][3]
                    act.wait_ge(sems["scores2"], gi * NV + v + 1)
                    act.wait_ge(sems["pv_done"], gi * NV + v + 1)
                    nc.scalar.activation(EB[v % NE][:, off:CH], SB[v % NS2][:, off:CH], ACT.Exp,
                                         scale=SCALE).then_inc(sems["exp_done"], 1)
                    outputs_at(gi, v, 4, previous, lambda g, o: act_copy(act, g, o))
                    outputs_at(gi, v, 8, previous, lambda g, o: act_inv(act, g, o))

            def act_copy(act, gi, o):
                act.wait_ge(sems["pv_done"], gi * NV + ends[o] + 1 + NE)
                src, dst, _, _ = out_of(o)
                nc.scalar.copy(dst, src).then_inc(sems["o_sb"], 1)

            def act_inv(act, gi, o):
                act.wait_ge(sems["den"], gi * NO + o + 1)
                den, _, inv, _ = out_of(o)
                nc.scalar.activation(inv, den, ACT.Ln).then_inc(sems["log"], 1)
                act.wait_ge(sems["log"], gi * NO + o + 1)
                nc.scalar.activation(inv, inv, ACT.Exp, scale=-1.0).then_inc(sems["inv"], 1)

            def dve_max(dve, gi, p, u):
                if u == NU:
                    dve_rows(dve, gi, p)
                    return
                dve.wait_ge(sems["scores1"], gi * NU + u + 1)
                j, qt, half, width, _ = s1[u]
                at = 32 if j == "x" else QT * j + qt
                nc.vector.tensor_reduce(m_cat[:, half, at:at + 1], SA[u % 3][:, 0:width], AX.X,
                                        ALU.max).then_inc(sems["scores1_read"], 1)

            def dve_rows(dve, gi, p):
                dve.wait_ge(sems["scores1_read"], gi * (NU + 1) + NU + 1)
                nc.vector.tensor_tensor(m_col[:, 0:NM], m_cat[:, 0, 0:NM], m_cat[:, 1, 0:NM],
                                        ALU.max).then_inc(sems["m_ready"], 1)
                dve.wait_ge(sems["m_turned"], gi + 1)
                nc.vector.tensor_scalar(m_neg[:, 0, :], SA[0][0:40, 0:P], -1.0, None,
                                        ALU.mult).then_inc(sems["scores1_read"], 1)
                k = gi * 3
                dve.wait_ge(sems["scores1_read"], (gi + 1) * (NU + 1) + 1)
                nc.vector.tensor_copy(m_parts[:, p, 0, :], m_neg[:, 0, :]).then_inc(sems["m_chain"], 1)
                dve.wait_ge(sems["m_chain"], k + 1)
                nc.vector.tensor_tensor(m_neg[:, 1, :], m_neg[:, 0, :], m_parts[:, p, 0, :],
                                        ALU.subtract).then_inc(sems["m_chain"], 1)
                dve.wait_ge(sems["m_chain"], k + 2)
                nc.vector.tensor_copy(m_parts[:, p, 1, :], m_neg[:, 1, :]).then_inc(sems["m_chain"], 1)
                dve.wait_ge(sems["m_chain"], k + 3)
                nc.vector.tensor_tensor(m_parts[:, p, 2, :], m_neg[:, 1, :], m_parts[:, p, 1, :],
                                        ALU.subtract).then_inc(sems["m_split"], 1)

            def dve_out(dve, gi, o):
                dve.wait_ge(sems["inv"], gi * NO + o + 1)
                _, src, inv, dst = out_of(o)
                dve.wait_ge(o_stored[o], gi * 16 + 16)
                nc.vector.tensor_tensor(dst, src, inv, ALU.mult).then_inc(sems["normed"], 1)
                dve.wait_ge(sems["normed"], gi * NO + o + 1)
                dve.sem_inc(sems["o_free"], 1)

            def dve_step(dve, gi, p, previous, ahead):
                for v in range(NV):
                    for d, u in plan[2 * v] + plan[2 * v + 1]:
                        if d <= ahead:
                            dve_max(dve, gi + d, (p + d) % NB, u)
                    outputs_at(gi, v, 12, previous, lambda g, o: dve_out(dve, g, o))

            return dict(locals())

        def run_attention(tag, causal):
            t = attention(tag, causal)
            sems, NO, NX, NV, NU, AHEAD, NS2, NE = (t[n] for n in ("sems", "NO", "NX", "NV", "NU", "AHEAD", "NS2", "NE"))
            trips = (GROUPS - 4) // NB
            tail = range(1 + trips * NB, GROUPS)
            ahead = [min(2, GROUPS - 1 - g) for g in range(GROUPS)]
            assert ahead[tail[0] - 1] == 2
            v_init, s_init = sem(f"{tag}_v_init"), sem(f"{tag}_init")
            s_xrows = [sem(f"{tag}_xrows{p}") for p in range(NB)]
            with nc.Block() as block:
                @block.sync
                def _(sp):
                    for q in range(NO):
                        sp.sem_inc(t["o_stored"][q], 16)
                    for g in range(NB):
                        sp.wait_ge(s_init, 2 * g + 2)
                        t["sp_load"](sp, g, g)
                        if NX:
                            for j in range(GH):
                                r = HR * (j % 2) + R_MASK
                                sp.dma_start(x_cols(g, j)[r:r + 2, :], a["x_rows"]).then_inc(s_xrows[g], 16)
                    t["sp_rows"](sp, 0, 0)
                    t["sp_step"](sp, 0, 0, True, True)
                    with sp.Fori(0, trips) as i:
                        for s in range(1, NB + 1):
                            t["sp_step"](sp, i * NB + s, s % NB, True, True)
                    for g in tail:
                        t["sp_step"](sp, g, g % NB, g + 1 < GROUPS, g + NB < GROUPS)
                    for q in range(NO):
                        sp.wait_ge(t["o_stored"][q], 16 * (GROUPS + 1))

                @block.tensor
                def _(pe):
                    pe.sem_inc(sems["pv_done"], NE)
                    for u in range(NU + 1):
                        if NX and u == NU - 2:
                            for p in range(NB):
                                pe.wait_ge(s_xrows[p], 16 * GH)
                        t["pe_max"](pe, 0, 0, 1, u)
                    for u in range(AHEAD):
                        t["pe_max"](pe, 1, 1, 1, u)
                    for v in range(NS2):
                        t["pe_scores"](pe, 0, 0, 1, v)
                    t["pe_step"](pe, 0, 0, 1, False, 2)
                    with pe.Fori(0, trips) as i:
                        for s in range(1, NB + 1):
                            t["pe_step"](pe, i * NB + s, s % NB, i + (1 + s // NB), True, 2)
                    for g in tail:
                        t["pe_step"](pe, g, g % NB, g // NB + 1, True, ahead[g])
                    t["pe_den"](pe, GROUPS - 1, NO - 1)

                @block.scalar
                def _(act):
                    act.preload_act_table_set("natural_log_exp_and_others")
                    act.sem_inc(sems["exp_done"], NS2)
                    t["act_step"](act, 0, 0, False)
                    with act.Fori(0, trips) as i:
                        for s in range(1, NB + 1):
                            t["act_step"](act, i * NB + s, s % NB, True)
                    for g in tail:
                        t["act_step"](act, g, g % NB, True)
                    t["act_copy"](act, GROUPS - 1, NO - 1)
                    t["act_inv"](act, GROUPS - 1, NO - 1)

                @block.vector
                def _(dve):
                    for p in range(NB):
                        nc.vector.memset(QF[p], 0.0).then_inc(s_init, 1)
                        nc.vector.memset(KP[p][96:P, :, :], 1.0).then_inc(s_init, 1)
                    dve.sem_inc(sems["scores1_read"], 1)
                    dve.sem_inc(sems["o_free"], 2)
                    for u in range(NU + 1):
                        t["dve_max"](dve, 0, 0, u)
                    for u in range(AHEAD):
                        t["dve_max"](dve, 1, 1, u)
                    t["dve_step"](dve, 0, 0, False, 2)
                    with dve.Fori(0, trips) as i:
                        for s in range(1, NB + 1):
                            t["dve_step"](dve, i * NB + s, s % NB, True, 2)
                    for g in tail:
                        t["dve_step"](dve, g, g % NB, True, ahead[g])
                    t["dve_out"](dve, GROUPS - 1, NO - 1)

                def pool_v(pool, gi, p):
                    rows = v_tok[:, bass.ds(gi * (QT * GH * HD), QT * GH * HD)].rearrange(
                        "p (k j d) -> p k j d", k=QT, j=GH)
                    nc.gpsimd.tensor_copy(VP[p][:, :, :, 0:HD], rows).then_inc(sems["v_ready"], 1)

                @block.gpsimd
                def _(pool):
                    for p in range(NB):
                        pool.memset(VP[p], 0.0).then_inc(v_init, 1)
                        pool.wait_ge(v_init, 2 * p + 1)
                        pool.memset(VP[p][:, :, :, HD:HD + 1], 1.0).then_inc(v_init, 1)
                        pool.wait_ge(v_init, 2 * p + 2)
                    for g in range(NB):
                        pool_v(pool, g, g)
                    with pool.Fori(0, (GROUPS - 1) // NB - 1) as i:
                        for s in range(NB):
                            pool.wait_ge(sems["pv_done"], i * (NB * NV) + (s + 1) * NV + NE)
                            pool_v(pool, i * NB + (s + NB), s)
                    pool.wait_ge(sems["pv_done"], (GROUPS - NB) * NV + NE)
                    pool_v(pool, GROUPS - 1, (GROUPS - 1) % NB)

        s_w, s_small, s_zero = sem("s_w"), sem("s_small"), sem("s_zero")
        s_gate, s_rows0 = [sem(f"s_gate{i}") for i in range(8)], sem("s_rows0")
        zero_tile = work[:, 1, :].bitcast(BF16)[:, 0:S]
        with nc.Block() as block:
            @block.sync
            def _(sp):
                for name, t in w.items():
                    dst = t[tuple(slice(None) for _ in t.shape)]
                    sp.dma_start(dst, a[name]).then_inc(s_w, 16)
                sp.wait_ge(s_zero, 1)
                for b in range(B):
                    hs = slice(b * H, (b + 1) * H)
                    for dram in (scratch_q, scratch_k):
                        sp.dma_start(dram[hs, R_MASK:HR, :], zero_tile[0:2 * H, :]).then_inc(s_rows0, 16)
                sp.wait_ge(s_rows0, 16 * 2 * B)

            @block.gpsimd
            def _(pool):
                pool.memset(zero_tile, 0.0).then_inc(s_zero, 1)
                pool.memset(eps_col[:, 0:1], EPS).then_inc(s_zero, 1)
                pool.memset(eps_col[:, 1:2], EPS * EPS).then_inc(s_zero, 1)
                pool.memset(m_cat[:, :, :], -3.0e38)
                pool.memset(m_col[:, :], 0.0)

            @block.scalar
            def _(act):
                act.preload_act_table_set("natural_log_exp_and_others")
                act.wait_ge(s_w, 16 * len(w))
                act.wait_ge(s_gate[7], 1)
                nc.scalar.activation(a_neg[:, :], a_neg[:, :],
                                     ACT.Exp).then_inc(s_gate[0], 1)
                nc.scalar.activation(gate_tmp[:, 0:1], col("q_gate"), ACT.Square).then_inc(s_gate[1], 1)
                act.wait_ge(s_gate[2], 1)
                nc.scalar.activation(gate_tmp[0:H, 1:2], ps[0:H, 0, 0:1], ACT.Ln).then_inc(s_gate[3], 1)
                act.wait_ge(s_gate[3], 1)
                nc.scalar.activation(gate_tmp[0:H, 2:3], gate_tmp[0:H, 1:2], ACT.Exp, scale=-0.5).then_inc(s_gate[4], 1)

            @block.tensor
            def _(pe):
                pe.wait_ge(s_w, 16 * len(w))
                pe.wait_ge(s_gate[1], 1)
                nc.tensor.matmul(ps[0:H, 0, 0:1], w["head_sel"][:, :], gate_tmp[:, 0:1], start=True,
                                 stop=True).then_inc(s_gate[2], 1)
                pe.wait_ge(s_gate[4], 1)
                nc.tensor.matmul(ps[:, 1, 0:1], w["head_back"][:, :], gate_tmp[0:H, 2:3], start=True,
                                 stop=True).then_inc(s_gate[5], 1)

            @block.vector
            def _(dve):
                dve.wait_ge(s_w, 16 * len(w))
                nc.vector.tensor_scalar(a_neg[:, :], w["cols"][:, COLS["A_log"][0]:COLS["A_log"][0] + CI * DS], 80.0,
                                        None, ALU.min).then_inc(s_gate[7], 1)
                dve.wait_ge(s_gate[0], 1)
                nc.vector.tensor_scalar(a_neg[:, :], a_neg[:, :], -1.0, None, ALU.mult)
                dve.wait_ge(s_gate[5], 1)
                nc.vector.tensor_tensor(gate_tmp[:, 3:4], col("q_gate"), ps[:, 1, 0:1], ALU.mult).then_inc(s_gate[6], 1)
                dve.wait_ge(s_gate[6], 1)
                nc.vector.tensor_scalar(q_gate_sel[:, :], w["head_sel"][:, :], gate_tmp[:, 3:4], None, ALU.mult)

        end_phase()

        a_norm, a_qkv = norm_sems("a_norm"), qkv_sems("a_qkv")
        a_norm.update({k: sem(f"a_norm_{k}") for k in ("log2", "rstd2", "out2")})
        RSTD2 = chunks(14)
        a_x = [sem(f"a_x{c}") for c in range(2)]
        a_free, a_turned, a_copied, a_kept, a_stats_read = (
            sem("a_" + k) for k in ("free", "turned", "copied", "kept", "stats_read"))
        a_stored = [[sem(f"a_stored{s}{c}") for c in range(2)] for s in range(2)]
        A_PARTS = [PARTS, parts_at(15)]
        x_dram = a["x"]
        with nc.Block() as block:
            @block.sync
            def _(sp):
                for s in range(2):
                    for c in range(2):
                        sp.sem_inc(a_stored[s][c], 16)

                def load(b):
                    for c in range(2):
                        sp.wait_ge(a_free, b * 2 + c + 1)
                        sp.dma_start(XIN[c], x_dram[bass.ds(b * QT + 4 * c, 4), :, :].rearrange("t p f -> p t f")
                                     ).then_inc(a_x[c], 16)

                load(0)
                with sp.Fori(0, B // 2 - 1) as i:
                    for s in range(2):
                        b = i * 2 + s
                        load(b + 1)
                        qkv_store(sp, a_qkv, b * 2 + 1, b, a_stored[s], A_PARTS[s])
                load(B - 1)
                for s in range(2):
                    qkv_store(sp, a_qkv, (B - 2 + s) * 2 + 1, B - 2 + s, a_stored[s], A_PARTS[s])
                for s in range(2):
                    for c in range(2):
                        sp.wait_ge(a_stored[s][c], STORED * (B // 2) + 16)

            @block.tensor
            def _(pe):
                pe.sem_inc(a_free, 2)
                with pe.Fori(0, B) as b:
                    pe.wait_ge(a_stats_read, b + 1)
                    for c in range(2):
                        pe.wait_ge(a_x[c], b * 16 + 16)
                        for t in range(4):
                            mm = nc.tensor.transpose(ps[:, 4 * c, t * P:(t + 1) * P], XIN[c][:, t, :], w["ident"][:, :])
                        mm.then_inc(a_turned, 1)
                        pe.wait_ge(a_turned, b * 2 + c + 1)
                        pe.sem_inc(a_free, 1)
                    norm_pe(pe, a_norm, b * 2 + 1, XR, lambda e, c: e.wait_ge(a_copied, b * 2 + c + 1))
                    qkv_pe(pe, a_qkv, b * 2 + 1, w["qkv_w"], XN, lambda e, c: e.wait_ge(a_norm["affine"], b * 2 + c + 1))

            @block.scalar
            def _(act):
                act.preload_act_table_set("natural_log_exp_and_others")
                act.sem_inc(a_stats_read, 1)
                with act.Fori(0, B // 2) as i:
                    for s in range(2):
                        b = i * 2 + s
                        norm_act(act, a_norm, b * 2 + 1, both=RSTD2)
                        act.sem_inc(a_stats_read, 1)
                        for c in range(2):
                            act.wait_ge(a_stored[s][c], i * STORED + 16)
                        qkv_act(act, a_qkv, b * 2 + 1, True, A_PARTS[s])

            @block.vector
            def _(dve):
                with dve.Fori(0, B // 2) as i:
                    for s in range(2):
                        b = i * 2 + s
                        n = b * 2 + 1
                        for c in range(2):
                            dve.wait_ge(a_turned, n + c)
                            nc.vector.tensor_copy(XR[c], bank(c, 0)).then_inc(a_copied, 1)
                        for c in range(2):
                            dve.wait_ge(a_norm["mean"], n + c)
                            nc.vector.tensor_tensor(DEV[c], XR[c], bank(c, 0), ALU.subtract).then_inc(a_norm["centred"], 1)
                        for c in range(2):
                            dve.wait_ge(a_norm["rstd2"], n + c)
                            nc.vector.tensor_tensor(XN[c], DEV[c], RSTD2[c], ALU.mult).then_inc(a_norm["out2"], 1)
                            dve.wait_ge(a_norm["out2"], n + c)
                            nc.vector.tensor_scalar(XN[c], XN[c], col("g_attn"), col("b_attn"), ALU.mult,
                                                    ALU.add).then_inc(a_norm["affine"], 1)
                            dve.wait_ge(a_norm["rstd"], n + c)
                            nc.vector.tensor_tensor(h0[:, bass.ds(b * S + c * CH, CH)], DEV[c], RSTD[c],
                                                    ALU.mult).then_inc(a_norm["out"], 1)
                        qkv_dve(dve, a_qkv, n, b, True, A_PARTS[s])
                        dve.wait_ge(a_kept, n + 1)

            @block.gpsimd
            def _(pool):
                with pool.Fori(0, B) as b:
                    for c in range(2):
                        pool.wait_ge(a_copied, b * 2 + c + 1)
                        nc.gpsimd.tensor_copy(x_res[:, bass.ds(b * S + c * CH, CH)], XR[c]).then_inc(a_kept, 1)

        end_phase()
        run_attention("b", True)
        end_phase()

        CV = [[work[:, 13 + c, i * CH:(i + 1) * CH] for i in range(CI)] for c in range(2)]
        SZ, U, DL, DU, DA, DBU, HC = ([work[:, k + i, :] for i in range(CI)] for k in (5, 7, 9, 11, 13, 15, 19))
        HS = [[work[:, k, :] for k in ks] for ks in ((17, 18), (2, 4))]
        CR = [work[:, k, :] for k in (1, 3)]
        SP1 = [[work[:, 15 + c, i * CH:(i + 1) * CH] for i in range(CI)] for c in range(2)]
        SP2 = chunks(20)
        YT = DBU
        B_HI = [SQ[c].bitcast(BF16)[0:6 * DS, 0:CH] for c in range(2)]
        B_MID = [SQ[c].bitcast(BF16)[0:6 * DS, CH:2 * CH] for c in range(2)]
        B_REST = [DEV[c][0:6 * DS, :] for c in range(2)]
        DT = [RSTD[c][0:DR, :] for c in range(2)]
        SIM16 = [work[0:H, 14, c * CH:(c + 1) * CH] for c in range(2)]

        def gate(c, k):
            return small[:, c, 32 * k:32 * k + 32].rearrange("p (t e) -> p t e", t=4)

        gmax = [small[:, c, 128:132] for c in range(2)]
        gmin = [small[:, c, 132:136] for c in range(2)]
        lim_run = [small[:, c, 136:138] for c in range(2)]
        lim_part = [small[:, c, 138:140] for c in range(2)]
        iota = w["iota"]

        NLN = 8
        ln = norm_sems("c_norm")
        qs = qkv_sems("c_qkv")
        c_stored = [sem(f"c_stored{c}") for c in range(2)]
        cs = {k: sem("c_" + k) for k in (
            "att", "ctx", "xa", "rec", "tanh", "vel", "drag", "xs", "xa2",
            "ffh", "gelu", "ffy", "xa3", "xr1", "gates", "g_sb", "g_max", "g_less", "g_cand", "g_min", "onehot",
            "oh_turned", "oh_b", "mask", "moe_h", "relu", "moe_y", "moe_y_sb", "masked", "acc", "xr2",
            "pad", "inp", "in_sb", "tap", "u", "xp", "bc_hi", "bc_rest", "bc_mid", "bc", "dt", "dtp", "sp_abs",
            "sp_exp", "sp", "dl", "du", "b_row", "c_row", "c_sb", "da", "dbu", "state", "hc", "y_sum", "yy", "yg", "op", "ao",
            "xr3", "kept", "q_sq", "sim_parts", "sim_log", "sim_inv", "sim_prod", "sim", "sim_kept", "lim", "lim_part")}
        c_ol = [sem(f"c_ol{c}") for c in range(2)]

        def cols_of(b, c):
            return bass.ds(b * S + c * CH, CH)

        with nc.Block() as block:
            @block.sync
            def _(sp):
                def load(b):
                    for c in range(2):
                        sp.dma_start(OL[c], heads_o[b, :, :, c * CH:(c + 1) * CH]).then_inc(c_ol[c], 16)

                for c in range(2):
                    sp.sem_inc(c_stored[c], 16)
                load(0)
                with sp.Fori(0, B - 1) as b:
                    sp.wait_ge(cs["op"], b * 2 + 2)
                    load(b + 1)
                    qkv_store(sp, qs, b * 2 + 1, b, c_stored, PARTS)
                qkv_store(sp, qs, B * 2 - 1, B - 1, c_stored, PARTS)
                for c in range(2):
                    sp.wait_ge(c_stored[c], STORED * B + 16)

            @block.tensor
            def _(pe):
                with pe.Fori(0, B) as b:
                    n = b * 2 + 1

                    def lnv(i):
                        return b * (2 * NLN) + 2 * i + 1

                    def ready(s, value):
                        return lambda e, c: e.wait_ge(s, value + c)

                    for c in range(2):
                        pe.wait_ge(c_ol[c], b * 16 + 16)
                        nc.tensor.matmul(bank(c, 1), w["out_w"][:, :], OL[c], start=True, stop=True).then_inc(cs["att"], 1)
                    norm_pe(pe, ln, lnv(0), XA, ready(cs["xa"], n))
                    def from_context(s, c):
                        if s >= 2:
                            pe.wait_ge(cs["tanh"], b * (2 * STEPS) + 2 * (s - 2) + c + 1)
                        nc.tensor.matmul(bank(c, 1 + s % 2), w["w_ctx"][:, :], CTX[c], start=True, stop=False)

                    for c in range(2):
                        pe.wait_ge(cs["ctx"], n + c)
                        from_context(0, c)
                    for s in range(STEPS):
                        for c in range(2):
                            if s == 0:
                                pe.wait_ge(ln["affine"], b * 6 + 1 + c)
                            else:
                                pe.wait_ge(cs["xs"], b * (2 * STEPS) + 2 * s - 1 + c)
                            nc.tensor.matmul(bank(c, 1 + s % 2), w["w_x"][:, :], XS[c], start=False,
                                             stop=True).then_inc(cs["rec"], 1)
                            if s + 1 < STEPS:
                                from_context(s + 1, c)
                    norm_pe(pe, ln, lnv(1), XA, ready(cs["xa2"], n))
                    M = FF // P
                    for m in range(M):
                        for c in range(2):
                            if m == 0:
                                pe.wait_ge(ln["affine"], b * 6 + 3 + c)
                            if m >= 2:
                                pe.wait_ge(cs["gelu"], b * (2 * M) + 2 * (m - 2) + c + 1)
                            nc.tensor.matmul(bank(c, 1 + m % 2), w["ff_w1"][:, m * P:(m + 1) * P], NRM[c], start=True,
                                             stop=True).then_inc(cs["ffh"], 1)
                    for m in range(M):
                        for c in range(2):
                            pe.wait_ge(cs["gelu"], b * (2 * M) + 2 * m + c + 1)
                            mm = nc.tensor.matmul(bank(c, 3), w["ff_w2"][:, m, :], HID[c][:, m, :], start=(m == 0),
                                                  stop=(m == M - 1))
                            if m == M - 1:
                                mm.then_inc(cs["ffy"], 1)
                    norm_pe(pe, ln, lnv(2), XA, ready(cs["xa3"], n))
                    norm_pe(pe, ln, lnv(3), XR, ready(cs["xr1"], n))
                    for c in range(2):
                        pe.wait_ge(ln["out"], lnv(3) + c)
                        for t in range(CH // P):
                            mm = nc.tensor.matmul(bank(c, 1)[:, t * E:(t + 1) * E], NRM[c][:, t * P:(t + 1) * P],
                                                  w["Wg"][:, :], start=True, stop=True)
                        mm.then_inc(cs["gates"], 1)
                    for c in range(2):
                        pe.wait_ge(cs["onehot"], n + c)
                        for t in range(CH // P):
                            mm = nc.tensor.matmul(bank(c, 2)[0:E, t * P:(t + 1) * P], gate(c, 3)[:, t, :],
                                                  w["ident"][:, :], start=True, stop=True)
                        mm.then_inc(cs["oh_turned"], 1)
                    for e in range(E):
                        for c in range(2):
                            if e == 0:
                                pe.wait_ge(cs["oh_b"], n + c)
                            else:
                                pe.wait_ge(cs["masked"], b * (2 * E) + 2 * (e - 1) + c + 1)
                            nc.tensor.matmul(bank(c, 0), w["exp_sel"][:, e, :], onehot_b[:, c, :], start=True,
                                             stop=True).then_inc(cs["mask"], 1)
                            for m in range(M):
                                if m >= 2:
                                    pe.wait_ge(cs["relu"], b * (2 * E * M) + (2 * e + c) * M + m - 1)
                                nc.tensor.matmul(bank(c, 1 + m % 2), w["W1"][:, e, m * P:(m + 1) * P], NRM[c],
                                                 start=True, stop=True).then_inc(cs["moe_h"], 1)
                        for c in range(2):
                            if e:
                                pe.wait_ge(cs["moe_y_sb"], b * (2 * E) + 2 * (e - 1) + c + 1)
                            for m in range(M):
                                pe.wait_ge(cs["relu"], b * (2 * E * M) + (2 * e + c) * M + m + 1)
                                mm = nc.tensor.matmul(bank(c, 3), w["W2"][:, e, m, :], HID[c][:, m, :], start=(m == 0),
                                                      stop=(m == M - 1))
                            mm.then_inc(cs["moe_y"], 1)
                    norm_pe(pe, ln, lnv(4), ACC, ready(cs["acc"], b * (2 * (E - 1)) + 2 * (E - 2) + 1))
                    norm_pe(pe, ln, lnv(5), XR, ready(cs["xr2"], n))
                    for o in range(2 * CI):
                        for c in range(2):
                            if o == 0:
                                pe.wait_ge(ln["affine"], b * 6 + 5 + c)
                            if o >= 2:
                                pe.wait_ge(cs["in_sb"], b * (4 * CI) + 2 * (o - 2) + c + 1)
                            nc.tensor.matmul(bank(c, 1 + o % 2), w["in_proj_w"][:, o * P:(o + 1) * P], NRM[c], start=True,
                                             stop=True).then_inc(cs["inp"], 1)
                    for c in range(2):
                        pe.wait_ge(cs["u"], b * 4 + 2 * c + 2)
                        at = slice(c * CH, (c + 1) * CH)
                        for i in range(CI):
                            nc.tensor.matmul(bank(c, 1)[0:DR, :], w["x_proj_dt"][:, i, :], U[i][:, at], start=(i == 0),
                                             stop=(i == CI - 1))
                        for i in range(CI):
                            mm = nc.tensor.matmul(bank(c, 2)[0:6 * DS, :], w["x_proj_bc"][:, i, :], U[i][:, at],
                                                  start=(i == 0), stop=(i == CI - 1))
                        mm.then_inc(cs["xp"], 1)
                    for c in range(2):
                        pe.wait_ge(cs["dt"], n + c)
                        for i in range(CI):
                            mm = nc.tensor.matmul(bank(c, 1 + 2 * i), w["dt_proj_w"][:, i * P:(i + 1) * P], DT[c],
                                                  start=True, stop=True)
                        mm.then_inc(cs["dtp"], 1)

                    def row(k, bank0, s):
                        for c in range(2):
                            mm = nc.tensor.matmul(ps[:, bank0 + c, :], w["bc_sel"][:, k, :],
                                                  bc_parts[:, c * CH:(c + 1) * CH], start=True, stop=True)
                        mm.then_inc(s, 1)

                    def add_state(k, i):
                        pe.wait_ge(cs["hc"], b * (DS * CI) + 2 * k + i + 1)
                        for c in range(2):
                            mm = nc.tensor.matmul(ps[:, 4 + 2 * i + c, :], w["ident"][:, :], HC[i][:, c * CH:(c + 1) * CH],
                                                  start=(k == 0), stop=(k == DS - 1))
                        mm.then_inc(cs["y_sum"], 1)

                    pe.wait_ge(cs["bc"], n + 1)
                    pe.wait_ge(cs["du"], b * 4 + 4)
                    row(0, 0, cs["b_row"])
                    row(DS, 2, cs["c_row"])
                    for k in range(DS):
                        if k:
                            add_state(k - 1, 0)
                        if k + 1 < DS:
                            pe.wait_ge(cs["dbu"], b * (DS * CI) + 2 * k + 2)
                            row(k + 1, 0, cs["b_row"])
                        if k:
                            add_state(k - 1, 1)
                        if k + 1 < DS:
                            pe.wait_ge(cs["c_sb"], b * DS + k + 1)
                            row(DS + k + 1, 2, cs["c_row"])
                    for i in range(CI):
                        add_state(DS - 1, i)
                    for c in range(2):
                        pe.wait_ge(cs["yg"], b * 4 + 2 * c + 2)
                        for i in range(CI):
                            mm = nc.tensor.matmul(bank(c, 1), w["out_proj_w"][:, i, :], YT[i][:, c * CH:(c + 1) * CH],
                                                  start=(i == 0), stop=(i == CI - 1))
                        mm.then_inc(cs["op"], 1)
                    norm_pe(pe, ln, lnv(6), TT_, ready(cs["ao"], n))
                    norm_pe(pe, ln, lnv(7), XR, ready(cs["xr3"], n))
                    qkv_pe(pe, qs, n, w["qkv2_w"], XN, ready(ln["out"], lnv(7)))
                    for c in range(2):
                        pe.wait_ge(cs["q_sq"], n + c)
                        nc.tensor.matmul(bank(c, 0)[0:H, :], w["head_sel"][:, :], SQ[c], start=True, stop=True)
                        nc.tensor.matmul(bank(c, 1)[0:H, :], q_gate_sel[:, :], QK32[c][:, 0, :], start=True,
                                         stop=True).then_inc(cs["sim_parts"], 1)
                    for c in range(2):
                        pe.wait_ge(cs["sim_prod"], n + c)
                        nc.tensor.matmul(bank(c, 2), w["sim_sum"][:, :], SIM16[c], start=True,
                                         stop=True).then_inc(cs["sim"], 1)

            @block.scalar
            def _(act):
                with act.Fori(0, B) as b:
                    n = b * 2 + 1

                    def lnv(i):
                        return b * (2 * NLN) + 2 * i + 1

                    act.preload_act_table_set("natural_log_exp_and_others")
                    norm_act(act, ln, lnv(0))
                    for c in range(2):
                        act.wait_ge(c_stored[c], b * STORED + 16)
                    for s in range(STEPS):
                        for c in range(2):
                            act.wait_ge(cs["rec"], b * (2 * STEPS) + 2 * s + c + 1)
                            nc.scalar.activation(TT_[c], bank(c, 1 + s % 2), ACT.Tanh, bias=col("b_inl")).then_inc(cs["tanh"], 1)
                    act.preload_act_table_set("natural_log_exp_and_others")
                    norm_act(act, ln, lnv(1))
                    M = FF // P
                    for m in range(M):
                        for c in range(2):
                            act.wait_ge(cs["ffh"], b * (2 * M) + 2 * m + c + 1)
                            nc.scalar.activation(HID[c][:, m, :], bank(c, 1 + m % 2), ACT.Gelu,
                                                 bias=col("ff_b1", m)).then_inc(cs["gelu"], 1)
                    act.preload_act_table_set("natural_log_exp_and_others")
                    norm_act(act, ln, lnv(2))
                    norm_act(act, ln, lnv(3))
                    for e in range(E):
                        for c in range(2):
                            if e:
                                act.wait_ge(cs["moe_y"], b * (2 * E) + 2 * (e - 1) + c + 1)
                            for m in range(M):
                                act.wait_ge(cs["moe_h"], b * (2 * E * M) + (2 * e + c) * M + m + 1)
                                nc.scalar.activation(HID[c][:, m, :], bank(c, 1 + m % 2), ACT.Relu,
                                                     bias=col("moe_b1", e * M + m)).then_inc(cs["relu"], 1)
                        for c in range(2):
                            act.wait_ge(cs["moe_y"], b * (2 * E) + 2 * e + c + 1)
                            if e:
                                act.wait_ge(cs["masked"], b * (2 * E) + 2 * (e - 1) + c + 1)
                            nc.scalar.activation(MOE_Y[c], bank(c, 3), ACT.Identity,
                                                 bias=col("moe_b2", e)).then_inc(cs["moe_y_sb"], 1)
                    norm_act(act, ln, lnv(4))
                    norm_act(act, ln, lnv(5), twice=True)
                    for o in range(2 * CI):
                        for c in range(2):
                            act.wait_ge(cs["inp"], b * (4 * CI) + 2 * o + c + 1)
                            if o < CI:
                                at = KC - 1 + c * CH
                                ins = nc.scalar.copy(CONV[:, o, at:at + CH], bank(c, 1 + o % 2))
                            else:
                                ins = nc.scalar.activation(SZ[o - CI][:, c * CH:(c + 1) * CH], bank(c, 1 + o % 2), ACT.Silu)
                            ins.then_inc(cs["in_sb"], 1)
                    for c in range(2):
                        for i in range(CI):
                            act.wait_ge(cs["tap"], b * 16 + c * 8 + 2 * (KC - 1) + i + 1)
                            nc.scalar.activation(U[i][:, c * CH:(c + 1) * CH], CV[c][i], ACT.Silu).then_inc(cs["u"], 1)
                    act.preload_act_table_set("natural_log_exp_and_others")
                    for c in range(2):
                        act.wait_ge(cs["xp"], n + c)
                        nc.scalar.copy(DT[c], bank(c, 1)[0:DR, :]).then_inc(cs["dt"], 1)
                    for c in range(2):
                        act.wait_ge(cs["dtp"], n + c)
                        for i in range(CI):
                            k = b * 4 + 2 * c + i + 1
                            nc.scalar.activation(SP1[c][i], bank(c, 1 + 2 * i), ACT.Abs,
                                                 bias=col("dt_b", i)).then_inc(cs["sp_abs"], 1)
                            if c:
                                act.wait_ge(cs["dl"], b * 4 + i + 1)
                            nc.scalar.activation(SP2[i], bank(c, 1 + 2 * i), ACT.Relu, bias=col("dt_b", i))
                            act.wait_ge(cs["sp_abs"], k)
                            nc.scalar.activation(SP1[c][i], SP1[c][i], ACT.Exp, scale=-1.0).then_inc(cs["sp_exp"], 1)
                            act.wait_ge(cs["sp_exp"], k)
                            nc.scalar.activation(SP1[c][i], SP1[c][i], ACT.Ln, bias=1.0).then_inc(cs["sp"], 1)
                    act.wait_ge(cs["du"], b * 4 + 4)
                    for k in range(DS):
                        for i in range(CI):
                            if k:
                                act.wait_ge(cs["state"], b * (DS * CI) + 2 * (k - 1) + i + 1)
                            nc.scalar.activation(DA[i], DL[i], ACT.Exp,
                                                 scale=a_neg[:, i * DS + k:i * DS + k + 1]).then_inc(cs["da"], 1)
                        act.wait_ge(cs["c_row"], b * DS + k + 1)
                        if k >= 2:
                            act.wait_ge(cs["hc"], b * (DS * CI) + 2 * (k - 2) + 2)
                        nc.scalar.copy(CR[k % 2], ps[:, 2:4, :].rearrange("p a n -> p (a n)")).then_inc(cs["c_sb"], 1)
                    norm_act(act, ln, lnv(6))
                    norm_act(act, ln, lnv(7))
                    qkv_act(act, qs, n, False, PARTS)
                    for c in range(2):
                        nc.scalar.activation(SQ[c], QK32[c][:, 0, :], ACT.Square).then_inc(cs["q_sq"], 1)
                    for c in range(2):
                        act.wait_ge(cs["sim_parts"], n + c)
                        nc.scalar.activation(RSTD[c][0:H, :], bank(c, 0)[0:H, :], ACT.Ln).then_inc(cs["sim_log"], 1)
                        act.wait_ge(cs["sim_log"], n + c)
                        nc.scalar.activation(RSTD[c][0:H, :], RSTD[c][0:H, :], ACT.Exp, scale=-0.5).then_inc(cs["sim_inv"], 1)

            @block.vector
            def _(dve):
                for c in range(2):
                    nc.vector.memset(lim_run[c][:, 0:1], 3.0e38)
                    nc.vector.memset(lim_run[c][:, 1:2], -3.0e38).then_inc(cs["lim"], 1)
                with dve.Fori(0, B) as b:
                    n = b * 2 + 1

                    def lnv(i):
                        return b * (2 * NLN) + 2 * i + 1

                    for c in range(2):
                        dve.wait_ge(cs["att"], n + c)
                        nc.vector.tensor_scalar(CTX[c], bank(c, 1), col("out_b"), None, ALU.add).then_inc(cs["ctx"], 1)
                        dve.wait_ge(cs["ctx"], n + c)
                        nc.vector.tensor_tensor(XA[c], CTX[c], h0[:, cols_of(b, c)], ALU.add).then_inc(cs["xa"], 1)
                    norm_dve(dve, ln, lnv(0), XA, XS, "g1", "b1")
                    for s in range(STEPS):
                        k = b * (2 * STEPS) + 2 * s + 1
                        for c in range(2):
                            dve.wait_ge(cs["tanh"], k + c)
                            if s:
                                dve.wait_ge(cs["drag"], b * (2 * STEPS - 2) + 2 * s - 1 + c)
                                ins = nc.vector.tensor_tensor(GV[c], CW[c], TT_[c], ALU.add)
                            else:
                                ins = nc.vector.tensor_tensor(GV[c], TT_[c], XS[c], ALU.subtract)
                            ins.then_inc(cs["vel"], 1)
                            dve.wait_ge(cs["vel"], k + c)
                            nc.vector.scalar_tensor_tensor(out=XS[c], in0=GV[c], scalar=0.01, in1=XS[c], op0=ALU.mult,
                                                           op1=ALU.add).then_inc(cs["xs"], 1)
                        if s + 1 < STEPS:
                            for c in range(2):
                                dve.wait_ge(cs["xs"], k + c)
                                nc.vector.scalar_tensor_tensor(out=CW[c], in0=GV[c], scalar=0.9, in1=XS[c], op0=ALU.mult,
                                                               op1=ALU.subtract).then_inc(cs["drag"], 1)
                    for c in range(2):
                        dve.wait_ge(cs["xs"], b * (2 * STEPS) + 2 * STEPS - 1 + c)
                        nc.vector.tensor_tensor(XA[c], XA[c], XS[c], ALU.add).then_inc(cs["xa2"], 1)
                    norm_dve(dve, ln, lnv(1), XA, NRM, "g2", "b2")
                    for c in range(2):
                        dve.wait_ge(cs["ffy"], n + c)
                        nc.vector.scalar_tensor_tensor(out=XA[c], in0=bank(c, 3), scalar=col("ff_b2"), in1=XA[c],
                                                       op0=ALU.add, op1=ALU.add).then_inc(cs["xa3"], 1)
                    norm_dve(dve, ln, lnv(2), XA, NRM)
                    for c in range(2):
                        dve.wait_ge(ln["out"], lnv(2) + c)
                        nc.vector.tensor_tensor(XR[c], NRM[c], x_res[:, cols_of(b, c)], ALU.add).then_inc(cs["xr1"], 1)
                    norm_dve(dve, ln, lnv(3), XR, NRM)
                    for c in range(2):
                        dve.wait_ge(cs["gates"], n + c)
                        nc.vector.tensor_tensor(small[:, c, 0:32], bank(c, 1)[:, 0:32], w["bg"][:, :],
                                                ALU.add).then_inc(cs["g_sb"], 1)
                        dve.wait_ge(cs["g_sb"], n + c)
                        nc.vector.tensor_reduce(gmax[c], gate(c, 0), AX.X, ALU.max).then_inc(cs["g_max"], 1)
                        dve.wait_ge(cs["g_max"], n + c)
                        for t in range(4):
                            ins = nc.vector.tensor_scalar(gate(c, 1)[:, t, :], gate(c, 0)[:, t, :], gmax[c][:, t:t + 1], None,
                                                          ALU.is_lt)
                        ins.then_inc(cs["g_less"], 1)
                        dve.wait_ge(cs["g_less"], n + c)
                        nc.vector.scalar_tensor_tensor(out=gate(c, 2), in0=gate(c, 1), scalar=float(E), in1=iota[:, :, :],
                                                       op0=ALU.mult, op1=ALU.add).then_inc(cs["g_cand"], 1)
                        dve.wait_ge(cs["g_cand"], n + c)
                        nc.vector.tensor_reduce(gmin[c], gate(c, 2), AX.X, ALU.min).then_inc(cs["g_min"], 1)
                        dve.wait_ge(cs["g_min"], n + c)
                        for t in range(4):
                            ins = nc.vector.tensor_scalar(gate(c, 3)[:, t, :], iota[:, t, :], gmin[c][:, t:t + 1], None,
                                                          ALU.is_equal)
                        ins.then_inc(cs["onehot"], 1)
                    for c in range(2):
                        dve.wait_ge(cs["oh_turned"], n + c)
                        nc.vector.tensor_copy(onehot_b[:, c, :], bank(c, 2)[0:E, :]).then_inc(cs["oh_b"], 1)
                    for e in range(E):
                        for c in range(2):
                            k = b * (2 * E) + 2 * e + c + 1
                            dve.wait_ge(cs["moe_y_sb"], k)
                            dve.wait_ge(cs["mask"], k)
                            dst = TT_[c] if e else ACC[c]
                            nc.vector.tensor_tensor(dst, MOE_Y[c], bank(c, 0), ALU.mult).then_inc(cs["masked"], 1)
                            if e:
                                dve.wait_ge(cs["masked"], k)
                                nc.vector.tensor_tensor(ACC[c], ACC[c], TT_[c], ALU.add).then_inc(cs["acc"], 1)
                    norm_dve(dve, ln, lnv(4), ACC, NRM)
                    for c in range(2):
                        dve.wait_ge(ln["out"], lnv(4) + c)
                        nc.vector.tensor_tensor(XR[c], XR[c], NRM[c], ALU.add).then_inc(cs["xr2"], 1)
                    norm_dve(dve, ln, lnv(5), XR, NRM, "norm_w", "norm_b")
                    nc.vector.memset(CONV[:, :, 0:KC - 1], 0.0).then_inc(cs["pad"], 1)
                    dve.wait_ge(cs["pad"], b + 1)
                    for c in range(2):
                        for tap in range(KC):
                            for i in range(CI):
                                k = b * 16 + c * 8 + 2 * tap + i + 1
                                src = CONV[:, i, c * CH + tap:c * CH + tap + CH]
                                if tap == 0:
                                    dve.wait_ge(cs["in_sb"], b * (4 * CI) + 2 * i + c + 1)
                                    ins = nc.vector.tensor_scalar(CV[c][i], src, col("conv_w", i * KC), col("conv_b", i),
                                                                  ALU.mult, ALU.add)
                                else:
                                    dve.wait_ge(cs["tap"], k - 2)
                                    ins = nc.vector.scalar_tensor_tensor(out=CV[c][i], in0=src, scalar=col("conv_w", i * KC + tap),
                                                                         in1=CV[c][i], op0=ALU.mult, op1=ALU.add)
                                ins.then_inc(cs["tap"], 1)
                    for c in range(2):
                        dve.wait_ge(cs["xp"], n + c)
                        rows = slice(0, 6 * DS)
                        nc.vector.tensor_copy(B_HI[c], bank(c, 2)[rows, :]).then_inc(cs["bc_hi"], 1)
                        dve.wait_ge(cs["bc_hi"], n + c)
                        nc.vector.scalar_tensor_tensor(out=B_REST[c], in0=B_HI[c], scalar=col("part12")[rows, :],
                                                       in1=bank(c, 2)[rows, :], op0=ALU.mult, op1=ALU.add).then_inc(cs["bc_rest"], 1)
                        dve.wait_ge(cs["bc_rest"], n + c)
                        nc.vector.tensor_copy(B_MID[c], B_REST[c]).then_inc(cs["bc_mid"], 1)
                        dve.wait_ge(cs["bc_mid"], n + c)
                        nc.vector.scalar_tensor_tensor(out=bc_parts[:, c * CH:(c + 1) * CH], in0=B_MID[c],
                                                       scalar=col("part2")[rows, :], in1=B_REST[c], op0=ALU.mult,
                                                       op1=ALU.add).then_inc(cs["bc"], 1)
                    for c in range(2):
                        at = slice(c * CH, (c + 1) * CH)
                        for i in range(CI):
                            k = b * 4 + 2 * c + i + 1
                            dve.wait_ge(cs["sp"], k)
                            nc.vector.tensor_tensor(DL[i][:, at], SP1[c][i], SP2[i], ALU.add).then_inc(cs["dl"], 1)
                            dve.wait_ge(cs["dl"], k)
                            nc.vector.tensor_tensor(DU[i][:, at], DL[i][:, at], U[i][:, at], ALU.mult).then_inc(cs["du"], 1)
                    b_rows = ps[:, 0:2, :].rearrange("p a n -> p (a n)")
                    for k in range(DS):
                        at = b * (DS * CI) + 2 * k + 1
                        for i in range(CI):
                            if k == 0:
                                dve.wait_ge(cs["du"], b * 4 + 4)
                            dve.wait_ge(cs["b_row"], b * DS + k + 1)
                            if k:
                                dve.wait_ge(cs["state"], at - 2 + i)
                            nc.vector.tensor_tensor(DBU[i], DU[i], b_rows, ALU.mult).then_inc(cs["dbu"], 1)
                        for i in range(CI):
                            dve.wait_ge(cs["da"], at + i)
                            dve.wait_ge(cs["dbu"], at + i)
                            if k >= 2:
                                dve.wait_ge(cs["hc"], at - 4 + i)
                            nc.vector.tensor_tensor_scan(HS[k % 2][i], DA[i], DBU[i], 0.0, ALU.mult, ALU.add).then_inc(cs["state"], 1)
                    dve.wait_ge(cs["y_sum"], b * (DS * CI) + DS * CI)
                    for c in range(2):
                        at = slice(c * CH, (c + 1) * CH)
                        for i in range(CI):
                            nc.vector.scalar_tensor_tensor(out=YT[i][:, at], in0=U[i][:, at], scalar=col("D_param", i),
                                                           in1=ps[:, 4 + 2 * i + c, :], op0=ALU.mult,
                                                           op1=ALU.add).then_inc(cs["yy"], 1)
                        for i in range(CI):
                            dve.wait_ge(cs["yy"], b * 4 + 2 * c + i + 1)
                            nc.vector.tensor_tensor(YT[i][:, at], YT[i][:, at], SZ[i][:, at], ALU.mult).then_inc(cs["yg"], 1)
                    for c in range(2):
                        dve.wait_ge(cs["op"], n + c)
                        nc.vector.tensor_copy(TT_[c], bank(c, 1)).then_inc(cs["ao"], 1)
                    norm_dve(dve, ln, lnv(6), TT_, NRM)
                    for c in range(2):
                        dve.wait_ge(ln["out"], lnv(6) + c)
                        nc.vector.tensor_tensor(XR[c], XR[c], NRM[c], ALU.add).then_inc(cs["xr3"], 1)
                    norm_dve(dve, ln, lnv(7), XR, XN)
                    qkv_dve(dve, qs, n, b, False, PARTS)
                    for c in range(2):
                        dve.wait_ge(cs["sim_inv"], n + c)
                        nc.vector.tensor_tensor(SIM16[c], bank(c, 1)[0:H, :], RSTD[c][0:H, :], ALU.mult).then_inc(cs["sim_prod"], 1)
                    for c in range(2):
                        dve.wait_ge(cs["sim"], n + c)
                        nc.vector.tensor_scalar(h0[:, cols_of(b, c)], bank(c, 2), 1.0, None, ALU.mult).then_inc(cs["sim_kept"], 1)
                        first = REG if c == 0 else 0
                        nc.vector.tensor_reduce(lim_part[c][:, 0:1], bank(c, 2)[:, first:CH], AX.X, ALU.min)
                        nc.vector.tensor_reduce(lim_part[c][:, 1:2], bank(c, 2)[:, first:CH], AX.X, ALU.max).then_inc(cs["lim_part"], 1)
                        dve.wait_ge(cs["lim_part"], n + c)
                        dve.wait_ge(cs["lim"], n + c)
                        nc.vector.tensor_tensor(lim_run[c][:, 0:1], lim_run[c][:, 0:1], lim_part[c][:, 0:1], ALU.min)
                        nc.vector.tensor_tensor(lim_run[c][:, 1:2], lim_run[c][:, 1:2], lim_part[c][:, 1:2], ALU.max).then_inc(cs["lim"], 1)
                    dve.wait_ge(cs["kept"], n + 1)

            @block.gpsimd
            def _(pool):
                with pool.Fori(0, B) as b:
                    for k in range(DS):
                        at = b * (DS * CI) + 2 * k + 1
                        pool.wait_ge(cs["c_sb"], b * DS + k + 1)
                        for i in range(CI):
                            pool.wait_ge(cs["state"], at + i)
                            if k:
                                pool.wait_ge(cs["y_sum"], at - 2 + i)
                            nc.gpsimd.tensor_tensor(HC[i], HS[k % 2][i], CR[k % 2], ALU.mult).then_inc(cs["hc"], 1)
                    for c in range(2):
                        pool.wait_ge(cs["xr3"], b * 2 + c + 1)
                        nc.gpsimd.tensor_copy(x_res[:, cols_of(b, c)], XR[c]).then_inc(cs["kept"], 1)

        end_phase()

        d_chain, d_sign, d_rows, d_regs, d_stored = (sem("d_" + k) for k in ("chain", "sign", "rows", "regs", "stored"))
        lim = small[:, 0, 0:4]
        mask_rows = work[:, 0:2, :].rearrange("p a n -> p (a n)").bitcast(BF16)
        with nc.Block() as block:
            @block.vector
            def _(dve):
                count = [0]

                def link(ins):
                    count[0] += 1
                    ins.then_inc(d_chain, 1)
                    dve.wait_ge(d_chain, count[0])

                link(nc.vector.tensor_tensor(lim[:, 0:1], lim_run[0][:, 0:1], lim_run[1][:, 0:1], ALU.min))
                link(nc.vector.tensor_tensor(lim[:, 1:2], lim_run[0][:, 1:2], lim_run[1][:, 1:2], ALU.max))
                link(nc.vector.tensor_tensor(lim[:, 2:3], lim[:, 1:2], lim[:, 0:1], ALU.subtract))
                link(nc.vector.reciprocal(lim[:, 3:4], lim[:, 2:3]))
                for b in range(B):
                    sims = h0[:, b * S:(b + 1) * S]
                    link(nc.vector.tensor_scalar(sims, sims, lim[:, 0:1], lim[:, 3:4], ALU.subtract, ALU.mult))
                    nc.vector.tensor_scalar(sims, sims, 0.9, None, ALU.is_gt).then_inc(d_sign, 1)

            @block.scalar
            def _(act):
                for b in range(B):
                    act.wait_ge(d_sign, b + 1)
                    nc.scalar.activation(mask_rows[:, b * S:(b + 1) * S], h0[:, b * S:(b + 1) * S], ACT.Identity,
                                         scale=col("mask_mul"), bias=col("mask_add")).then_inc(d_rows, 1)
                    act.wait_ge(d_rows, b + 1)
                    nc.scalar.activation(mask_rows[:, b * S:b * S + REG], h0[:, b * S:b * S + REG], ACT.Identity,
                                         scale=0.0, bias=col("mask_reg")).then_inc(d_regs, 1)

            @block.sync
            def _(sp):
                for b in range(0, B, 2):
                    sp.wait_ge(d_regs, b + 2)
                    for k, (dram, row) in enumerate(((scratch_q, R_MASK), (scratch_q, R_MASK + 1), (scratch_k, R_MASK),
                                                     (scratch_k, R_MASK + 1))):
                        dst = dram[b * H:(b + 2) * H, row, :].rearrange("(b h) n -> h b n", b=2)
                        src = mask_rows[32 * k:32 * k + H, b * S:(b + 2) * S].rearrange("h (b n) -> h b n", b=2)
                        sp.dma_start(dst, src).then_inc(d_stored, 16)
                sp.wait_ge(d_stored, 16 * 4 * (B // 2))

        end_phase()
        run_attention("e", False)
        end_phase()

        fs = {k: sem("f_" + k) for k in ("reg_sum", "reg", "proj", "ao", "xr", "turned", "y_sb", "ox")}
        f_norm = norm_sems("f_norm")
        NC = 4
        TRIPS = B * S // CH // NC
        f_ol = [sem(f"f_ol{t}") for t in range(TRIPS)]
        f_out = [sem(f"f_out{c}") for c in range(NC)]
        F_DEV, F_SQ, F_RSTD, F_NRM, F_XA, F_XR, F_YO = (chunks(2 * i) + chunks(2 * i + 1) for i in range(7))
        F_OL = [chunks(14 + 2 * t) + chunks(15 + 2 * t) for t in range(TRIPS)]
        quad = (F_DEV, F_SQ, F_RSTD, [ps[:, 2 * c, :] for c in range(NC)])
        acc = [ps[:, 2 * c + 1, :] for c in range(NC)]
        OX = work[:, 18, 0:B * XQ].rearrange("p (b n) -> p b n", b=B)
        out_rows = out.rearrange("b (t p) f -> (b t) p f", p=P)
        with nc.Block() as block:
            @block.sync
            def _(sp):
                for b in range(B):
                    sp.dma_start(OX[:, b, :], heads_x[b, :, :, :]).then_inc(fs["ox"], 16)
                for t in range(TRIPS):
                    for c in range(NC):
                        src = heads_o[2 * t + c // 2, :, :, (c % 2) * CH:(c % 2 + 1) * CH]
                        sp.dma_start(F_OL[t][c], src).then_inc(f_ol[t], 16)
                for t in range(TRIPS):
                    for c in range(NC):
                        sp.wait_ge(fs["y_sb"], t * NC + c + 1)
                        sp.dma_start(out_rows[4 * (t * NC + c):4 * (t * NC + c + 1), :, :].rearrange("t p f -> p t f"),
                                     F_YO[c].rearrange("p (t f) -> p t f", t=4)).then_inc(f_out[c], 16)
                for c in range(NC):
                    sp.wait_ge(f_out[c], 16 * TRIPS)

            @block.tensor
            def _(pe):
                for t in range(TRIPS):
                    n = t * NC + 1
                    pe.wait_ge(f_ol[t], 16 * NC)
                    pe.wait_ge(fs["reg"], 2 * t + 2)
                    for c in range(NC):
                        if t:
                            pe.wait_ge(fs["y_sb"], n - NC + c)
                        nc.tensor.matmul(acc[c], w["proj_w"][:, :], F_OL[t][c], start=True, stop=True).then_inc(fs["proj"], 1)
                    norm_pe(pe, f_norm, n, F_XA, lambda e, c: e.wait_ge(fs["ao"], n + c), tiles=quad)
                    for c in range(NC):
                        pe.wait_ge(fs["xr"], n + c)
                        for i in range(CH // P):
                            mm = nc.tensor.transpose(acc[c][:, i * P:(i + 1) * P], F_XR[c][:, i * P:(i + 1) * P],
                                                     w["ident"][:, :])
                        mm.then_inc(fs["turned"], 1)

            @block.scalar
            def _(act):
                act.preload_act_table_set("natural_log_exp_and_others")
                for t in range(TRIPS):
                    n = t * NC + 1
                    norm_act(act, f_norm, n, tiles=quad)
                    for c in range(NC):
                        act.wait_ge(fs["turned"], n + c)
                        if t:
                            act.wait_ge(f_out[c], 16 * t)
                        nc.scalar.copy(F_YO[c], acc[c]).then_inc(fs["y_sb"], 1)

            @block.vector
            def _(dve):
                dve.wait_ge(fs["ox"], 16 * B)
                for t in range(TRIPS):
                    n = t * NC + 1
                    dve.wait_ge(f_ol[t], 16 * NC)
                    for i in range(2):
                        ox, ol = OX[:, 2 * t + i, 0:REG], F_OL[t][2 * i][:, 0:REG]
                        nc.vector.tensor_tensor(ox, ox, ol, ALU.add).then_inc(fs["reg_sum"], 1)
                        dve.wait_ge(fs["reg_sum"], 2 * t + i + 1)
                        nc.vector.tensor_scalar(ol, ox, 0.5, None, ALU.mult).then_inc(fs["reg"], 1)
                    for c in range(NC):
                        dve.wait_ge(fs["proj"], n + c)
                        nc.vector.tensor_scalar(F_XA[c], acc[c], col("proj_b"), None, ALU.add).then_inc(fs["ao"], 1)
                    norm_dve(dve, f_norm, n, F_XA, F_NRM, tiles=quad)
                    for c in range(NC):
                        at = (t * NC + c) * CH
                        dve.wait_ge(f_norm["out"], n + c)
                        nc.vector.tensor_tensor(F_XR[c], F_NRM[c], x_res[:, at:at + CH], ALU.add).then_inc(fs["xr"], 1)

def kernel(**inputs):
    import numpy as np
    import concourse.bacc as _bacc
    from concourse.bass_utils import run_bass_kernel_spmd as _run

    x = {k: np.asarray(v) for k, v in inputs.items()}
    f32, bf16 = np.float32, mybir.dt.np(BF16)

    def vec(v):
        return v.reshape(-1, P).T

    rows = np.arange(6 * DS)
    part = lambda n: np.pad((rows >= n * 2 * DS).astype(f32), (0, P - 6 * DS)).reshape(1, P)
    kinds = lambda *values: np.repeat(np.array(values, f32), 32).reshape(P, 1)
    columns = {
        "q_b": vec(x["L0_attn_qkv_b"][0:D]), "k_b": vec(x["L0_attn_qkv_b"][D:2 * D]), "out_b": vec(x["L0_attn_out_b"]),
        "g_attn": vec(x["L0_attn_g_attn"]), "b_attn": vec(x["L0_attn_b_attn"]), "g1": vec(x["L0_attn_g1"]),
        "b1": vec(x["L0_attn_b1"]), "g2": vec(x["L0_attn_g2"]), "b2": vec(x["L0_attn_b2"]),
        "b_inl": vec(x["L0_attn_b_inl"]), "ff_b1": vec(x["L0_attn_ff_b1"]), "ff_b2": vec(x["L0_attn_ff_b2"]),
        "moe_b1": vec(x["L0_ffn_b1"]), "moe_b2": vec(x["L0_ffn_b2"]), "norm_w": vec(x["L1_attn_norm_w"]),
        "norm_b": vec(x["L1_attn_norm_b"]),
        "conv_w": x["L1_attn_conv_w"].reshape(CI, P, KC).transpose(1, 0, 2).reshape(P, -1),
        "conv_b": vec(x["L1_attn_conv_b"]), "dt_b": vec(x["L1_attn_dt_proj_b"]),
        "A_log": x["L1_attn_A_log"].reshape(CI, P, DS).transpose(1, 0, 2).reshape(P, -1),
        "D_param": vec(x["L1_attn_D_param"]), "q_gate": vec(x["L1_ffn_g_info"][0, 0]), "proj_b": vec(x["L1_ffn_b_proj"]),
        "part12": -part(1).T, "part2": -part(2).T,
        "mask_mul": kinds(1.0, -1.0, -NEG, NEG), "mask_add": kinds(0.0, 1.0, NEG, 0.0), "mask_reg": kinds(1.0, 0.0, 0.0, 0.0),
    }
    for name, (_, n) in COLS.items():
        assert columns[name].shape == (P, n), name
    eye = np.eye(P, dtype=f32)
    q = np.arange(P)
    head = (q[:, None] // HD == np.arange(H)[None, :]).astype(f32)
    den = np.zeros((P, P), f32)
    den[q // 32 * 32 + HD, q] = 1.0
    bc = x["L1_attn_x_proj_w"][:, DR:].reshape(CI, P, 2 * DS).transpose(1, 0, 2)
    arrays = {
        "x": x["L0_attn_x"].reshape(B * QT, P, D),
        "cols": np.concatenate([columns[name] for name in COLS], axis=1),
        "qkv_w": x["L0_attn_qkv_w"], "v_bias": np.tile(x["L0_attn_qkv_b"][2 * D:], (P, CH // D)),
        "out_w": x["L0_attn_out_w"], "w_ctx": x["L0_attn_w_ctx"], "w_x": x["L0_attn_w_x"],
        "ff_w1": x["L0_attn_ff_w1"], "ff_w2": x["L0_attn_ff_w2"].reshape(FF // P, P, D).transpose(1, 0, 2),
        "Wg": x["L0_ffn_Wg"], "bg": np.tile(x["L0_ffn_bg"], (P, CH // P)), "W1": x["L0_ffn_W1"].transpose(1, 0, 2),
        "W2": x["L0_ffn_W2"].reshape(E, FF // P, P, D).transpose(2, 0, 1, 3), "in_proj_w": x["L1_attn_in_proj_w"],
        "x_proj_dt": x["L1_attn_x_proj_w"][:, 0:DR].reshape(CI, P, DR).transpose(1, 0, 2),
        "x_proj_bc": np.concatenate([bc, bc, bc], axis=2), "dt_proj_w": x["L1_attn_dt_proj_w"],
        "out_proj_w": x["L1_attn_out_proj_w"].reshape(CI, P, D).transpose(1, 0, 2),
        "qkv2_w": x["L1_ffn_W_qkv"], "proj_w": x["L1_ffn_W_proj"],
        "ident": eye, "mean_w": np.full((P, P), 1.0 / D, f32), "den_sel": den, "head_sel": head, "head_back": head.T,
        "sim_sum": np.full((H, P), 1.0 / H, f32), "iota": np.broadcast_to(np.arange(E, dtype=f32), (P, CH // P, E)),
        "ident_b": eye.astype(bf16), "mask_qk": np.where(q[None, :] > q[:, None], NEG, 0.0).astype(bf16),
        "mask_kq": np.where(q[:, None] > q[None, :], NEG, 0.0).astype(bf16),
        "exp_sel": np.repeat(np.eye(E, dtype=f32)[:, :, None], P, axis=2).astype(bf16),
        "bc_sel": np.repeat((rows[:, None] % (2 * DS) == np.arange(2 * DS)[None, :])[:, :, None], P, axis=2).astype(bf16),
        "x_rows": np.repeat(np.array([[0.0], [1.0]], f32), XQ, axis=1).astype(bf16),
    }
    arrays = {k: np.ascontiguousarray(v) for k, v in arrays.items()}
    nc = _bacc.Bacc("TRN2", target_bir_lowering=False, num_devices=1)
    handles = {k: nc.dram_tensor(f"in_{k}", v.shape, mybir.dt.from_np(v.dtype), kind="ExternalInput").ap()
               for k, v in arrays.items()}
    out = nc.dram_tensor("out_0", (B, S, D), F32, kind="ExternalOutput").ap()
    build(nc, handles, out)
    r = _run(nc, [{f"in_{k}": v for k, v in arrays.items()}], core_ids=[0])
    return r.results[0]["out_0"]
```
